# Optimizing a Trainium2 kernel written in Bass

```python
import numpy as np
import jax
import jax.numpy as jnp

def _softmax(x, axis=-1):
    return jax.nn.softmax(x, axis=axis)

def _gelu(x):
    return jax.nn.gelu(x, approximate=True)

def _silu(x):
    return jax.nn.silu(x)

def _sigmoid(x):
    return jax.nn.sigmoid(x)

def _layernorm(x, axis=-1, eps=1e-05):
    m = jnp.mean(x, axis=axis, keepdims=True)
    v = jnp.var(x, axis=axis, keepdims=True)
    return (x - m) / jnp.sqrt(v + eps)

def _scatter_add(tgt, idx, src, axis=0):
    return tgt.at[idx].add(src)

def _segment_sum(src, seg, n):
    return jax.ops.segment_sum(src, seg, n)
kernel_name = 'mk_decoder_postln_d2_seqx_r8_28a507'

def setup_inputs(seed: int=0):
    np.random.seed(seed)
    _w = jnp.asarray

    def _rec_inputs():
        import jax
        import jax.numpy as jnp
        _rk = jax.random.key(seed)
        x = -0.0002928 + 1 * jax.random.normal(jax.random.fold_in(_rk, 1), (8, 256, 128), jnp.float32)
        _lenS = 256 - jax.random.randint(jax.random.fold_in(_rk, 7), (8,), 0, max(1, 256 // 4) + 1, jnp.int32)
        _lenS2 = 256 - jax.random.randint(jax.random.fold_in(_rk, 8), (8,), 0, max(1, 256 // 4) + 1, jnp.int32)
        _ctx_1024P = jax.random.normal(jax.random.fold_in(_rk, 11), (8, 16, 128), jnp.float32)
        _ctx_1024c = jax.random.dirichlet(jax.random.fold_in(_rk, 511), 0.3 * jnp.ones((16,), jnp.float32), (8, 256))
        _ctx_1024t = jnp.einsum('bsk,bkd->bsd', _ctx_1024c, _ctx_1024P)
        _ctx_1024t = _ctx_1024t * jax.lax.rsqrt(jnp.mean(jnp.square(_ctx_1024t)) + 1e-12) * 0.953939
        ctx_1024 = -1.39393e-06 + 0.999914 * (_ctx_1024t + 0.3 * jax.random.normal(jax.random.fold_in(_rk, 611), (8, 256, 128), jnp.float32))
        _validS = jnp.arange(256)[None, :] < _lenS[:, None]
        _validS2 = jnp.arange(256)[None, :] < _lenS2[:, None]
        _causal = jnp.tril(jnp.ones((256, 256), dtype=bool))
        mask_1x1xSxS2_ik0 = jnp.where(jnp.broadcast_to(_validS2[0:1, None, None, :], (1, 1, 256, 256)), 0, 1).astype(jnp.int32)
        return (x, ctx_1024, mask_1x1xSxS2_ik0)
    x, ctx_1024, mask_1x1xSxS2_ik0 = _rec_inputs()

    def _L0_attn_setup():
        import jax, jax.numpy as jnp
        import numpy as np
        B, S, D = (2, 128, 128)
        NH = 8
        QK = D // 2
        V = D
        DQK = QK // NH
        DV = V // NH
        CAP = 15.0
        EPS = 1e-06

        def soft_cap(t, cap=CAP):
            return cap * jnp.tanh(t / cap)

        def _mlstm_forward(x, Wq, Wk, Wv, Wog, Wi, bi, Wf, bf, ln_w, ln_b, Wout):
            Bx, Sx, _ = x.shape
            q = (x @ Wq.T).reshape(Bx, Sx, NH, DQK)
            k = (x @ Wk.T).reshape(Bx, Sx, NH, DQK)
            v = (x @ Wv.T).reshape(Bx, Sx, NH, DV)
            o_preact = x @ Wog.T
            i_pre = soft_cap(x @ Wi.T + bi)
            f_pre = soft_cap(x @ Wf.T + bf)
            qT = jnp.moveaxis(q, 1, 0)
            kT = jnp.moveaxis(k, 1, 0)
            vT = jnp.moveaxis(v, 1, 0)
            iT = jnp.moveaxis(i_pre, 1, 0)
            fT = jnp.moveaxis(f_pre, 1, 0)
            qk_scale = DQK ** (-0.5)

            def step(carry, inp):
                C, n, m = carry
                q_t, k_t, v_t, i_t, f_t = inp
                m_new = jnp.maximum(f_t + m, i_t)
                f_act = jnp.exp(f_t + m - m_new)
                i_act = jnp.exp(i_t - m_new)
                C = f_act[..., None, None] * C + i_act[..., None, None] * (k_t[..., :, None] * v_t[..., None, :])
                n = f_act[..., None] * n + i_act[..., None] * k_t
                qs = q_t * qk_scale
                num = jnp.einsum('bhk,bhkv->bhv', qs, C)
                qn = jnp.einsum('bhk,bhk->bh', qs, n)
                denom = jnp.maximum(jnp.abs(qn), jnp.exp(-m_new)) + 1e-06
                h_t = num / denom[..., None]
                return ((C, n, m_new), h_t)
            C0 = jnp.zeros((Bx, NH, DQK, DV), x.dtype)
            n0 = jnp.zeros((Bx, NH, DQK), x.dtype)
            m0 = jnp.zeros((Bx, NH), x.dtype)
            _, hs = jax.lax.scan(step, (C0, n0, m0), (qT, kT, vT, iT, fT))
            h = jnp.moveaxis(hs, 0, 1).reshape(Bx, Sx, NH * DV)
            mu = jnp.mean(h, axis=-1, keepdims=True)
            var = jnp.mean((h - mu) ** 2, axis=-1, keepdims=True)
            h_norm = (h - mu) * jax.lax.rsqrt(var + EPS) * ln_w + ln_b
            h_out = jax.nn.sigmoid(o_preact) * h_norm
            y = h_out @ Wout.T
            return y
        key = jax.random.key(seed)
        ks = jax.random.split(key, 12)
        sc = 0.02
        return {'x': jax.random.normal(ks[0], (B, S, D), jnp.float32), 'Wq': jax.random.normal(ks[1], (QK, D), jnp.float32) * sc, 'Wk': jax.random.normal(ks[2], (QK, D), jnp.float32) * sc, 'Wv': jax.random.normal(ks[3], (V, D), jnp.float32) * sc, 'Wog': jax.random.normal(ks[4], (V, D), jnp.float32) * sc, 'Wi': jax.random.normal(ks[5], (NH, D), jnp.float32) * sc, 'bi': jax.random.normal(ks[6], (NH,), jnp.float32) * sc, 'Wf': jax.random.normal(ks[7], (NH, D), jnp.float32) * sc, 'bf': jax.random.normal(ks[8], (NH,), jnp.float32) * sc + 3.0, 'ln_w': jnp.ones((NH * DV,), jnp.float32), 'ln_b': jnp.zeros((NH * DV,), jnp.float32), 'Wout': jax.random.normal(ks[9], (D, V), jnp.float32) * sc}
    _L0_attn_all = _L0_attn_setup()
    _L0_attn_in = {k: v for k, v in _L0_attn_all.items() if k in ('Wq', 'Wk', 'Wv', 'Wog', 'Wi', 'bi', 'Wf', 'bf', 'ln_w', 'ln_b', 'Wout')}
    del _L0_attn_all

    def _L0_xattn_setup():
        import jax, jax.numpy as jnp
        import numpy as np
        B, L, D, H = (2, 256, 128, 16)
        HD = D // H

        def _xavier(key, out_f, in_f):
            std = (2.0 / (in_f + out_f)) ** 0.5
            return jax.random.normal(key, (out_f, in_f), dtype=jnp.float32) * std
        key = jax.random.key(seed)
        k = jax.random.split(key, 8)
        Q = jax.random.normal(k[0], (B, L, D), dtype=jnp.float32)
        K = jax.random.normal(k[1], (B, L, D), dtype=jnp.float32)
        V = jax.random.normal(k[2], (B, L, D), dtype=jnp.float32)
        mask = jnp.tril(jnp.ones((L, L), dtype=jnp.int32))[None, None]
        wq = _xavier(k[3], D, D)
        wk = _xavier(k[4], D, D)
        wv = _xavier(k[5], D, D)
        wo = _xavier(k[6], D, D)
        bo = jnp.zeros((D,), dtype=jnp.float32)
        return {'Q': Q, 'K': K, 'V': V, 'mask': mask, 'wq': wq, 'wk': wk, 'wv': wv, 'wo': wo, 'bo': bo}
    _L0_xattn_all = _L0_xattn_setup()
    _L0_xattn_in = {k: v for k, v in _L0_xattn_all.items() if k in ('wq', 'wk', 'wv', 'wo', 'bo')}
    del _L0_xattn_all

    def _L0_ffn_setup():
        import jax, jax.numpy as jnp
        import numpy as np
        B, M, D = (4, 256, 128)
        N, P = (64, 32)
        key = jax.random.key(seed)
        k1, k2, k3, k4 = jax.random.split(key, 4)
        x = jax.random.normal(k1, (B, M, D), dtype=jnp.float32)
        phi = jax.random.normal(k2, (D, N, P), dtype=jnp.float32) * (1.0 / np.sqrt(D))
        W = jax.random.normal(k3, (N, D, D), dtype=jnp.float32) * (1.0 / np.sqrt(D))
        b = jax.random.normal(k4, (N, D), dtype=jnp.float32) * 0.01
        return {'x': x, 'phi': phi, 'W': W, 'b': b}
    _L0_ffn_all = _L0_ffn_setup()
    _L0_ffn_in = {k: v for k, v in _L0_ffn_all.items() if k in ('phi', 'W', 'b')}
    del _L0_ffn_all

    def _L1_attn_setup():
        import jax, jax.numpy as jnp
        import numpy as np
        N_INPUT = 128
        N_HEAD = 16
        ATT_DIM = N_INPUT // N_HEAD * N_HEAD
        V_DIM = N_INPUT // 2 * N_HEAD
        COMB_DIM = 2 * ATT_DIM + V_DIM
        SCALE = (N_INPUT // N_HEAD) ** 0.5
        key = jax.random.key(seed)
        k1, k2, k3 = jax.random.split(key, 3)
        B, T = (8, 128)
        representations = jax.random.normal(k1, (B, T, N_INPUT), dtype=jnp.float32)
        Wc = jax.random.normal(k2, (COMB_DIM, N_INPUT), dtype=jnp.float32) * (0.1 * np.sqrt(2.0 / (COMB_DIM + N_INPUT)))
        bc = jnp.zeros((COMB_DIM,), dtype=jnp.float32)
        Wo = jax.random.normal(k3, (N_INPUT, V_DIM), dtype=jnp.float32) * (0.1 * np.sqrt(2.0 / (N_INPUT + V_DIM)))
        bo = jnp.zeros((N_INPUT,), dtype=jnp.float32)
        return {'representations': representations, 'Wc': Wc, 'bc': bc, 'Wo': Wo, 'bo': bo}
    _L1_attn_all = _L1_attn_setup()
    _L1_attn_in = {k: v for k, v in _L1_attn_all.items() if k in ('Wc', 'bc', 'Wo', 'bo')}
    del _L1_attn_all

    def _L1_xattn_setup():
        import jax, jax.numpy as jnp
        import numpy as np
        D_MODEL = 128
        NUM_HEADS = 16
        HEAD_DIM = D_MODEL // NUM_HEADS
        key = jax.random.key(seed)
        ks = jax.random.split(key, 10)
        B, SQ, SKV = (2, 256, 256)
        s = 1.0 / np.sqrt(D_MODEL)
        inp = {'query': jax.random.normal(ks[0], (B, SQ, D_MODEL), jnp.float32), 'key_value': jax.random.normal(ks[1], (B, SKV, D_MODEL), jnp.float32), 'Wq': jax.random.normal(ks[2], (D_MODEL, D_MODEL), jnp.float32) * s, 'bq': jnp.zeros((D_MODEL,), jnp.float32), 'Wk': jax.random.normal(ks[3], (D_MODEL, D_MODEL), jnp.float32) * s, 'bk': jnp.zeros((D_MODEL,), jnp.float32), 'Wv': jax.random.normal(ks[4], (D_MODEL, D_MODEL), jnp.float32) * s, 'bv': jnp.zeros((D_MODEL,), jnp.float32), 'Wo': jax.random.normal(ks[5], (D_MODEL, D_MODEL), jnp.float32) * s, 'bo': jnp.zeros((D_MODEL,), jnp.float32)}
        return inp
    _L1_xattn_all = _L1_xattn_setup()
    _L1_xattn_in = {k: v for k, v in _L1_xattn_all.items() if k in ('Wq', 'bq', 'Wk', 'bk', 'Wv', 'bv', 'Wo', 'bo')}
    del _L1_xattn_all

    def _L1_ffn_setup():
        import jax, jax.numpy as jnp
        import numpy as np

        def _bitlinear(x, w_latent):
            scale = jax.lax.stop_gradient(jnp.clip(jnp.mean(jnp.abs(w_latent), axis=1, keepdims=True), 1e-05, None))
            tern = jnp.clip(jnp.round(w_latent / scale), -1.0, 1.0)
            w = w_latent + jax.lax.stop_gradient(tern - w_latent)
            return x @ (w * scale).T
        key = jax.random.key(seed)
        ks = jax.random.split(key, 6)
        dim, hidden, rank = (128, 512, 16)
        B, S = (4, 512)
        x = jax.random.normal(ks[0], (B, S, dim), dtype=jnp.float32)
        w_fc = 0.02 * jax.random.normal(ks[1], (hidden, dim), dtype=jnp.float32)
        w_proj = 0.02 * jax.random.normal(ks[2], (dim, hidden), dtype=jnp.float32)
        u = 0.02 * jax.random.normal(ks[3], (hidden, rank), dtype=jnp.float32)
        v = 0.02 * jax.random.normal(ks[4], (rank, dim), dtype=jnp.float32)
        fast_b = jax.random.normal(ks[5], (rank, rank), dtype=jnp.float32)
        gate = jnp.float32(0.05)
        return {'x': x, 'fast_b': fast_b, 'w_fc': w_fc, 'w_proj': w_proj, 'u': u, 'v': v, 'gate': gate}
    _L1_ffn_all = _L1_ffn_setup()
    _L1_ffn_in = {k: v for k, v in _L1_ffn_all.items() if k in ('fast_b', 'w_fc', 'w_proj', 'u', 'v', 'gate')}
    del _L1_ffn_all
    return {'x': x, 'ctx_1024': ctx_1024, 'mask_1x1xSxS2_ik0': mask_1x1xSxS2_ik0, 'L0_attn_Wq': _L0_attn_in['Wq'], 'L0_attn_Wk': _L0_attn_in['Wk'], 'L0_attn_Wv': _L0_attn_in['Wv'], 'L0_attn_Wog': _L0_attn_in['Wog'], 'L0_attn_Wi': _L0_attn_in['Wi'], 'L0_attn_bi': _L0_attn_in['bi'], 'L0_attn_Wf': _L0_attn_in['Wf'], 'L0_attn_bf': _L0_attn_in['bf'], 'L0_attn_ln_w': _L0_attn_in['ln_w'], 'L0_attn_ln_b': _L0_attn_in['ln_b'], 'L0_attn_Wout': _L0_attn_in['Wout'], 'L0_xattn_wq': _L0_xattn_in['wq'], 'L0_xattn_wk': _L0_xattn_in['wk'], 'L0_xattn_wv': _L0_xattn_in['wv'], 'L0_xattn_wo': _L0_xattn_in['wo'], 'L0_xattn_bo': _L0_xattn_in['bo'], 'L0_ffn_phi': _L0_ffn_in['phi'], 'L0_ffn_W': _L0_ffn_in['W'], 'L0_ffn_b': _L0_ffn_in['b'], 'L1_attn_Wc': _L1_attn_in['Wc'], 'L1_attn_bc': _L1_attn_in['bc'], 'L1_attn_Wo': _L1_attn_in['Wo'], 'L1_attn_bo': _L1_attn_in['bo'], 'L1_xattn_Wq': _L1_xattn_in['Wq'], 'L1_xattn_bq': _L1_xattn_in['bq'], 'L1_xattn_Wk': _L1_xattn_in['Wk'], 'L1_xattn_bk': _L1_xattn_in['bk'], 'L1_xattn_Wv': _L1_xattn_in['Wv'], 'L1_xattn_bv': _L1_xattn_in['bv'], 'L1_xattn_Wo': _L1_xattn_in['Wo'], 'L1_xattn_bo': _L1_xattn_in['bo'], 'L1_ffn_fast_b': _L1_ffn_in['fast_b'], 'L1_ffn_w_fc': _L1_ffn_in['w_fc'], 'L1_ffn_w_proj': _L1_ffn_in['w_proj'], 'L1_ffn_u': _L1_ffn_in['u'], 'L1_ffn_v': _L1_ffn_in['v'], 'L1_ffn_gate': _L1_ffn_in['gate']}

def reference(x, ctx_1024, mask_1x1xSxS2_ik0, L0_attn_Wq, L0_attn_Wk, L0_attn_Wv, L0_attn_Wog, L0_attn_Wi, L0_attn_bi, L0_attn_Wf, L0_attn_bf, L0_attn_ln_w, L0_attn_ln_b, L0_attn_Wout, L0_xattn_wq, L0_xattn_wk, L0_xattn_wv, L0_xattn_wo, L0_xattn_bo, L0_ffn_phi, L0_ffn_W, L0_ffn_b, L1_attn_Wc, L1_attn_bc, L1_attn_Wo, L1_attn_bo, L1_xattn_Wq, L1_xattn_bq, L1_xattn_Wk, L1_xattn_bk, L1_xattn_Wv, L1_xattn_bv, L1_xattn_Wo, L1_xattn_bo, L1_ffn_fast_b, L1_ffn_w_fc, L1_ffn_w_proj, L1_ffn_u, L1_ffn_v, L1_ffn_gate):
    import jax
    import jax.numpy as jnp

    def _L0_attn_ref(x, Wq, Wk, Wv, Wog, Wi, bi, Wf, bf, ln_w, ln_b, Wout):
        import jax, jax.numpy as jnp
        import numpy as np
        B, S, D = (2, 128, 128)
        NH = 8
        QK = D // 2
        V = D
        DQK = QK // NH
        DV = V // NH
        CAP = 15.0
        EPS = 1e-06

        def soft_cap(t, cap=CAP):
            return cap * jnp.tanh(t / cap)

        def _mlstm_forward(x, Wq, Wk, Wv, Wog, Wi, bi, Wf, bf, ln_w, ln_b, Wout):
            Bx, Sx, _ = x.shape
            q = (x @ Wq.T).reshape(Bx, Sx, NH, DQK)
            k = (x @ Wk.T).reshape(Bx, Sx, NH, DQK)
            v = (x @ Wv.T).reshape(Bx, Sx, NH, DV)
            o_preact = x @ Wog.T
            i_pre = soft_cap(x @ Wi.T + bi)
            f_pre = soft_cap(x @ Wf.T + bf)
            qT = jnp.moveaxis(q, 1, 0)
            kT = jnp.moveaxis(k, 1, 0)
            vT = jnp.moveaxis(v, 1, 0)
            iT = jnp.moveaxis(i_pre, 1, 0)
            fT = jnp.moveaxis(f_pre, 1, 0)
            qk_scale = DQK ** (-0.5)

            def step(carry, inp):
                C, n, m = carry
                q_t, k_t, v_t, i_t, f_t = inp
                m_new = jnp.maximum(f_t + m, i_t)
                f_act = jnp.exp(f_t + m - m_new)
                i_act = jnp.exp(i_t - m_new)
                C = f_act[..., None, None] * C + i_act[..., None, None] * (k_t[..., :, None] * v_t[..., None, :])
                n = f_act[..., None] * n + i_act[..., None] * k_t
                qs = q_t * qk_scale
                num = jnp.einsum('bhk,bhkv->bhv', qs, C)
                qn = jnp.einsum('bhk,bhk->bh', qs, n)
                denom = jnp.maximum(jnp.abs(qn), jnp.exp(-m_new)) + 1e-06
                h_t = num / denom[..., None]
                return ((C, n, m_new), h_t)
            C0 = jnp.zeros((Bx, NH, DQK, DV), x.dtype)
            n0 = jnp.zeros((Bx, NH, DQK), x.dtype)
            m0 = jnp.zeros((Bx, NH), x.dtype)
            _, hs = jax.lax.scan(step, (C0, n0, m0), (qT, kT, vT, iT, fT))
            h = jnp.moveaxis(hs, 0, 1).reshape(Bx, Sx, NH * DV)
            mu = jnp.mean(h, axis=-1, keepdims=True)
            var = jnp.mean((h - mu) ** 2, axis=-1, keepdims=True)
            h_norm = (h - mu) * jax.lax.rsqrt(var + EPS) * ln_w + ln_b
            h_out = jax.nn.sigmoid(o_preact) * h_norm
            y = h_out @ Wout.T
            return y
        return _mlstm_forward(x, Wq, Wk, Wv, Wog, Wi, bi, Wf, bf, ln_w, ln_b, Wout)

    def _L0_xattn_ref(Q, K, V, mask, wq, wk, wv, wo, bo):
        import jax, jax.numpy as jnp
        import numpy as np
        B, L, D, H = (2, 256, 128, 16)
        HD = D // H

        def _xavier(key, out_f, in_f):
            std = (2.0 / (in_f + out_f)) ** 0.5
            return jax.random.normal(key, (out_f, in_f), dtype=jnp.float32) * std
        N, Lq, Dm = Q.shape
        q = (Q @ wq.T).reshape(N, Lq, H, HD).transpose(0, 2, 1, 3)
        kk = (K @ wk.T).reshape(N, Lq, H, HD).transpose(0, 2, 1, 3)
        v = (V @ wv.T).reshape(N, Lq, H, HD).transpose(0, 2, 1, 3)
        score = jnp.einsum('bhqd,bhkd->bhqk', q, kk) / jnp.sqrt(jnp.float32(HD))
        score = jnp.where(mask == 0, -jnp.inf, score)
        weights = jax.nn.softmax(score, axis=-1)
        attn = jnp.einsum('bhqk,bhkd->bhqd', weights, v)
        out = attn.transpose(0, 2, 1, 3).reshape(N, Lq, Dm)
        return out @ wo.T + bo

    def _L0_ffn_ref(x, phi, W, b):
        import jax, jax.numpy as jnp
        import numpy as np
        B, M, D = (4, 256, 128)
        N, P = (64, 32)
        logits = jnp.einsum('bmd,dnp->bmnp', x, phi)
        dispatch = jax.nn.softmax(logits, axis=0)
        bsz, m, n, p = logits.shape
        combine = jax.nn.softmax(logits.reshape(bsz, m, n * p), axis=-1).reshape(bsz, m, n, p)
        slots = jnp.einsum('bmd,bmnp->bnpd', x, dispatch)
        y = jnp.einsum('bnpd,nde->bnpe', slots, W) + b[None, :, None, :]
        out = jnp.einsum('bnpd,bmnp->bmd', y, combine)
        return out

    def _L1_attn_ref(representations, Wc, bc, Wo, bo):
        import jax, jax.numpy as jnp
        import numpy as np
        N_INPUT = 128
        N_HEAD = 16
        ATT_DIM = N_INPUT // N_HEAD * N_HEAD
        V_DIM = N_INPUT // 2 * N_HEAD
        COMB_DIM = 2 * ATT_DIM + V_DIM
        SCALE = (N_INPUT // N_HEAD) ** 0.5
        B, T, D = representations.shape
        H = N_HEAD
        dh = ATT_DIM // H
        dv = V_DIM // H
        cp = jax.nn.leaky_relu(jnp.einsum('btd,cd->btc', representations, Wc) + bc)
        q = cp[..., :ATT_DIM].reshape(B, T, H, dh)
        k = cp[..., ATT_DIM:2 * ATT_DIM].reshape(B, T, H, dh)
        v = cp[..., 2 * ATT_DIM:].reshape(B, T, H, dv)
        scores = jnp.einsum('bqhd,bkhd->bhqk', q, k) / SCALE
        attn = jax.nn.softmax(scores, axis=-1)
        out = jnp.einsum('bhqk,bkhd->bqhd', attn, v).reshape(B, T, V_DIM)
        proj = jax.nn.leaky_relu(jnp.einsum('btv,dv->btd', out, Wo) + bo)
        return representations + proj

    def _L1_xattn_ref(query, key_value, Wq, bq, Wk, bk, Wv, bv, Wo, bo):
        import jax, jax.numpy as jnp
        import numpy as np
        D_MODEL = 128
        NUM_HEADS = 16
        HEAD_DIM = D_MODEL // NUM_HEADS
        B, SQ, _ = query.shape
        SKV = key_value.shape[1]
        Q = query @ Wq.T + bq
        K = key_value @ Wk.T + bk
        V = key_value @ Wv.T + bv
        Q = Q.reshape(B, SQ, NUM_HEADS, HEAD_DIM).transpose(0, 2, 1, 3)
        K = K.reshape(B, SKV, NUM_HEADS, HEAD_DIM).transpose(0, 2, 1, 3)
        V = V.reshape(B, SKV, NUM_HEADS, HEAD_DIM).transpose(0, 2, 1, 3)
        scores = jnp.einsum('bhqd,bhkd->bhqk', Q, K) / np.sqrt(HEAD_DIM)
        causal = jnp.tril(jnp.ones((SQ, SKV), bool))
        scores = jnp.where(causal[None, None], scores, -jnp.inf)
        attn = jax.nn.softmax(scores, axis=-1)
        out = jnp.einsum('bhqk,bhkd->bhqd', attn, V)
        out = out.transpose(0, 2, 1, 3).reshape(B, SQ, D_MODEL)
        return out @ Wo.T + bo

    def _L1_ffn_ref(x, fast_b, w_fc, w_proj, u, v, gate):
        import jax, jax.numpy as jnp
        import numpy as np

        def _bitlinear(x, w_latent):
            scale = jax.lax.stop_gradient(jnp.clip(jnp.mean(jnp.abs(w_latent), axis=1, keepdims=True), 1e-05, None))
            tern = jnp.clip(jnp.round(w_latent / scale), -1.0, 1.0)
            w = w_latent + jax.lax.stop_gradient(tern - w_latent)
            return x @ (w * scale).T
        h = _bitlinear(x, w_fc) + gate * (x @ v.T @ fast_b.T @ u.T)
        r = jnp.maximum(h, 0.0)
        return _bitlinear(r * r, w_proj)
    x = _layernorm(x + _L0_attn_ref(x, L0_attn_Wq, L0_attn_Wk, L0_attn_Wv, L0_attn_Wog, L0_attn_Wi, L0_attn_bi, L0_attn_Wf, L0_attn_bf, L0_attn_ln_w, L0_attn_ln_b, L0_attn_Wout), axis=-1)
    x = _layernorm(x + _L0_xattn_ref(x, ctx_1024, ctx_1024, mask_1x1xSxS2_ik0, L0_xattn_wq, L0_xattn_wk, L0_xattn_wv, L0_xattn_wo, L0_xattn_bo), axis=-1)
    x = _layernorm(x + _L0_ffn_ref(x, L0_ffn_phi, L0_ffn_W, L0_ffn_b), axis=-1)
    x = _layernorm(x + _L1_attn_ref(x, L1_attn_Wc, L1_attn_bc, L1_attn_Wo, L1_attn_bo), axis=-1)
    x = _layernorm(x + _L1_xattn_ref(x, ctx_1024, L1_xattn_Wq, L1_xattn_bq, L1_xattn_Wk, L1_xattn_bk, L1_xattn_Wv, L1_xattn_bv, L1_xattn_Wo, L1_xattn_bo), axis=-1)
    x = _layernorm(x + _L1_ffn_ref(x, L1_ffn_fast_b, L1_ffn_w_fc, L1_ffn_w_proj, L1_ffn_u, L1_ffn_v, L1_ffn_gate), axis=-1)
    return x

_drawn_inputs = setup_inputs


def setup_inputs(seed=0):
    import zlib

    import numpy as np

    out = dict(_drawn_inputs(seed))
    spreads = {'L0_attn_ln_w': (1.0, 0.6),
     'L0_attn_ln_b': (0.0, 0.384),
     'L0_xattn_bo': (0.0, 0.1),
     'L1_attn_bc': (0.0, 0.8),
     'L1_attn_bo': (0.0, 0.287),
     'L1_xattn_bq': (0.0, 0.399),
     'L1_xattn_bk': (0.0, 2.0),
     'L1_xattn_bv': (0.0, 0.1),
     'L1_xattn_bo': (0.0, 0.1)}
    factors = {'L0_attn_Wog': 8.0,
     'L0_attn_Wi': 6.711,
     'L0_attn_bi': 39.293,
     'L0_attn_Wf': 27.718,
     'L0_attn_bf': 64.0,
     'L0_ffn_b': 64.0,
     'L1_attn_Wc': 8.0,
     'L1_attn_Wo': 8.0,
     'L1_ffn_fast_b': 8.0,
     'L1_ffn_w_fc': 7.289,
     'L1_ffn_w_proj': 6.723,
     'L1_ffn_u': 8.0,
     'L1_ffn_v': 8.0}
    for name, (base, spread) in spreads.items():
        noise = np.random.default_rng([zlib.crc32(name.encode()), seed]).standard_normal(out[name].shape)
        drawn = base * np.exp(spread * noise) if base else spread * noise
        out[name] = jnp.asarray(drawn.astype(out[name].dtype))
    for name, factor in factors.items():
        out[name] = (out[name] * factor).astype(out[name].dtype)
    return out
```

```python
from contextlib import ExitStack

import concourse.bass as bass
from concourse import mybir

F32 = mybir.dt.float32
BF16 = mybir.dt.bfloat16
I32 = mybir.dt.int32
ALU = mybir.AluOpType
ACT = mybir.ActivationFunctionType
AX = mybir.AxisListType

B, S, D = 8, 256, 128
P = 128
TT = S // P
EPS = 1e-5
BIG = 1e30
H, HD = 16, 8
NG, GJ = 4, 4
PARTS = 3
STACK = PARTS * PARTS * HD
SCALE = float(HD) ** -0.5


class Scope:

    def __init__(self, nc, ctx, tag):
        self.nc, self.ctx, self.tag, self.sems = nc, ctx, tag, []
        ctx.callback(self.clear)

    def sb(self, name, shape, dt=F32):
        return self.ctx.enter_context(self.nc.sbuf_tensor(f"{self.tag}_{name}", shape, dt))

    def ps(self, name, shape, dt=F32):
        return self.ctx.enter_context(self.nc.psum_tensor(f"{self.tag}_{name}", shape, dt))

    def sem(self, name):
        self.sems.append(self.nc.alloc_semaphore(f"{self.tag}_{name}"))
        return self.sems[-1]

    def clear(self):
        if self.sems:
            self.nc.all_engine_barrier()
            self.nc.clear_and_free_semaphores(self.sems)
            self.nc.all_engine_barrier()


class Chain:

    def __init__(self, eng, sem):
        self.eng, self.sem, self.n, self.off = eng, sem, 0, 0

    def link(self, ins):
        self.n += 1
        ins.then_inc(self.sem, 1)
        self.eng.wait_ge(self.sem, self.off + self.n)


def settle(eng, spare):
    eng.sem_inc(spare, 1)


def ring_uses(names, first, off):
    return {name: ((first + i) % 2, (first + i) // 2 + 1 + off) for i, name in enumerate(names)}



def norm_stats(dve, link, t, ve_done, spare, eps=EPS):
    for tt in range(TT):
        dve.bn_stats(t.stats[:, tt, :], t.r[:, tt, :]) if tt < TT - 1 else \
            link(dve.bn_stats(t.stats[:, tt, :], t.r[:, tt, :]))
    settle(dve, spare)
    for tt in range(TT):
        dve.bn_aggr(t.mv[:, tt, :], t.stats[:, tt, :]) if tt < TT - 1 else \
            link(dve.bn_aggr(t.mv[:, tt, :], t.stats[:, tt, :]))
    dve.tensor_scalar(t.ve[:, :], t.mv[:, :, 1], eps, None, ALU.add).then_inc(ve_done, 1)


def norm_apply(dve, t, out, tt):
    return dve.tensor_scalar(out, t.r[:, tt, :], t.mv[:, tt, 0:1], t.rstd[:, tt:tt + 1], ALU.subtract, ALU.mult)


class NormTiles:
    def __init__(self, sc):
        self.r = sc.sb("r", [P, TT, D])
        self.stats = sc.sb("stats", [P, TT, 6])
        self.mv = sc.sb("mv", [P, TT, 2])
        self.ve = sc.sb("ve", [P, TT])
        self.rstd = sc.sb("rstd", [P, TT])
        self.half = sc.sb("half", [P, TT])



def attention(nc, x_all, w, tag, causal=False, masked=False, own=False, wide=False):
    C = 2 if wide else 1
    VH = 64 if wide else 32
    NV = 4 if wide else 1
    NO = 2 if wide else 1
    OS = 1 if wide else 2
    LOADS = 2 * PARTS + 1
    UNITS = 2 * NG
    NB = 3
    with ExitStack() as ctx:
        sc = Scope(nc, ctx, tag)
        A = sc.ps("A", [P, 2, 512])
        Sc = sc.ps("Sc", [P, 2, 1024])
        O = sc.ps("O", [P, OS, C, 512 // C])
        Zc = sc.ps("Zc", [P, 512]) if wide else O[:, 0, 0, :]

        wq = sc.sb("wq", [P, P])
        wk = sc.sb("wk", [P, P])
        wv = sc.sb("wv", [P, 1024 if wide else P])
        wo = sc.sb("wo", [P, NG * C, D])
        bo = sc.sb("bo", [P, D])
        bq = sc.sb("bq", [P, 1])
        bk = sc.sb("bk", [P, 1])
        bv = sc.sb("bv", [P, 1024 if wide else P])
        ident = sc.sb("ident", [P, P])
        identb = sc.sb("identb", [P, P], BF16)
        collect = sc.sb("collect", [P, NG, 32 if wide else P])
        spread = sc.sb("spread", [P, NG, P])
        maskq = sc.sb("maskq", [P, TT, 2, S if masked else P], BF16)
        maskk = sc.sb("maskk", [P, TT, 2, S if masked else P], BF16)
        mask32 = sc.sb("mask32", [P, 2, TT, S], I32) if masked else None

        xb = sc.sb("xb", [P, TT, D])
        xT = sc.sb("xT", [P, S])
        ctxT = sc.sb("ctxT", [P, NB, S])
        z = sc.sb("z", [P, 2, S])
        zu = sc.sb("zu", [P, 2, S])
        zl = sc.sb("zl", [P, 2, S]) if own else z
        parts = sc.sb("parts", [P, 2, PARTS, S], BF16)
        qst = [sc.sb(f"qst{i}", [P, H, S], BF16) for i in range(NB)]
        kst = [sc.sb(f"kst{i}", [P, H, S], BF16) for i in range(NB)]
        V = [sc.sb(f"V{i}", [P, TT, H, VH]) for i in range(NB)]
        zv = sc.sb("zv", [P, TT, 1024]) if wide else None
        mx = sc.sb("mx", [P, TT, H])
        nmT = sc.sb("nmT", [H, S], BF16)
        E = sc.sb("E", [P, 4, GJ, S])
        Os = sc.sb("Os", [P, NG, C, S])
        Rz = sc.sb("Rz", [P, S])
        ON = sc.sb("ON", [P, NG, C, S])
        xres = sc.sb("xres", [P, TT, D])
        res = sc.sb("res", [P, TT, D])
        nt = NormTiles(sc)
        scratch = [nc.dram_tensor(f"{tag}_scratch{i}", (2, PARTS, P, S), BF16).ap() for i in range(NB)]

        a_full = [sc.sem(f"a_full{i}") for i in range(2)]
        a_free = [sc.sem(f"a_free{i}") for i in range(2)]
        (w_in, const_in, cleared, consts, scores, exp_done, pv_done, o_done, zc_full, rz_done, chain, pchain, mrow,
         xb_done, ctx_in, parts_done, scr_done, stack_in, v_done, leaky_done, xres_done, ve_done, rstd_done, x_done,
         spare) = (sc.sem(n) for n in (
             "w_in", "const_in", "cleared", "consts", "scores", "exp_done", "pv_done", "o_done", "zc_full", "rz_done",
             "chain", "pchain", "mrow", "xb_done", "ctx_in", "parts_done", "scr_done", "stack_in", "v_done",
             "leaky_done", "xres_done", "ve_done", "rstd_done", "x_done", "spare"))

        has_bias = f"{tag}_bq" in w
        loads = [(wq, w[f"{tag}_wq"]), (wk, w[f"{tag}_wk"]), (wv, w[f"{tag}_wv"]), (wo, w[f"{tag}_wo"]),
                 (bo, w[f"{tag}_bo"].partition_broadcast(P)), (ident, w["ident"]), (identb, w["identb"]),
                 (collect, w["collect_wide" if wide else "collect"]), (spread, w["spread"])]
        if has_bias:
            loads += [(bq, w[f"{tag}_bq"]), (bk, w[f"{tag}_bk"]), (bv, w[f"{tag}_bv"].partition_broadcast(P))]
        if causal:
            loads += [(maskq, w["causal_q"]), (maskk, w["causal_k"])]
        if masked:
            loads += [(mask32, w["mask"])]

        def m_names(g):
            return [f"m{g}{u}{qt}" for u in range(2) for qt in range(TT)]

        order = [("max", m_names(0)), ("prep", ["xT"]), ("max", m_names(1)),
                 ("prep", [f"v{n}" for n in range(NV)] + ["q", "k"]), ("max", m_names(2) + m_names(3)),
                 ("weights", ["b0", "b1"]), ("max", ["mT"]), ("weights", [f"out{n}" for n in range(NO)])]

        class Step:

            def __init__(self, s, turn, first, off, has=("max", "weights", "prep")):
                self.bm = s if "max" in has else None
                self.bw = s - 1 if "weights" in has else None
                self.bp = s + 1 if "prep" in has else None
                self.im, self.iw, self.ip = turn % NB, (turn - 1) % NB, (turn + 1) % NB
                self.uses = [n for kind, ns in order if kind in has for n in ns]
                self.ring = ring_uses(self.uses, first, off)

        full = [n for _, ns in order for n in ns]

        def walk(eng, do, chains=()):
            n = 0
            for s, has in ((-1, ("prep",)), (0, ("max", "prep"))):
                step = Step(s, s, n, 0, has)
                do(step)
                n += len(step.uses)
            per = NB * len(full)
            assert per % 2 == 0
            marks = [c.n for c in chains]
            rounds = (B - 2) // NB
            with eng.Fori(0, rounds) as i:
                for c in chains:
                    c.off = i * c.per
                for k in range(NB):
                    do(Step(i * NB + (1 + k), 1 + k, n + k * len(full), i * (per // 2)))
            for c, m in zip(chains, marks):
                assert c.n - m == c.per, (tag, c.n - m)
                c.off, c.n = 0, m + rounds * c.per
            n += rounds * per
            for s, has in ((B - 1, ("max", "weights")), (B, ("weights",))):
                step = Step(s, s, n, 0, has)
                do(step)
                n += len(step.uses)

        def first_of(b, n):
            return isinstance(b, int) and b < n

        def tiles(b, tt=0, n=TT):
            return slice(2 * b + tt, 2 * b + tt + n) if isinstance(b, int) else bass.ds(b * 2 + tt, n)

        with nc.Block() as block:

            @block.sync
            def _(sp):
                for dst, src in loads:
                    sp.dma_start(dst[:], src).then_inc(w_in, 16)
                sp.wait_ge(cleared, 2 * NB)
                for i in range(NB):
                    sp.dma_start(kst[i][STACK:STACK + 1], w["ones_row"]).then_inc(const_in, 16)

                def do(st):
                    if st.bp is not None:
                        if not own:
                            if not first_of(st.bp, NB):
                                sp.wait_ge(parts_done, st.bp - (NB - 2))
                                settle(sp, spare)
                            sp.dma_start(ctxT[:, st.ip, :], w["ctxT"][st.bp]).then_inc(ctx_in, 16)
                        sp.wait_ge(parts_done, st.bp + 2)
                        for t in range(2):
                            sp.dma_start(scratch[st.ip][t].rearrange("c p n -> p c n"),
                                         parts[:, t]).then_inc(scr_done, 16)
                        sp.wait_ge(scr_done, 32 * (st.bp + 1))
                        settle(sp, spare)
                        if not first_of(st.bp, NB):
                            sp.wait_ge(scores, UNITS * (st.bp - 2) + 1)
                        for a in range(PARTS):
                            rows = slice(a * PARTS * HD, (a + 1) * PARTS * HD)
                            src = scratch[st.ip][0, a].rearrange("(d h) n -> d (h n)", d=HD)
                            sp.dma_start(qst[st.ip][rows].rearrange("p h n -> p (h n)"),
                                         src.unsqueeze(0).broadcast_to([PARTS, HD, H * S])).then_inc(stack_in, 16)
                            src = scratch[st.ip][1].rearrange("c (d h) n -> (c d) (h n)", d=HD)
                            sp.dma_start(kst[st.ip][rows].rearrange("p h n -> p (h n)"), src).then_inc(stack_in, 16)
                        sp.dma_start(qst[st.ip][STACK:STACK + 1], w["zeros_row"]).then_inc(stack_in, 16)
                    if st.bm is not None:
                        bank, k = st.ring["mT"]
                        sp.wait_ge(a_free[bank], k + 1)
                        sp.dma_start(qst[st.im][STACK:STACK + 1], nmT[:, :]).then_inc(mrow, 16)

                walk(sp, do)

            @block.gpsimd
            def _(pool):
                for s, n in ((a_free[0], 1), (a_free[1], 1), (exp_done, 2), (pv_done, 2), (o_done, OS),
                             (parts_done, 1), (scores, 1)):
                    pool.sem_inc(s, n)
                for t in (*qst, *kst):
                    pool.memset(t[:].bitcast(F32), 0.0).then_inc(cleared, 1)
                for t in V:
                    pool.memset(t[:], 0.0).then_inc(consts, 1)
                pool.memset(nt.half[:, :], -0.5).then_inc(consts, 1)
                pool.wait_ge(consts, NB + 1)
                if not wide:
                    for t in V:
                        pool.memset(t[:, :, :, HD:HD + 1], 1.0).then_inc(consts, 1)
                    pool.wait_ge(consts, 2 * NB + 1)
                pool.wait_ge(w_in, 16 * len(loads))
                ch = Chain(pool, pchain)
                ch.per = NB * 3

                def do(st):
                    if st.bp is not None:
                        pool.tensor_copy(xb[:, :, :], x_all[:, tiles(st.bp), :]).then_inc(xb_done, 1)
                        if own:
                            pool.wait_ge(leaky_done, st.bp + 1)
                        else:
                            for name in ("q", "k"):
                                bank, k = st.ring[name]
                                pool.wait_ge(a_free[bank], k + 1)
                        pool.wait_ge(scr_done, 32 * st.bp)
                        settle(pool, spare)
                        ch.link(pool.tensor_copy(parts[:, :, 0, :], zl[:]))
                        ch.link(pool.tensor_tensor(zu[:], zl[:], parts[:, :, 0, :], ALU.subtract))
                        settle(pool, spare)
                        ch.link(pool.tensor_copy(parts[:, :, 1, :], zu[:]))
                        pool.tensor_tensor(parts[:, :, 2, :], zu[:], parts[:, :, 1, :],
                                           ALU.subtract).then_inc(parts_done, 1)
                    if st.bw is not None:
                        other = x_all[:, tiles(st.bw), :] if own else bo[:, :].unsqueeze(1).broadcast_to([P, TT, D])
                        pool.tensor_tensor(xres[:, :, :], x_all[:, tiles(st.bw), :], other,
                                           ALU.add).then_inc(xres_done, 1)
                        pool.wait_ge(ve_done, st.bw + 1)
                        pool.tensor_tensor(nt.rstd[:, :], nt.ve[:, :], nt.half[:, :], ALU.pow).then_inc(rstd_done, 1)

                walk(pool, do, [ch])

            @block.scalar
            def _(act):
                act.wait_ge(w_in, 16 * len(loads))

                def take(st, name):
                    bank, k = st.ring[name]
                    act.wait_ge(a_full[bank], k)
                    return A[:, bank, :], a_free[bank]

                def exps(st, g):
                    for kt in range(TT):
                        act.wait_ge(scores, UNITS * st.bw + 2 * g + kt + 2)
                        act.wait_ge(pv_done, NG * st.bw + g + 1)
                        slot = (2 * g + kt) % 4
                        if causal and kt == 1:
                            src = Sc[:, kt, 0:GJ * P].rearrange("p (j q) -> p j q", j=GJ)
                            dst = E[:, slot, :, P:S]
                        else:
                            src = Sc[:, kt, :].rearrange("p (j q) -> p j q", j=GJ)
                            dst = E[:, slot, :, :]
                        act.activation(dst, src, ACT.Exp, scale=SCALE).then_inc(exp_done, 1)

                def keep(st, g):
                    act.wait_ge(pv_done, NG * st.bw + g + 3)
                    act.activation(Os[:, g], O[:, g % OS, :, 0:S], ACT.Copy).then_inc(o_done, 1)

                def do(st):
                    w_, p_ = st.bw is not None, st.bp is not None
                    if w_:
                        exps(st, 0)
                    if p_:
                        src, done = take(st, "xT")
                        act.activation(xT[:, :], src[:, 0:S], ACT.Copy).then_inc(done, 1)
                    if w_:
                        exps(st, 1)
                        keep(st, 0)
                    if p_:
                        for t, (name, bias) in enumerate((("q", bq), ("k", bk))):
                            src, done = take(st, name)
                            if t == 0:
                                act.wait_ge(parts_done, st.bp + 1)
                            act.activation(z[:, t, :], src[:, 0:S], ACT.Identity,
                                           bias=bias[:, 0:1] if has_bias else 0.0).then_inc(done, 1)
                    if w_:
                        exps(st, 2)
                        keep(st, 1)
                        exps(st, 3)
                        keep(st, 2)
                        keep(st, 3)
                    if st.bm is not None:
                        src, done = take(st, "mT")
                        act.wait_ge(mrow, 16 * st.bm)
                        act.activation(nmT[:, :], src[0:H, 0:S], ACT.Copy, scale=-1.0).then_inc(done, 1)

                walk(act, do)

            @block.vector
            def _(dve):
                dve.wait_ge(w_in, 16 * len(loads))
                ready = NB + 1 if wide else 2 * NB + 1
                dve.wait_ge(consts, ready)
                ch = Chain(dve, chain)
                ch.per = NB * (4 if own else 2)
                if masked:
                    for n, m in enumerate((maskq, maskk)):
                        for c in range(2):
                            dve.tensor_scalar(m[:, :, c, :], mask32[:, n], 0, -BIG, ALU.is_equal,
                                              ALU.mult).then_inc(consts, 1)

                def take(st, name):
                    bank, k = st.ring[name]
                    dve.wait_ge(a_full[bank], k)
                    return A[:, bank, :], a_free[bank]

                def maxima(st, g):
                    for u in range(2):
                        for qt in range(TT):
                            src, done = take(st, f"m{g}{u}{qt}")
                            keys = P if causal and qt == 0 else S
                            h = GJ * g + 2 * u
                            dve.tensor_reduce(mx[:, qt, h:h + 2],
                                              src[:, 0:2 * keys].rearrange("p (h k) -> p h k", h=2),
                                              AX.X, ALU.max).then_inc(done, 1)

                def project(st):
                    if wide:
                        vals = V[st.ip][:].rearrange("p t h v -> p t (h v)")
                        for n in range(NV):
                            src, done = take(st, f"v{n}")
                            cols = slice(512 * (n % 2), 512 * (n % 2) + 512)
                            dve.tensor_tensor(zv[:, n // 2, cols], src, bv[:, cols], ALU.add).then_inc(done, 1)
                            dve.wait_ge(done, st.ring[f"v{n}"][1] + 1)
                            dve.scalar_tensor_tensor(vals[:, n // 2, cols], zv[:, n // 2, cols], 0.01,
                                                     zv[:, n // 2, cols], ALU.mult, ALU.max).then_inc(v_done, 1)
                    else:
                        src, done = take(st, "v0")
                        src = src[:, 0:S].rearrange("p (t h d) -> p t h d", t=TT, h=H)
                        for tt in range(TT):
                            dst = V[st.ip][:, tt, :, 0:HD]
                            if has_bias:
                                ins = dve.tensor_tensor(dst, src[:, tt], bv[:, :].rearrange("p (h d) -> p h d", h=H),
                                                        ALU.add)
                            else:
                                ins = dve.tensor_copy(dst, src[:, tt])
                        ins.then_inc(done, 1)
                    if own:
                        for name in ("q", "k"):
                            bank, k = st.ring[name]
                            dve.wait_ge(a_free[bank], k + 1)
                        dve.scalar_tensor_tensor(zl[:], z[:], 0.01, z[:], ALU.mult, ALU.max).then_inc(leaky_done, 1)

                def divide(st):
                    for n in range(2):
                        src, done = take(st, f"b{n}")
                        gs = slice(2 * n, 2 * n + 2)
                        src = src.rearrange("p (g q) -> p g q", g=2)
                        if C == 1:
                            dve.tensor_tensor(ON[:, gs, 0], Os[:, gs, 0], src, ALU.mult).then_inc(done, 1)
                        else:
                            dve.tensor_tensor(ON[:, gs], Os[:, gs], src.unsqueeze(2).broadcast_to([P, 2, C, S]),
                                              ALU.mult).then_inc(done, 1)

                def finish(st):
                    dve.wait_ge(xres_done, st.bw + 1)
                    for n in range(NO):
                        src, done = take(st, f"out{n}")
                        tts = slice(n * TT // NO, (n + 1) * TT // NO)
                        src = src[:, 0:TT // NO * D].rearrange("p (t d) -> p t d", d=D)
                        if own:
                            boc = bo[:, :].unsqueeze(1).broadcast_to([P, TT // NO, D])
                            dve.tensor_tensor(res[:, tts], src, boc, ALU.add).then_inc(done, 1)
                        else:
                            dve.tensor_tensor(nt.r[:, tts], src, xres[:, tts], ALU.add).then_inc(done, 1)
                    for n in range(NO):
                        bank, k = st.ring[f"out{n}"]
                        dve.wait_ge(a_free[bank], k + 1)
                    if own:
                        ch.link(dve.scalar_tensor_tensor(nt.r[:], res[:], 0.01, res[:], ALU.mult, ALU.max))
                        ch.link(dve.tensor_tensor(nt.r[:], nt.r[:], xres[:], ALU.add))
                    norm_stats(dve, ch.link, nt, ve_done, spare)
                    dve.wait_ge(rstd_done, st.bw + 1)
                    for tt in range(TT):
                        norm_apply(dve, nt, x_all[:, tiles(st.bw, tt, 1), :].squeeze(1), tt).then_inc(x_done, 1)

                def do(st):
                    m_, w_, p_ = st.bm is not None, st.bw is not None, st.bp is not None
                    if m_:
                        maxima(st, 0)
                        maxima(st, 1)
                    if p_:
                        project(st)
                    if m_:
                        maxima(st, 2)
                    if w_:
                        dve.wait_ge(zc_full, st.bw + 1)
                        dve.reciprocal(Rz[:, :], Zc[:, 0:S]).then_inc(rz_done, 1)
                    if m_:
                        maxima(st, 3)
                    if w_:
                        divide(st)
                        finish(st)

                walk(dve, do, [ch])

            @block.tensor
            def _(pe):
                pe.wait_ge(w_in, 16 * len(loads))
                pe.wait_ge(const_in, 16 * NB)
                pe.wait_ge(consts, (NB + 1 if wide else 2 * NB + 1) + (4 if masked else 0))

                def use(st, name):
                    bank, k = st.ring[name]
                    pe.wait_ge(a_free[bank], k)
                    return A[:, bank, :], a_full[bank]

                def maxima(st, g):
                    q, k = qst[st.im], kst[st.im]
                    if g == 0:
                        pe.wait_ge(stack_in, 16 * LOADS * (st.bm + 1))
                    for u in range(2):
                        for qt in range(TT):
                            dst, done = use(st, f"m{g}{u}{qt}")
                            keys = P if causal and qt == 0 else S
                            for n in range(2):
                                h = GJ * g + 2 * u + n
                                mm = pe.matmul(dst[:, n * keys:(n + 1) * keys], q[:, h, qt * P:(qt + 1) * P],
                                               k[:, h, 0:keys], start=n == 0, stop=not (masked or causal) and n == 1,
                                               skip_group_check=True)
                            if masked:
                                mm = pe.matmul(dst[:, 0:2 * S], identb[:, :],
                                               maskq[:, qt].rearrange("p c k -> p (c k)"), start=False, stop=True,
                                               skip_group_check=True)
                            if causal:
                                mm = pe.matmul(dst[:, 0:2 * keys].rearrange("p (c k) -> p c k", c=2)[:, :, keys - P:keys],
                                               identb[:, :], maskq[:, qt], start=False, stop=True,
                                               skip_group_check=True)
                            mm.then_inc(done, 1)

                def by_key(st, g):
                    q, k = qst[st.iw], kst[st.iw]
                    if g == 0:
                        pe.wait_ge(mrow, 16 * (st.bw + 1))
                    for kt in range(TT):
                        pe.wait_ge(exp_done, UNITS * st.bw + 2 * g + kt + 1)
                        short = causal and kt == 1
                        nq = P if short else S
                        for bank in range(1 if short else 2):
                            heads = range(GJ) if short else range(2 * bank, 2 * bank + 2)
                            dst = Sc[:, kt, 512 * bank:512 * bank + 512]
                            for n, j in enumerate(heads):
                                mm = pe.matmul(dst[:, n * nq:(n + 1) * nq],
                                               k[:, GJ * g + j, kt * P:(kt + 1) * P],
                                               q[:, GJ * g + j, S - nq:S], start=n == 0,
                                               stop=not (masked or causal) and j == heads[-1], skip_group_check=True)
                            if masked:
                                mm = pe.matmul(dst, identb[:, :], maskk[:, kt].rearrange("p c q -> p (c q)"),
                                               start=False, stop=True, skip_group_check=True)
                            if causal:
                                d3 = dst.rearrange("p (n q) -> p n q", n=len(heads))
                                for n in range(0, len(heads), 2):
                                    mm = pe.matmul(d3[:, n:n + 2, 0:P], identb[:, :], maskk[:, kt],
                                                   start=False, stop=n + 2 == len(heads), skip_group_check=True)
                        mm.then_inc(scores, 1)

                def outputs(st, g):
                    if g == 0 and wide:
                        pe.wait_ge(v_done, NV * (st.bw + 1))
                    pe.wait_ge(o_done, NG * st.bw + g + 1)
                    for kt in range(TT):
                        pe.wait_ge(exp_done, UNITS * st.bw + 2 * g + kt + 3)
                        slot = (2 * g + kt) % 4
                        q0 = P if causal and kt == 1 else 0
                        for c in range(C):
                            for j in range(GJ):
                                mm = pe.matmul(O[32 * j:32 * j + 32, g % OS, c, q0:S],
                                               V[st.iw][:, kt, GJ * g + j, 32 * c:32 * c + 32],
                                               E[:, slot, j, q0:S], start=kt == 0 and c == 0, stop=kt == 1,
                                               skip_group_check=True)
                        if wide:
                            for j in range(GJ):
                                mm = pe.matmul(Zc[32 * j:32 * j + 32, 0:S], collect[:, g, :], E[:, slot, j, :],
                                               start=g == 0 and kt == 0, stop=g == NG - 1 and kt == 1,
                                               skip_group_check=True)
                    mm.then_inc(pv_done, 1)

                def denominators(st):
                    pe.wait_ge(o_done, NG * (st.bw + 1) + OS)
                    if wide:
                        pe.sem_inc(zc_full, 1)
                        return
                    for g in range(NG):
                        mm = pe.matmul(Zc[:, 0:S], collect[:, g, :], Os[:, g, 0, :], start=g == 0, stop=g == NG - 1)
                    mm.then_inc(zc_full, 1)

                def reciprocals(st):
                    pe.wait_ge(rz_done, st.bw + 1)
                    for n in range(2):
                        dst, done = use(st, f"b{n}")
                        for k in range(2):
                            mm = pe.matmul(dst[:, k * S:(k + 1) * S], spread[:, 2 * n + k, :], Rz[:, :], start=True,
                                           stop=True)
                        mm.then_inc(done, 1)

                def turn(st):
                    bank, k = st.ring["m311"]
                    pe.wait_ge(a_free[bank], k + 1)
                    dst, done = use(st, "mT")
                    for qt in range(TT):
                        mm = pe.transpose(dst[0:H, qt * P:(qt + 1) * P], mx[:, qt, :], ident[:, :])
                    mm.then_inc(done, 1)

                def turn_x(st):
                    pe.wait_ge(xb_done, st.bp + 1)
                    dst, done = use(st, "xT")
                    for tt in range(TT):
                        mm = pe.transpose(dst[:, tt * P:(tt + 1) * P], xb[:, tt, :], ident[:, :])
                    mm.then_inc(done, 1)

                def project(st):
                    bank, k = st.ring["xT"]
                    pe.wait_ge(a_free[bank], k + 1)
                    kv = xT[:, :] if own else ctxT[:, st.ip, :]
                    if not own:
                        pe.wait_ge(ctx_in, 16 * (st.bp + 1))
                    if wide:
                        for n in range(NV):
                            dst, done = use(st, f"v{n}")
                            pe.matmul(dst, kv[:, (n // 2) * P:(n // 2 + 1) * P],
                                      wv[:, 512 * (n % 2):512 * (n % 2) + 512], start=True,
                                      stop=True).then_inc(done, 1)
                    else:
                        dst, done = use(st, "v0")
                        for tt in range(TT):
                            mm = pe.matmul(dst[:, tt * D:(tt + 1) * D], kv[:, tt * P:(tt + 1) * P], wv[:, :],
                                           start=True, stop=True)
                        mm.then_inc(done, 1)
                    for name, wt, src in (("q", wq, xT[:, :]), ("k", wk, kv)):
                        dst, done = use(st, name)
                        pe.matmul(dst[:, 0:S], wt[:, :], src, start=True, stop=True).then_inc(done, 1)

                def output(st):
                    bank, k = st.ring["b1"]
                    pe.wait_ge(a_free[bank], k + 1)
                    for tt in range(TT):
                        if tt % (TT // NO) == 0:
                            dst, done = use(st, f"out{tt // (TT // NO)}")
                        at = tt % (TT // NO)
                        for n in range(NG * C):
                            mm = pe.matmul(dst[:, at * D:(at + 1) * D], ON[:, n // C, n % C, tt * P:(tt + 1) * P],
                                           wo[:, n, :], start=n == 0, stop=n == NG * C - 1, skip_group_check=True)
                        if tt % (TT // NO) == TT // NO - 1:
                            mm.then_inc(done, 1)

                def do(st):
                    m_, w_, p_ = st.bm is not None, st.bw is not None, st.bp is not None
                    if m_:
                        maxima(st, 0)
                    if w_:
                        by_key(st, 0)
                    if p_:
                        turn_x(st)
                    if m_:
                        maxima(st, 1)
                    if w_:
                        by_key(st, 1)
                        outputs(st, 0)
                    if p_:
                        project(st)
                    if w_:
                        by_key(st, 2)
                        outputs(st, 1)
                        by_key(st, 3)
                        outputs(st, 2)
                        outputs(st, 3)
                    if m_:
                        maxima(st, 2)
                    if w_:
                        denominators(st)
                    if m_:
                        maxima(st, 3)
                    if w_:
                        reciprocals(st)
                    if m_:
                        turn(st)
                    if w_:
                        output(st)

                walk(pe, do)


def moe(nc, x_all, w):
    NE, NP_ = 64, 32
    SL = NE * NP_
    CH = SL // P
    EC = P // NP_
    QT = 4
    NQ = CH // QT
    with ExitStack() as outer:
        so = Scope(nc, outer, "c")
        phi = so.sb("phi", [P, SL])
        xT = so.sb("xT", [P, B, S])
        yall = so.sb("yall", [P, CH, B, D + 1])
        rows = so.sb("rows", [P, B, S], BF16)
        ident = so.sb("ident", [P, P])

        with ExitStack() as ctx:
            sc = Scope(nc, ctx, "c1")
            We = [sc.sb(f"We{i}", [P, EC, D]) for i in range(2)]
            eb = sc.sb("eb", [P, CH, D])
            E = sc.sb("E", [P, 2, TT, B, P])
            M = sc.sb("M", [P, TT, P])
            Zs = sc.sb("Zs", [P, TT, P])
            Rz = sc.sb("Rz", [P, TT, P])
            slots = sc.sb("slots", [P, B, P])
            pm = sc.sb("pm", [P, TT, B, CH])
            R = sc.sb("R", [P, TT, B])
            RT = sc.sb("RT", [TT * B, P], BF16)
            L = sc.ps("L", [P, TT, B, P])
            ST = sc.ps("ST", [P, B, P])
            Y = sc.ps("Y", [P, B, P])
            w_in = [sc.sem(f"w_in{i}") for i in range(2)]
            e_in = [sc.sem(f"e_in{i}") for i in range(2)]
            xt_full, xt_done = sc.sem("xt_full"), sc.sem("xt_done")
            consts = sc.sem("consts")
            l_full = sc.sem("l_full")
            shifted = sc.sem("shifted")
            exp_done = sc.sem("exp_done")
            rz_done = sc.sem("rz_done")
            weights_done = sc.sem("weights_done")
            st_full, st_done = sc.sem("st_full"), sc.sem("st_done")
            y_full, y_done = sc.sem("y_full"), sc.sem("y_done")
            chain = sc.sem("chain")
            r_done, rt_full, rt_done, row_in = (sc.sem(n) for n in ("r_done", "rt_full", "rt_done", "row_in"))
            spare = sc.sem("spare")

            with nc.Block() as block:

                def loop(eng, do, chain=None):
                    do(0, 0, True, False)
                    n = chain.n if chain else 0
                    with eng.Fori(0, (CH - 2) // 2) as i:
                        if chain:
                            chain.off = i * chain.per
                        do(i * 2 + 1, 1, True, True)
                        do(i * 2 + 2, 0, True, True)
                    if chain:
                        assert chain.n - n == chain.per, chain.n - n
                        chain.off, chain.n = 0, n + chain.per * (CH - 2) // 2
                    do(CH - 1, 1, False, True)

                @block.sync
                def _(sp):
                    sp.dma_start(ident[:, :], w["ident"]).then_inc(w_in[0], 16)
                    sp.dma_start(phi[:, :], w["c_phi"]).then_inc(w_in[0], 16)
                    sp.dma_start(eb[:], w["c_b"]).then_inc(w_in[1], 16)

                    def do(c, par, more, before):
                        experts = slice(0, EC) if isinstance(c, int) and c == 0 else \
                            slice(EC * c, EC * c + EC) if isinstance(c, int) else bass.ds(c * EC, EC)
                        if before:
                            sp.wait_ge(y_full, c)
                            settle(sp, spare)
                        sp.dma_start(We[par][:], w["c_W"][:, experts, :]).then_inc(e_in[par], 16)
                    loop(sp, do)
                    sp.wait_ge(rt_done, 1)
                    sp.wait_ge(consts, 2)
                    for tt in range(TT):
                        sp.dma_start(rows[0:1, :, tt * P:(tt + 1) * P],
                                     RT[tt * B:(tt + 1) * B, :]).then_inc(row_in, 16)
                    sp.wait_ge(row_in, 32)

                @block.gpsimd
                def _(pool):
                    pool.sem_inc(y_full, 1)
                    pool.memset(rows[:], 0.0).then_inc(consts, 1)
                    pool.memset(yall[:, :, :, D:D + 1], 1.0).then_inc(consts, 1)

                    def do(c, par, more, before):
                        for tt in range(TT):
                            pool.wait_ge(rz_done, c * 2 + (tt + 1))
                            pool.tensor_tensor(E[:, par, tt], E[:, par, tt],
                                               Rz[:, tt, :].unsqueeze(1).broadcast_to([P, B, P]),
                                               ALU.mult).then_inc(weights_done, 1)
                    loop(pool, do)

                @block.scalar
                def _(act):
                    for n in range(4):
                        act.wait_ge(xt_full, n + 1)
                        act.activation(xT[:, 2 * n:2 * n + 2, :],
                                       L[:].rearrange("p t b n -> p (t b n)")[:, 512 * n:512 * n + 512]
                                       .rearrange("p (b m) -> p b m", b=2), ACT.Copy).then_inc(xt_done, 1)

                    def exps(c, par):
                        for tt in range(TT):
                            act.wait_ge(shifted, c * 2 + (tt + 1))
                            act.activation(E[:, par, tt], E[:, par, tt], ACT.Exp).then_inc(exp_done, 1)

                    exps(0, 0)

                    def do(c, par, more, before):
                        if more:
                            exps(c + 1, 1 - par)
                        act.wait_ge(st_full, c + 1)
                        if before:
                            act.wait_ge(y_full, c + 1)
                        act.activation(slots[:], ST[:], ACT.Copy).then_inc(st_done, 1)
                    loop(act, do)
                    act.wait_ge(rt_full, 1)
                    act.activation(RT[:, :], L[0:TT * B, 0, 0, :], ACT.Copy, scale=-1.0).then_inc(rt_done, 1)

                @block.vector
                def _(dve):
                    ch = Chain(dve, chain)
                    ch.per = 2 * 4

                    def shift(c, par):
                        for tt in range(TT):
                            dve.wait_ge(l_full, c * 2 + (tt + 1))
                            src = L[:, tt]
                            dve.tensor_reduce(pm[:, tt, :, c] if isinstance(c, int)
                                              else pm[:, tt, :, bass.ds(c, 1)].squeeze(2),
                                              src, AX.X, ALU.max)
                            ch.link(dve.tensor_reduce(M[:, tt, :], src.rearrange("p b n -> p n b"), AX.X, ALU.max))
                            dve.tensor_tensor(E[:, par, tt], src, M[:, tt, :].unsqueeze(1).broadcast_to([P, B, P]),
                                              ALU.subtract).then_inc(shifted, 1)

                    shift(0, 0)
                    dve.wait_ge(w_in[1], 16)

                    def evacuate(c):
                        dve.wait_ge(y_full, c + 2)
                        if isinstance(c, int):
                            dst, bias = yall[:, c, :, 0:D], eb[:, c, :]
                        else:
                            dst, bias = yall[:, bass.ds(c, 1), :, 0:D].squeeze(1), eb[:, bass.ds(c, 1), :].squeeze(1)
                        dve.tensor_tensor(dst, Y[:], bias.unsqueeze(1).broadcast_to([P, B, D]),
                                          ALU.add).then_inc(y_done, 1)

                    def do(c, par, more, before):
                        for tt in range(TT):
                            dve.wait_ge(exp_done, c * 2 + (tt + 1))
                            ch.link(dve.tensor_reduce(Zs[:, tt, :], E[:, par, tt].rearrange("p b n -> p n b"),
                                                      AX.X, ALU.add))
                            if before:
                                dve.wait_ge(weights_done, c * 2 + (tt - 1))
                            dve.reciprocal(Rz[:, tt, :], Zs[:, tt, :]).then_inc(rz_done, 1)
                        if more:
                            if before:
                                dve.wait_ge(st_full, c)
                            shift(c + 1, 1 - par)
                        if before:
                            evacuate(c - 1)
                    loop(dve, do, ch)
                    evacuate(CH - 1)
                    dve.tensor_reduce(R[:], pm[:], AX.X, ALU.max).then_inc(r_done, 1)

                @block.tensor
                def _(pe):
                    pe.wait_ge(w_in[0], 32)
                    flat = L[:].rearrange("p t b n -> p (t b n)")
                    for n in range(4):
                        for k in range(4):
                            mm = pe.transpose(flat[:, 512 * n + P * k:512 * n + P * k + P],
                                              x_all[:, 4 * n + k, :], ident[:, :])
                        mm.then_inc(xt_full, 1)
                    pe.wait_ge(xt_done, 4)

                    def logits(c, before):
                        cols = slice(c * P, c * P + P) if isinstance(c, int) else bass.ds(c * P, P)
                        for tt in range(TT):
                            if before:
                                pe.wait_ge(shifted, c * 2 + (tt - 1))
                            for b in range(B):
                                mm = pe.matmul(L[:, tt, b, :], xT[:, b, tt * P:(tt + 1) * P], phi[:, cols],
                                               start=True, stop=True)
                            mm.then_inc(l_full, 1)

                    logits(0, False)

                    def do(c, par, more, before):
                        if more:
                            logits(c + 1, True)
                        pe.wait_ge(weights_done, c * 2 + 2)
                        if before:
                            pe.wait_ge(st_done, c)
                        for b in range(B):
                            for tt in range(TT):
                                mm = pe.matmul(ST[:, b, :], x_all[:, 2 * b + tt, :], E[:, par, tt, b, :],
                                               start=tt == 0, stop=tt == TT - 1)
                        mm.then_inc(st_full, 1)
                        pe.wait_ge(st_done, c + 1)
                        if before:
                            pe.wait_ge(y_done, c)
                        pe.wait_ge(e_in[par], 16 * (c // 2 + 1) if isinstance(c, int) else c * 8 + (16 - 8 * par))
                        for b in range(B):
                            for n in range(EC):
                                mm = pe.matmul(Y[NP_ * n:NP_ * n + NP_, b, :], slots[:, b, NP_ * n:NP_ * n + NP_],
                                               We[par][:, n, :], start=True, stop=True, skip_group_check=True)
                        mm.then_inc(y_full, 1)
                    loop(pe, do)
                    pe.wait_ge(r_done, 1)
                    pe.transpose(L[0:TT * B, 0, 0, :], R[:].rearrange("p t b -> p (t b)"),
                                 ident[:, :]).then_inc(rt_full, 1)

        with ExitStack() as ctx:
            sc = Scope(nc, ctx, "c2")
            CE = sc.sb("CE", [P, NQ, QT, S])
            onesb = sc.sb("onesb", [P, P], BF16)
            rz = sc.sb("rz", [P, TT])
            nt = NormTiles(sc)
            LT = sc.ps("LT", [P, 2, QT, S])
            O = sc.ps("O", [P, TT, D + 1])
            consts = sc.sem("consts")
            l_full, exp_done, used = sc.sem("l_full"), sc.sem("exp_done"), sc.sem("used")
            o_done = sc.sem("o_done")
            rz_done, ve_done, rstd_done, x_done = (sc.sem(n) for n in ("rz_done", "ve_done", "rstd_done", "x_done"))
            chain, spare = sc.sem("chain"), sc.sem("spare")
            with nc.Block() as block:

                @block.gpsimd
                def _(pool):
                    pool.memset(onesb[:, :], 1.0).then_inc(consts, 1)
                    pool.memset(nt.half[:, :], -0.5).then_inc(consts, 1)
                    pool.wait_ge(consts, 2)
                    pool.sem_inc(exp_done, 2)
                    pool.sem_inc(used, NQ)
                    pool.sem_inc(o_done, 2)
                    with pool.Fori(0, B) as b:
                        pool.wait_ge(ve_done, b + 1)
                        pool.tensor_tensor(nt.rstd[:, :], nt.ve[:, :], nt.half[:, :], ALU.pow).then_inc(rstd_done, 1)

                @block.scalar
                def _(act):
                    with act.Fori(0, B) as b:
                        for q in range(NQ):
                            act.wait_ge(l_full, b * NQ + (q + 1))
                            act.wait_ge(used, b * NQ + (q + 1))
                            act.activation(CE[:, q], LT[:, q % 2], ACT.Exp).then_inc(exp_done, 1)

                @block.vector
                def _(dve):
                    ch = Chain(dve, chain)
                    dve.wait_ge(consts, 2)
                    with dve.Fori(0, B) as b:
                        ch.off = b * 3
                        dve.wait_ge(used, b * NQ + 2 * NQ)
                        ch.link(dve.reciprocal(rz[:, :], O[:, :, D]))
                        for tt in range(TT):
                            xt = x_all[:, bass.ds(b * 2 + tt, 1), :].squeeze(1)
                            dve.scalar_tensor_tensor(nt.r[:, tt, :], O[:, tt, 0:D], rz[:, tt:tt + 1], xt,
                                                     ALU.mult, ALU.add).then_inc(o_done, 1)
                        dve.wait_ge(o_done, b * 2 + 4)
                        settle(dve, spare)
                        norm_stats(dve, ch.link, nt, ve_done, spare)
                        dve.wait_ge(rstd_done, b + 1)
                        for tt in range(TT):
                            norm_apply(dve, nt, x_all[:, bass.ds(b * 2 + tt, 1), :].squeeze(1), tt)\
                                .then_inc(x_done, 1)

                @block.tensor
                def _(pe):
                    pe.wait_ge(consts, 2)
                    with pe.Fori(0, B) as b:
                        xb = xT[:, bass.ds(b, 1), :].squeeze(1)
                        rb = rows[:, bass.ds(b, 1), :].broadcast_to([P, 2, S])

                        def logits(q):
                            pe.wait_ge(exp_done, b * NQ + (q + 1))
                            for bank in range(2):
                                for n in range(2):
                                    t = QT * q + 2 * bank + n
                                    pe.matmul(LT[:, q % 2, 2 * bank + n, :], phi[:, t * P:(t + 1) * P], xb,
                                              start=n == 0, stop=False, skip_group_check=True)
                                mm = pe.matmul(LT[:, q % 2, 2 * bank:2 * bank + 2, :], onesb[:, :], rb,
                                               start=False, stop=True, skip_group_check=True)
                            mm.then_inc(l_full, 1)

                        def outputs(q):
                            pe.wait_ge(exp_done, b * NQ + (q + 3))
                            if q == 0:
                                pe.wait_ge(o_done, b * 2 + 2)
                            for n in range(QT):
                                t = QT * q + n
                                for tt in range(TT):
                                    mm = pe.matmul(O[:, tt, :], CE[:, q, n, tt * P:(tt + 1) * P],
                                                   yall[:, t, bass.ds(b, 1), :].squeeze(1),
                                                   start=t == 0 and tt == 0, stop=t == CH - 1, skip_group_check=True)
                            mm.then_inc(used, 1)

                        for q in range(NQ):
                            logits(q)
                            if q >= 1:
                                outputs(q - 1)
                        outputs(NQ - 1)


def mlstm(nc, x_all, w):
    NH, DQ, DV = 8, 8, 16
    BH = B * NH
    CAP = 15.0
    EPS_H = 1e-6
    NGA = NH // GJ
    VC = 32
    with ExitStack() as outer:
        so = Scope(nc, outer, "a")
        bT = so.sb("bT", [P, TT, BH])
        emT = so.sb("emT", [P, TT, BH])
        ident = so.sb("ident", [P, P])
        g_dram = nc.dram_tensor("a_g", (BH, S), F32).ap()

        with ExitStack() as ctx:
            sc = Scope(nc, ctx, "a1")
            xT = sc.sb("xT", [P, B, S])
            wg = sc.sb("wg", [P, 2, B, BH])
            gb = sc.sb("gb", [BH, 2])
            pre = sc.sb("pre", [BH, 2, S])
            gate = sc.sb("gate", [BH, 2, S])
            zero = sc.sb("zero", [BH, S])
            F = sc.sb("F", [BH, S])
            bg = sc.sb("bg", [BH, S])
            g = sc.sb("g", [BH, S])
            m = sc.sb("m", [BH, S])
            em = sc.sb("em", [BH, S])
            G = sc.ps("G", [BH, 2, 512])
            T = sc.ps("T", [P, 2, TT, BH])
            w_in, x_in, g_full, pre_done, tanh_done, chain, g_done, m_done, em_done, t_full, t_done, g_out, consts = (
                sc.sem(n) for n in ("w_in", "x_in", "g_full", "pre_done", "tanh_done", "chain", "g_done", "m_done",
                                    "em_done", "t_full", "t_done", "g_out", "consts"))
            with nc.Block() as block:

                @block.sync
                def _(sp):
                    sp.dma_start(wg[:], w["a_wg"]).then_inc(w_in, 16)
                    sp.dma_start(gb[:, :], w["a_gb"]).then_inc(w_in, 16)
                    sp.dma_start(ident[:, :], w["ident"]).then_inc(w_in, 16)
                    sp.dma_start(xT[:], w["xT"].rearrange("b d n -> d b n")).then_inc(w_in, 16)
                    sp.dma_start(x_all[:], w["x"]).then_inc(x_in, 16)
                    sp.wait_ge(g_done, 1)
                    sp.dma_start(g_dram, g[:, :]).then_inc(g_out, 16)
                    sp.wait_ge(g_out, 16)
                    sp.wait_ge(x_in, 16)

                @block.tensor
                def _(pe):
                    pe.wait_ge(w_in, 64)
                    for k in range(2):
                        for b in range(B):
                            mm = pe.matmul(G[:, k, 0:S], wg[:, k, b, :], xT[:, b, :], start=b == 0, stop=b == B - 1)
                    mm.then_inc(g_full, 1)
                    pe.wait_ge(g_done, 1)
                    for tt in range(TT):
                        mm = pe.transpose(T[:, 0, tt, :], bg[:, tt * P:(tt + 1) * P], ident[0:BH, 0:BH])
                    pe.wait_ge(em_done, 1)
                    for tt in range(TT):
                        mm = pe.transpose(T[:, 1, tt, :], em[:, tt * P:(tt + 1) * P], ident[0:BH, 0:BH])
                    mm.then_inc(t_full, 1)

                @block.vector
                def _(dve):
                    ch = Chain(dve, chain)
                    ch.link(dve.memset(zero[:, :], 0.0))
                    dve.wait_ge(w_in, 64)
                    dve.wait_ge(g_full, 1)
                    for k in range(2):
                        dve.tensor_scalar(pre[:, k, :], G[:, k, 0:S], gb[:, k:k + 1], 1.0 / CAP, ALU.add,
                                          ALU.mult).then_inc(pre_done, 1)
                    dve.wait_ge(tanh_done, 1)
                    ch.link(dve.tensor_scalar(gate[:], gate[:], CAP, None, ALU.mult))
                    ch.link(dve.tensor_tensor_scan(F[:, :], gate[:, 1, :], zero[:, :], 0.0, ALU.add, ALU.add))
                    ch.link(dve.tensor_tensor(bg[:, :], gate[:, 0, :], F[:, :], ALU.subtract))
                    dve.tensor_tensor_scan(g[:, :], bg[:, :], bg[:, :], 0.0, ALU.max, ALU.max).then_inc(g_done, 1)
                    dve.wait_ge(g_done, 1)
                    dve.tensor_tensor(m[:, :], g[:, :], F[:, :], ALU.add).then_inc(m_done, 1)
                    dve.wait_ge(t_full, 1)
                    dve.tensor_copy(bT[:], T[:, 0]).then_inc(t_done, 1)
                    dve.tensor_copy(emT[:], T[:, 1]).then_inc(t_done, 1)

                @block.scalar
                def _(act):
                    act.wait_ge(pre_done, 2)
                    act.activation(gate[:], pre[:], ACT.Tanh).then_inc(tanh_done, 1)
                    act.wait_ge(m_done, 1)
                    act.activation(em[:, :], m[:, :], ACT.Exp, scale=-1.0).then_inc(em_done, 1)

        with ExitStack() as ctx:
            sc = Scope(nc, ctx, "a2")
            wq, wk = sc.sb("wq", [P, NGA, P]), sc.sb("wk", [P, NGA, P])
            wvo = sc.sb("wvo", [P, 2 * D])
            wout = sc.sb("wout", [P, D])
            lnw, lnb = sc.sb("lnw", [P, D]), sc.sb("lnb", [P, D])
            mask = sc.sb("mask", [P, S])
            xT = sc.sb("xT", [P, S])
            g = sc.sb("g", [P, NH, S])
            bs = sc.sb("bs", [P, TT, NH])
            q, kx = sc.sb("q", [P, NGA, S]), sc.sb("kx", [P, NGA, GJ, S])
            V = sc.sb("V", [P, TT, NH, VC])
            og = sc.sb("og", [P, TT, D])
            sg = sc.sb("sg", [P, TT, D])
            W = sc.sb("W", [P, NH, S + P])
            Os = sc.sb("Os", [P, NGA, S])
            den = sc.sb("den", [P, TT, NH])
            rden = sc.sb("rden", [P, TT, NH])
            hn = sc.sb("hn", [P, TT, D])
            hT = sc.sb("hT", [P, S])
            ht = NormTiles(sc)
            nt = NormTiles(Scope(nc, ctx, "a3"))
            X = sc.ps("X", [P, 512])
            O = sc.ps("O", [P, NGA, S])
            S0 = sc.ps("S0", [P, NH, S])
            S1 = sc.ps("S1", [P, NH, P])
            QK = S1[:].rearrange("p h n -> p (h n)").rearrange("p (t g n) -> p t g n", t=2, g=NGA)
            (w_in, x_in, consts, gt_in, x_full, x_free, qk_full, qk_done, bs_done, s_full, arg_done, w_done, p_done,
             pv_full, pv_free, chain, xg_done, h_ve, h_rstd, h_done, ve_done, rstd_done, x_done, spare, og_done,
             hT_done) = (sc.sem(n) for n in (
                 "w_in", "x_in", "consts", "gt_in", "x_full", "x_free", "qk_full", "qk_done", "bs_done", "s_full",
                 "arg_done", "w_done", "p_done", "pv_full", "pv_free", "chain", "xg_done", "h_ve", "h_rstd",
                 "h_done", "ve_done", "rstd_done", "x_done", "spare", "og_done", "hT_done"))
            loads = [(wq, w["a_wq"]), (wk, w["a_wk"]), (wvo, w["a_wvo"]), (wout, w["a_wout"]),
                     (lnw, w["a_lnw"].partition_broadcast(P)), (lnb, w["a_lnb"].partition_broadcast(P)),
                     (mask, w["a_mask"])]

            def uses(b, last):
                return (None, b * 4 + 2, b * 4 + 3, b * 4 + 4) if last else \
                    (b * 4 + 2, b * 4 + 3, b * 4 + 4, b * 4 + 5)

            def loop(eng, early, late, chain=None):
                early(0, 1)
                n = chain.n if chain else 0
                with eng.Fori(0, B - 1) as b:
                    if chain:
                        chain.off = b * chain.per
                    u = uses(b, False)
                    late(b, None, 0)
                    early(b + 1, u[0])
                    late(b, u, 1)
                if chain:
                    assert chain.n - n == chain.per, chain.n - n
                    chain.off, chain.n = 0, n + (B - 1) * chain.per
                late(B - 1, None, 0)
                late(B - 1, uses(B - 1, True), 1)

            def tiles(b, tt=0, n=1):
                return slice(2 * b + tt, 2 * b + tt + n) if isinstance(b, int) else bass.ds(b * 2 + tt, n)

            with nc.Block() as block:

                @block.sync
                def _(sp):
                    for dst, src in loads:
                        sp.dma_start(dst[:], src).then_inc(w_in, 16)

                    def early(b, _):
                        if not isinstance(b, int):
                            sp.wait_ge(s_full, b)
                            settle(sp, spare)
                            sp.wait_ge(arg_done, b * 2)
                            settle(sp, spare)
                        sp.dma_start(xT[:, :], w["xT"][b]).then_inc(x_in, 16)
                        rows = slice(0, NH) if isinstance(b, int) else bass.ds(b * NH, NH)
                        sp.dma_start(g[:], g_dram[rows, :].unsqueeze(0).broadcast_to([P, NH, S])).then_inc(gt_in, 16)
                    loop(sp, early, lambda *a: None)

                @block.gpsimd
                def _(pool):
                    pool.sem_inc(h_done, 1)
                    pool.sem_inc(pv_free, 1)
                    pool.memset(kx[:], 0.0).then_inc(consts, 1)
                    pool.memset(V[:], 0.0).then_inc(consts, 1)
                    pool.wait_ge(consts, 2)
                    pool.memset(V[:, :, :, DV:DV + 1], 1.0).then_inc(consts, 1)
                    pool.memset(ht.half[:, :], -0.5).then_inc(consts, 1)
                    pool.memset(nt.half[:, :], -0.5).then_inc(consts, 1)
                    pool.wait_ge(consts, 5)

                    def late(b, u, part):
                        if part == 1:
                            pool.wait_ge(h_ve, b + 1)
                            pool.tensor_tensor(ht.rstd[:, :], ht.ve[:, :], ht.half[:, :], ALU.pow).then_inc(h_rstd, 1)
                            pool.wait_ge(ve_done, b + 1)
                            pool.tensor_tensor(nt.rstd[:, :], nt.ve[:, :], nt.half[:, :], ALU.pow)\
                                .then_inc(rstd_done, 1)
                    loop(pool, lambda *a: None, late)

                @block.scalar
                def _(act):
                    act.wait_ge(consts, 5)

                    def early(b, use):
                        for t in range(2):
                            act.wait_ge(qk_full, b * 2 + t + 1)
                            if t == 0 and not isinstance(b, int):
                                act.wait_ge(s_full, b)
                            if t == 0:
                                act.activation(q[:], QK[:, t], ACT.Copy).then_inc(qk_done, 1)
                            else:
                                for j in range(GJ):
                                    rows = slice(32 * j, 32 * j + 32)
                                    act.activation(kx[rows, :, j, :], QK[rows, t], ACT.Copy).then_inc(qk_done, 1)
                        for kt in range(TT):
                            act.wait_ge(arg_done, b * 2 + kt + 1)
                            cols = slice(0, S) if kt == 0 else slice(S, S + P)
                            act.activation(W[:, :, cols], W[:, :, cols], ACT.Exp, scale=-1.0).then_inc(w_done, 1)

                    def late(b, u, part):
                        if part == 0:
                            act.wait_ge(p_done, b * 2 + 1)
                            act.wait_ge(h_done, b + 1)
                            act.activation(sg[:], og[:], ACT.Tanh, scale=0.5).then_inc(og_done, 1)
                            return
                        act.wait_ge(pv_full, b + 1)
                        act.activation(Os[:], O[:], ACT.Copy).then_inc(pv_free, 1)
                        act.wait_ge(x_full, u[2])
                        act.activation(hT[:, :], X[:, 0:S], ACT.Copy, scale=0.5).then_inc(x_free, 1)
                    loop(act, early, late)

                @block.vector
                def _(dve):
                    dve.wait_ge(w_in, 16 * len(loads))
                    dve.wait_ge(consts, 5)
                    ch = Chain(dve, chain)
                    ch.per = CHAIN_A

                    def early(b, use):
                        rows = slice(NH * b, NH * b + NH) if isinstance(b, int) else bass.ds(b * NH, NH)
                        ch.link(dve.tensor_copy(bs[:], bT[:, :, rows]))
                        dve.wait_ge(gt_in, (b + 1) * 16)
                        if not isinstance(b, int):
                            dve.wait_ge(pv_full, b)
                        for kt in range(TT):
                            for h in range(NH):
                                cols = slice(0, S) if kt == 0 else slice(S, S + P)
                                gs = g[:, h, 0:S] if kt == 0 else g[:, h, P:S]
                                ins = dve.scalar_tensor_tensor(W[:, h, cols], gs, bs[:, kt, h:h + 1],
                                                               mask[:, 0:S] if kt == 0 else mask[:, 0:P],
                                                               ALU.subtract, ALU.add)
                            ins.then_inc(arg_done, 1)
                        dve.wait_ge(x_full, use)
                        if not isinstance(b, int):
                            dve.wait_ge(og_done, b)
                        vo = X[:, :].rearrange("p (t n) -> p t n", t=TT)
                        for tt in range(TT):
                            dve.tensor_copy(V[:, tt, :, 0:DV], vo[:, tt, 0:D].rearrange("p (h d) -> p h d", h=NH))
                        dve.tensor_copy(og[:], vo[:, :, D:2 * D]).then_inc(x_free, 1)
                        dve.wait_ge(s_full, b + 1)
                        for kt in range(TT):
                            dve.wait_ge(w_done, b * 2 + kt + 1)
                            cols = slice(0, S) if kt == 0 else slice(S, S + P)
                            dve.scalar_tensor_tensor(W[:, :, cols], S0[:] if kt == 0 else S1[:],
                                                     float(DQ) ** -0.5, W[:, :, cols], ALU.mult,
                                                     ALU.mult).then_inc(p_done, 1)

                    def late(b, u, part):
                        if part == 0:
                            return
                        rows = slice(NH * b, NH * b + NH) if isinstance(b, int) else bass.ds(b * NH, NH)
                        dve.wait_ge(x_full, u[1])
                        o = X[:, :].rearrange("p (t h v) -> p t h v", t=TT, h=NH)
                        ch.link(dve.tensor_tensor(den[:], o[:, :, :, DV], emT[:, :, rows], ALU.max))
                        ch.link(dve.scalar_tensor_tensor(den[:], o[:, :, :, DV], -1.0, den[:], ALU.mult, ALU.max))
                        ch.link(dve.tensor_scalar(den[:], den[:], 1e-6, None, ALU.add))
                        ch.link(dve.reciprocal(rden[:], den[:]))
                        for tt in range(TT):
                            ins = dve.tensor_tensor(ht.r[:, tt, :].rearrange("p (h v) -> p h v", h=NH),
                                                    o[:, tt, :, 0:DV],
                                                    rden[:, tt, :].unsqueeze(2).broadcast_to([P, NH, DV]), ALU.mult)
                        ins.then_inc(x_free, 1)
                        dve.wait_ge(x_free, u[1])
                        settle(dve, spare)
                        norm_stats(dve, ch.link, ht, h_ve, spare, EPS_H)
                        dve.wait_ge(h_rstd, b + 1)
                        for tt in range(TT):
                            ins = norm_apply(dve, ht, hn[:, tt, :], tt)
                        ch.link(ins)
                        ch.link(dve.tensor_tensor(hn[:], hn[:], lnw[:, :].unsqueeze(1).broadcast_to([P, TT, D]),
                                                  ALU.mult))
                        ch.link(dve.tensor_tensor(hn[:], hn[:], lnb[:, :].unsqueeze(1).broadcast_to([P, TT, D]),
                                                  ALU.add))
                        dve.wait_ge(og_done, b + 1)
                        dve.scalar_tensor_tensor(hn[:], sg[:], 1.0, hn[:], ALU.add, ALU.mult).then_inc(h_done, 1)
                        dve.wait_ge(x_full, u[3])
                        y = X[:, 0:TT * D].rearrange("p (t d) -> p t d", t=TT)
                        dve.tensor_tensor(nt.r[:], y, x_all[:, tiles(b, 0, 2), :], ALU.add).then_inc(x_free, 1)
                        dve.wait_ge(x_free, u[3])
                        settle(dve, spare)
                        norm_stats(dve, ch.link, nt, ve_done, spare)
                        dve.wait_ge(rstd_done, b + 1)
                        for tt in range(TT):
                            norm_apply(dve, nt, x_all[:, tiles(b, tt), :].squeeze(1), tt).then_inc(x_done, 1)
                    loop(dve, early, late, ch)

                @block.tensor
                def _(pe):
                    pe.wait_ge(w_in, 16 * len(loads))
                    pe.wait_ge(consts, 5)

                    def early(b, use):
                        pe.wait_ge(x_in, (b + 1) * 16)
                        pe.wait_ge(x_free, use - 1)
                        for tt in range(TT):
                            mm = pe.matmul(X[:, tt * 2 * D:(tt + 1) * 2 * D], xT[:, tt * P:(tt + 1) * P], wvo[:, :],
                                           start=True, stop=True)
                        mm.then_inc(x_full, 1)
                        if not isinstance(b, int):
                            pe.wait_ge(p_done, b * 2)
                        for t, wt in enumerate((wq, wk)):
                            for gg in range(NGA):
                                mm = pe.matmul(QK[:, t, gg, :], wt[:, gg, :], xT[:, :], start=True, stop=True)
                            mm.then_inc(qk_full, 1)
                        pe.wait_ge(qk_done, b * 5 + 5)
                        for h in range(NH):
                            gg, j = h // GJ, h % GJ
                            pe.matmul(S0[:, h, :], kx[:, gg, j, 0:P], q[:, gg, :], start=True, stop=True)
                            mm = pe.matmul(S1[:, h, :], kx[:, gg, j, P:S], q[:, gg, P:S], start=True, stop=True)
                        mm.then_inc(s_full, 1)

                    def late(b, u, part):
                        if part == 0:
                            pe.wait_ge(p_done, b * 2 + 2)
                            pe.wait_ge(pv_free, b + 1)
                            for gg in range(NGA):
                                for kt in range(TT):
                                    for j in range(GJ):
                                        h = GJ * gg + j
                                        src = W[:, h, 0:S] if kt == 0 else W[:, h, S:S + P]
                                        mm = pe.matmul(O[32 * j:32 * j + 32, gg, kt * P:S], V[:, kt, h, :], src,
                                                       start=kt == 0, stop=kt == 1, skip_group_check=True)
                            mm.then_inc(pv_full, 1)
                            return
                        pe.wait_ge(pv_free, b + 2)
                        pe.wait_ge(x_free, u[1] - 1)
                        for tt in range(TT):
                            for gg in range(NGA):
                                mm = pe.transpose(X[:, (tt * NGA + gg) * P:(tt * NGA + gg + 1) * P],
                                                  Os[:, gg, tt * P:(tt + 1) * P], ident[:, :])
                        mm.then_inc(x_full, 1)
                        pe.wait_ge(h_done, b + 2)
                        for tt in range(TT):
                            mm = pe.transpose(X[:, tt * P:(tt + 1) * P], hn[:, tt, :], ident[:, :])
                        mm.then_inc(x_full, 1)
                        pe.wait_ge(x_free, u[2])
                        for tt in range(TT):
                            mm = pe.matmul(X[:, tt * D:(tt + 1) * D], hT[:, tt * P:(tt + 1) * P], wout[:, :],
                                           start=True, stop=True)
                        mm.then_inc(x_full, 1)
                    loop(pe, early, late)


CHAIN_A = 12


def ffn(nc, x_all, w, out):
    HID, RANK = 512, 16
    HC = HID // P
    with ExitStack() as ctx:
        sc = Scope(nc, ctx, "f")
        wf = sc.sb("wf", [P, HC, D])
        wp = sc.sb("wp", [P, HID])
        bf_, v = sc.sb("fast_bT", [RANK, RANK]), sc.sb("v", [RANK, D])
        uT = sc.sb("uT", [RANK, HID])
        gate = sc.sb("gate", [P, 1])
        ident = sc.sb("ident", [P, P])
        tmp = sc.sb("tmp", [P, HC, D])
        tern = sc.sb("tern", [P, HC, D])
        scf, scp = sc.sb("scf", [P, HC]), sc.sb("scp", [P, 1])
        half, nhalf = sc.sb("edge", [P, HC]), sc.sb("nedge", [P, HC])
        bv = sc.sb("bv", [RANK, D])
        A1 = sc.sb("A1", [P, HC, D])
        A2 = sc.sb("A2", [P, HC, D])
        A1T = sc.sb("A1T", [P, HC, P])
        A2T = sc.sb("A2T", [P, HC, D])
        xb = sc.sb("xb", [P, TT, D])
        xT = sc.sb("xT", [P, S])
        rl = sc.sb("rl", [P, HC, S])
        r2 = sc.sb("r2", [P, HC, S])
        y = sc.sb("y", [P, TT, D])
        nt = NormTiles(sc)
        XT = sc.ps("XT", [P, 512])
        HT = sc.ps("HT", [P, HC, S])
        Y = sc.ps("Y", [P, 512])
        WT = sc.ps("WT", [P, 2, HC, P])
        (w_in, chain, consts, bv_full, bv_done, um_full, a1_done, a2_done, wt_full, wt_done, xb_done, xt_full, xt_done,
         h_full, rl_done, r2_done, y_full, y_free, ve_done, rstd_done, n_done, out_done, spare) = (
            sc.sem(n) for n in ("w_in", "chain", "consts", "bv_full", "bv_done", "um_full", "a1_done", "a2_done",
                                "wt_full", "wt_done", "xb_done", "xt_full", "xt_done", "h_full", "rl_done",
                                "r2_done", "y_full", "y_free", "ve_done", "rstd_done", "n_done", "out_done", "spare"))
        loads = [(wf, w["f_wfc"]), (wp, w["f_wproj"]), (bf_, w["f_fast_bT"]), (v, w["f_v"]), (uT, w["f_uT"]),
                 (gate, w["f_gate"].partition_broadcast(P)), (ident, w["ident"])]

        def tiles(b, tt=0, n=1):
            return slice(2 * b + tt, 2 * b + tt + n) if isinstance(b, int) else bass.ds(b * 2 + tt, n)

        def loop(eng, early, late, chain=None):
            early(0)
            n = chain.n if chain else 0
            with eng.Fori(0, B - 1) as b:
                if chain:
                    chain.off = b * chain.per
                early(b + 1)
                late(b)
            if chain:
                assert chain.n - n == chain.per, chain.n - n
                chain.off, chain.n = 0, n + (B - 1) * chain.per
            late(B - 1)

        with nc.Block() as block:

            @block.sync
            def _(sp):
                for dst, src in loads:
                    sp.dma_start(dst[:], src).then_inc(w_in, 16)

                def late(b):
                    sp.wait_ge(n_done, b * 2 + 4)
                    settle(sp, spare)
                    sp.dma_start(out[b].rearrange("(t p) d -> p t d", p=P), y[:]).then_inc(out_done, 16)
                loop(sp, lambda b: None, late)
                sp.wait_ge(out_done, 16 * B + 16)

            @block.gpsimd
            def _(pool):
                for s, n in ((n_done, 2), (out_done, 16), (y_free, 1)):
                    pool.sem_inc(s, n)
                pool.memset(nt.half[:, :], -0.5).then_inc(consts, 1)
                pool.wait_ge(consts, 1)

                def early(b):
                    if not isinstance(b, int):
                        pool.wait_ge(xt_full, b)
                        settle(pool, spare)
                    pool.tensor_copy(xb[:], x_all[:, tiles(b, 0, 2), :]).then_inc(xb_done, 1)

                def late(b):
                    pool.wait_ge(ve_done, b + 1)
                    pool.tensor_tensor(nt.rstd[:, :], nt.ve[:, :], nt.half[:, :], ALU.pow).then_inc(rstd_done, 1)
                loop(pool, early, late)

            @block.scalar
            def _(act):
                act.wait_ge(bv_full, 1)
                act.activation(bv[:, :], XT[0:RANK, 0:D], ACT.Copy).then_inc(bv_done, 1)
                for n, (dst, width) in enumerate(((A1T, P), (A2T, D))):
                    act.wait_ge(wt_full, n + 1)
                    act.activation(dst[:], WT[:, n], ACT.Copy).then_inc(wt_done, 1)

                def early(b):
                    act.wait_ge(xt_full, b + 1)
                    if not isinstance(b, int):
                        act.wait_ge(h_full, b)
                    act.activation(xT[:, :], XT[:, 0:S], ACT.Copy).then_inc(xt_done, 1)
                    act.wait_ge(h_full, b + 1)
                    if not isinstance(b, int):
                        act.wait_ge(r2_done, b)
                    act.activation(rl[:], HT[:], ACT.Relu).then_inc(rl_done, 1)
                loop(act, early, lambda b: None)

            @block.vector
            def _(dve):
                ch = Chain(dve, chain)
                ch.per = 2
                dve.wait_ge(w_in, 16 * len(loads))
                wpt = wp[:, :].rearrange("p (c d) -> p c d", c=HC)

                def ternary(wt, scale, dst, tiles_):
                    ch.link(dve.scalar_tensor_tensor(tmp[:], wt, -1.0, wt, ALU.mult, ALU.max))
                    src = tmp[:] if tiles_ == HC else tmp[:].rearrange("p c d -> p (c d)").unsqueeze(1)
                    ch.link(dve.tensor_reduce(scale[:, :], src, AX.X, ALU.add))
                    ch.link(dve.tensor_scalar(scale[:, :], scale[:, :], tiles_ / float(HID), 1e-5, ALU.mult, ALU.max))
                    wide = scale[:, :].unsqueeze(2).broadcast_to([P, HC, D]) if tiles_ == HC else \
                        scale[:, :].unsqueeze(2).broadcast_to([P, HC, D])
                    ch.link(dve.tensor_scalar(half[:, 0:tiles_], scale[:, :], 0.5, None, ALU.mult))
                    ch.link(dve.tensor_scalar(nhalf[:, 0:tiles_], scale[:, :], -0.5, None, ALU.mult))
                    edge = half[:, 0:tiles_].unsqueeze(2).broadcast_to([P, HC, D])
                    ch.link(dve.tensor_tensor(tern[:], wt, edge, ALU.is_gt))
                    ch.link(dve.tensor_tensor(tmp[:], wt, nhalf[:, 0:tiles_].unsqueeze(2).broadcast_to([P, HC, D]), ALU.is_lt))
                    ch.link(dve.tensor_tensor(tern[:], tern[:], tmp[:], ALU.subtract))
                    ch.link(dve.tensor_tensor(tern[:], tern[:], wt, ALU.subtract))
                    ch.link(dve.tensor_tensor(tern[:], tern[:], wt, ALU.add))
                    return dve.tensor_tensor(dst[:], tern[:], wide, ALU.mult)

                ternary(wpt, scp, A2, 1).then_inc(a2_done, 1)
                dve.wait_ge(a2_done, 1)
                ch.link(ternary(wf[:], scf, A1, HC))
                dve.wait_ge(um_full, 1)
                um = HT[:, 0:2, :].rearrange("p a n -> p (a n)").rearrange("p (c d) -> p c d", c=HC)
                dve.scalar_tensor_tensor(A1[:], um, gate[:, 0:1], A1[:], ALU.mult, ALU.add).then_inc(a1_done, 1)

                def early(b):
                    dve.wait_ge(rl_done, b + 1)
                    if not isinstance(b, int):
                        dve.wait_ge(y_full, b)
                    dve.scalar_tensor_tensor(r2[:], HT[:], 0.0, rl[:], ALU.max, ALU.mult).then_inc(r2_done, 1)

                def late(b):
                    dve.wait_ge(y_full, b + 1)
                    dve.wait_ge(n_done, b * 2 + 2)
                    dve.tensor_tensor(nt.r[:], Y[:, 0:TT * D].rearrange("p (t d) -> p t d", t=TT),
                                      x_all[:, tiles(b, 0, 2), :], ALU.add).then_inc(y_free, 1)
                    dve.wait_ge(y_free, b + 2)
                    settle(dve, spare)
                    norm_stats(dve, ch.link, nt, ve_done, spare)
                    dve.wait_ge(rstd_done, b + 1)
                    dve.wait_ge(out_done, b * 16 + 16)
                    for tt in range(TT):
                        norm_apply(dve, nt, y[:, tt, :], tt).then_inc(n_done, 1)
                loop(dve, early, late, ch)

            @block.tensor
            def _(pe):
                pe.wait_ge(w_in, 16 * len(loads))
                pe.matmul(XT[0:RANK, 0:D], bf_[:, :], v[:, :], start=True, stop=True).then_inc(bv_full, 1)
                pe.wait_ge(bv_done, 1)
                um = HT[:, 0:2, :].rearrange("p a n -> p (a n)")
                for c in range(HC):
                    mm = pe.matmul(um[:, c * D:(c + 1) * D], uT[:, c * P:(c + 1) * P], bv[:, :], start=True, stop=True)
                mm.then_inc(um_full, 1)
                for n, (src, ready) in enumerate(((A1, a1_done), (A2, a2_done))):
                    pe.wait_ge(ready, 1)
                    for c in range(HC):
                        mm = pe.transpose(WT[:, n, c, :], src[:, c, :], ident[:, :])
                    mm.then_inc(wt_full, 1)
                pe.wait_ge(wt_done, 2)

                def early(b):
                    pe.wait_ge(xb_done, b + 1)
                    for tt in range(TT):
                        mm = pe.transpose(XT[:, tt * P:(tt + 1) * P], xb[:, tt, :], ident[:, :])
                    mm.then_inc(xt_full, 1)
                    pe.wait_ge(xt_done, b + 1)
                    if not isinstance(b, int):
                        pe.wait_ge(r2_done, b)
                    for c in range(HC):
                        mm = pe.matmul(HT[:, c, :], A1T[:, c, :], xT[:, :], start=True, stop=True)
                    mm.then_inc(h_full, 1)

                def late(b):
                    pe.wait_ge(r2_done, b + 1)
                    pe.wait_ge(y_free, b + 1)
                    for tt in range(TT):
                        for c in range(HC):
                            mm = pe.matmul(Y[:, tt * D:(tt + 1) * D], r2[:, c, tt * P:(tt + 1) * P], A2T[:, c, :],
                                           start=c == 0, stop=c == HC - 1)
                    mm.then_inc(y_full, 1)
                loop(pe, early, late)


def decoder(nc, w, out):
    with nc.sbuf_tensor("x_all", [P, B * TT, D], F32) as x_all:
        mlstm(nc, x_all, w)
        attention(nc, x_all, w, "b", masked=True)
        moe(nc, x_all, w)
        attention(nc, x_all, w, "d", own=True, wide=True)
        attention(nc, x_all, w, "e", causal=True)
        ffn(nc, x_all, w, out)



def lay(i):

    import numpy as np

    bf=np.dtype("bfloat16")
    f=lambda a: np.ascontiguousarray(a)
    B,S,D=8,256,128
    perm=lambda w: f(w.T.reshape(128,16,8).transpose(0,2,1).reshape(128,128))
    pcol=lambda b: f(b.reshape(16,8).T.reshape(128,1))
    def wo_n(w):
        t=w.T.reshape(4,4,8,128).transpose(1,2,0,3)
        o=np.zeros((4,32,4,128),w.dtype); o[:,:8]=t
        return o.reshape(128,4,128)
    eye=np.eye(128)
    c=np.where(np.arange(128)[None,:]>np.arange(128)[:,None],-1e30,0.0).astype(bf)
    o={
     "ctxT": f(i["ctx_1024"].transpose(0,2,1)),
     "ident": eye.astype(np.float32), "identb": eye.astype(bf),
     "ones_row": np.ones((1,16,256),bf), "zeros_row": np.zeros((1,16,256),bf),
     "causal_q": f(np.broadcast_to(c[:,None,None,:],(128,2,2,128))),
     "causal_k": f(np.broadcast_to(c.T[:,None,None,:],(128,2,2,128))),
     "b_wq": perm(i["L0_xattn_wq"]), "b_wk": perm(i["L0_xattn_wk"]), "b_wv": f(i["L0_xattn_wv"].T),
     "b_wo": wo_n(i["L0_xattn_wo"]), "b_bo": i["L0_xattn_bo"],
     "e_wq": perm(i["L1_xattn_Wq"]), "e_wk": perm(i["L1_xattn_Wk"]), "e_wv": f(i["L1_xattn_Wv"].T),
     "e_wo": wo_n(i["L1_xattn_Wo"]), "e_bo": i["L1_xattn_bo"],
     "e_bq": pcol(i["L1_xattn_bq"]), "e_bk": pcol(i["L1_xattn_bk"]), "e_bv": i["L1_xattn_bv"],
    }
    m=i["mask_1x1xSxS2_ik0"][0,0]
    o["mask"]=f(np.stack([m.reshape(2,128,256).transpose(1,0,2), m.T.reshape(2,128,256).transpose(1,0,2)],1))
    Wc=i["L1_attn_Wc"]; bc=i["L1_attn_bc"]
    o["d_wq"]=perm(Wc[:128]); o["d_wk"]=perm(Wc[128:256]); o["d_wv"]=f(Wc[256:].T)
    o["d_bq"]=pcol(bc[:128]); o["d_bk"]=pcol(bc[128:256]); o["d_bv"]=bc[256:]
    o["d_wo"]=f(i["L1_attn_Wo"].T.reshape(4,4,2,32,128).transpose(1,3,0,2,4).reshape(128,8,128))
    o["d_bo"]=i["L1_attn_bo"]
    r=np.arange(128)
    col=np.stack([((r[:,None]//32==r[None,:]//32)&(r[:,None]%32==8)&(r[None,:]%4==g)) for g in range(4)],1)
    o["collect"]=f(col.astype(np.float32))
    o["collect_wide"]=f(np.broadcast_to(np.stack([r[:32]%4==g for g in range(4)]),(128,4,32)).astype(np.float32))
    o["spread"]=f(np.stack([((r[:,None]//32==r[None,:]//32)&(r[:,None]%32==g)) for g in range(4)],1).astype(np.float32))
    x=i["x"]
    o["x"]=f(x.reshape(16,128,128).transpose(1,0,2)); o["xT"]=f(x.transpose(0,2,1))
    wg=np.zeros((128,2,8,8,8),np.float32)
    for b in range(8):
        wg[:,0,b,b]=i["L0_attn_Wi"].T; wg[:,1,b,b]=i["L0_attn_Wf"].T
    o["a_wg"]=wg.reshape(128,2,8,64)
    o["a_gb"]=f(np.stack([np.tile(i["L0_attn_bi"],8),np.tile(i["L0_attn_bf"],8)],1))
    def pad(w_):
        t=np.zeros((128,2,4,32),w_.dtype); t[...,:8]=w_.T.reshape(128,2,4,8); return t.reshape(128,2,128)
    o["a_wq"]=pad(i["L0_attn_Wq"]); o["a_wk"]=pad(i["L0_attn_Wk"])
    o["a_wvo"]=f(np.concatenate([i["L0_attn_Wv"].T,i["L0_attn_Wog"].T],1))
    o["a_wout"]=f(i["L0_attn_Wout"].T); o["a_lnw"]=i["L0_attn_ln_w"]; o["a_lnb"]=i["L0_attn_ln_b"]
    o["a_mask"]=f(np.where(np.arange(256)[None,:]<np.arange(128)[:,None],1e30,0.0).astype(np.float32))
    o["f_wfc"]=f(i["L1_ffn_w_fc"].reshape(4,128,128).transpose(1,0,2)); o["f_wproj"]=i["L1_ffn_w_proj"]
    o["f_fast_bT"]=f(i["L1_ffn_fast_b"].T); o["f_v"]=i["L1_ffn_v"]; o["f_uT"]=f(i["L1_ffn_u"].T)
    o["f_gate"]=i["L1_ffn_gate"].reshape(1)
    o["c_phi"]=f(i["L0_ffn_phi"].reshape(128,2048))
    o["c_W"]=f(i["L0_ffn_W"].transpose(1,0,2))
    o["c_b"]=f(np.broadcast_to(i["L0_ffn_b"].reshape(16,4,1,128),(16,4,32,128)).reshape(16,128,128).transpose(1,0,2))
    return o


def kernel(**inputs):
    import numpy as np
    import concourse.bacc as bacc
    from concourse.bass_utils import run_bass_kernel_spmd

    nc = bacc.Bacc("TRN2", target_bir_lowering=False, num_devices=1)
    arrays = {f"in_{k}": np.ascontiguousarray(v) for k, v in lay({k: np.asarray(v) for k, v in inputs.items()}).items()}
    w = {k[3:]: nc.dram_tensor(k, v.shape, mybir.dt.from_np(v.dtype), kind="ExternalInput").ap()
         for k, v in arrays.items()}
    out = nc.dram_tensor("out", (B, S, D), F32, kind="ExternalOutput").ap()
    decoder(nc, w, out)
    return run_bass_kernel_spmd(nc, [arrays], core_ids=[0]).results[0]["out"]
```

```python
from contextlib import ExitStack

import concourse.bass as bass
from concourse import mybir

F32 = mybir.dt.float32
BF16 = mybir.dt.bfloat16
I32 = mybir.dt.int32
ALU = mybir.AluOpType
ACT = mybir.ActivationFunctionType
AX = mybir.AxisListType

B, S, D = 8, 256, 128
P = 128
TT = S // P
EPS = 1e-5
BIG = 1e30
H, HD = 16, 8
NG, GJ = 4, 4
PARTS = 3
STACK = PARTS * PARTS * HD
SCALE = float(HD) ** -0.5


class Scope:

    def __init__(self, nc, ctx, tag):
        self.nc, self.ctx, self.tag, self.sems = nc, ctx, tag, []
        ctx.callback(self.clear)

    def sb(self, name, shape, dt=F32):
        return self.ctx.enter_context(self.nc.sbuf_tensor(f"{self.tag}_{name}", shape, dt))

    def ps(self, name, shape, dt=F32):
        return self.ctx.enter_context(self.nc.psum_tensor(f"{self.tag}_{name}", shape, dt))

    def sem(self, name):
        self.sems.append(self.nc.alloc_semaphore(f"{self.tag}_{name}"))
        return self.sems[-1]

    def clear(self):
        if self.sems:
            self.nc.all_engine_barrier()
            self.nc.clear_and_free_semaphores(self.sems)
            self.nc.all_engine_barrier()


class Chain:

    def __init__(self, eng, sem):
        self.eng, self.sem, self.n, self.off = eng, sem, 0, 0

    def link(self, ins):
        self.n += 1
        ins.then_inc(self.sem, 1)
        self.eng.wait_ge(self.sem, self.off + self.n)


def settle(eng, spare):
    eng.sem_inc(spare, 1)


def ring_uses(names, first, off):
    return {name: ((first + i) % 2, (first + i) // 2 + 1 + off) for i, name in enumerate(names)}



def norm_stats(dve, link, t, ve_done, spare, eps=EPS):
    for tt in range(TT):
        dve.bn_stats(t.stats[:, tt, :], t.r[:, tt, :]) if tt < TT - 1 else \
            link(dve.bn_stats(t.stats[:, tt, :], t.r[:, tt, :]))
    settle(dve, spare)
    for tt in range(TT):
        dve.bn_aggr(t.mv[:, tt, :], t.stats[:, tt, :]) if tt < TT - 1 else \
            link(dve.bn_aggr(t.mv[:, tt, :], t.stats[:, tt, :]))
    dve.tensor_scalar(t.ve[:, :], t.mv[:, :, 1], eps, None, ALU.add).then_inc(ve_done, 1)


def norm_apply(dve, t, out, tt):
    return dve.tensor_scalar(out, t.r[:, tt, :], t.mv[:, tt, 0:1], t.rstd[:, tt:tt + 1], ALU.subtract, ALU.mult)


class NormTiles:
    def __init__(self, sc):
        self.r = sc.sb("r", [P, TT, D])
        self.stats = sc.sb("stats", [P, TT, 6])
        self.mv = sc.sb("mv", [P, TT, 2])
        self.ve = sc.sb("ve", [P, TT])
        self.rstd = sc.sb("rstd", [P, TT])
        self.half = sc.sb("half", [P, TT])


def plan_of(text):
    return [(word.rstrip("0123456789"), int(word[len(word.rstrip("0123456789")):] or 0)) for word in text.split()]


PLANS = {
    "b": plan_of("""
        max0 key0 x_turn values0 max1 key1 max2 key2 max3 values1 project key3 values2 max4 values3 max5
        sums max6 max7 spread max_row output"""),
    "d": plan_of("""
        key0 max0 values0 max1 key1 max2 x_turn key2 max3 values1 key3 values2 project values3 max4 max5
        max6 sums max7 spread max_row output"""),
    "e": plan_of("""
        key0 max0 key1 max1 x_turn values0 max2 project key2 max3 values1 key3 values2 max4 values3 max5
        max6 sums max7 spread max_row output"""),
}



def attention(nc, x_all, w, tag, causal=False, masked=False, own=False, wide=False):
    C = 2 if wide else 1
    VH = 64 if wide else 32
    NV = 4 if wide else 1
    NO = 2 if wide else 1
    OS = 1 if wide else 2
    LOADS = 2 * PARTS + 1
    UNITS = 2 * NG
    NB = 3
    with ExitStack() as ctx:
        sc = Scope(nc, ctx, tag)
        A = sc.ps("A", [P, 2, 512])
        Sc = sc.ps("Sc", [P, 2, 1024])
        O = sc.ps("O", [P, OS, C, 512 // C])
        Zc = sc.ps("Zc", [P, 512]) if wide else O[:, 0, 0, :]

        wq = sc.sb("wq", [P, P])
        wk = sc.sb("wk", [P, P])
        wv = sc.sb("wv", [P, 1024 if wide else P])
        wo = sc.sb("wo", [P, NG * C, D])
        bo = sc.sb("bo", [P, D])
        bq = sc.sb("bq", [P, 1])
        bk = sc.sb("bk", [P, 1])
        bv = sc.sb("bv", [P, 1024 if wide else P])
        ident = sc.sb("ident", [P, P])
        identb = sc.sb("identb", [P, P], BF16)
        collect = sc.sb("collect", [P, NG, 32 if wide else P])
        spread = sc.sb("spread", [P, NG, P])
        maskq = sc.sb("maskq", [P, TT, 2, S if masked else P], BF16)
        maskk = sc.sb("maskk", [P, TT, 2, S if masked else P], BF16)
        mask32 = sc.sb("mask32", [P, 2, TT, S], I32) if masked else None

        xb = sc.sb("xb", [P, TT, D])
        xT = sc.sb("xT", [P, S])
        ctxT = sc.sb("ctxT", [P, NB, S])
        z = sc.sb("z", [P, 2, S])
        zu = sc.sb("zu", [P, 2, S])
        zl = sc.sb("zl", [P, 2, S]) if own else z
        parts = sc.sb("parts", [P, 2, PARTS, S], BF16)
        qst = [sc.sb(f"qst{i}", [P, H, S], BF16) for i in range(NB)]
        kst = [sc.sb(f"kst{i}", [P, H, S], BF16) for i in range(NB)]
        V = [sc.sb(f"V{i}", [P, TT, H, VH]) for i in range(NB)]
        zv = sc.sb("zv", [P, TT, 1024]) if wide else None
        mx = sc.sb("mx", [P, TT, H])
        nmT = sc.sb("nmT", [H, S], BF16)
        E = sc.sb("E", [P, 4, GJ, S])
        Os = sc.sb("Os", [P, NG, C, S])
        Rz = sc.sb("Rz", [P, S])
        ON = sc.sb("ON", [P, NG, C, S])
        xres = sc.sb("xres", [P, TT, D])
        res = sc.sb("res", [P, TT, D])
        nt = NormTiles(sc)
        scratch = [nc.dram_tensor(f"{tag}_scratch{i}", (2, PARTS, P, S), BF16).ap() for i in range(NB)]

        stack_in = [sc.sem(f"stack_in{i}") for i in range(NB)]
        ctx_in = [sc.sem(f"ctx_in{i}") for i in range(NB)]
        a_full = [sc.sem(f"a_full{i}") for i in range(2)]
        a_free = [sc.sem(f"a_free{i}") for i in range(2)]
        (proj_in, w_in, const_in, cleared, consts, scores, exp_done, pv_done, o_done, zc_full, rz_done, chain, pchain, mrow,
         xb_done, parts_done, scr_done, v_done, leaky_done, xres_done, ve_done, rstd_done, x_done,
         spare) = (sc.sem(n) for n in (
             "proj_in", "w_in", "const_in", "cleared", "consts", "scores", "exp_done", "pv_done", "o_done", "zc_full", "rz_done",
             "chain", "pchain", "mrow", "xb_done", "parts_done", "scr_done", "v_done",
             "leaky_done", "xres_done", "ve_done", "rstd_done", "x_done", "spare"))

        has_bias = f"{tag}_bq" in w
        first_loads = [(ident, w["ident"]), (wv, w[f"{tag}_wv"]), (wq, w[f"{tag}_wq"]), (wk, w[f"{tag}_wk"])]
        if has_bias:
            first_loads += [(bv, w[f"{tag}_bv"].partition_broadcast(P)), (bq, w[f"{tag}_bq"]), (bk, w[f"{tag}_bk"])]
        loads = [(identb, w["identb"]), (wo, w[f"{tag}_wo"]), (bo, w[f"{tag}_bo"].partition_broadcast(P)),
                 (collect, w["collect_wide" if wide else "collect"]), (spread, w["spread"])]
        if causal:
            loads += [(maskq, w["causal_q"]), (maskk, w["causal_k"])]
        if masked:
            loads += [(mask32, w["mask"])]

        plan = PLANS[tag]
        roles = {"max": "max", "max_row": "max", "x_turn": "prep", "project": "prep", "key": "weights",
                 "values": "weights", "sums": "weights", "spread": "weights", "output": "weights"}

        def uses_of(op, n):
            return {"max": [f"m{n}{qt}" for qt in range(TT)], "x_turn": ["xT"], "max_row": ["mT"],
                    "project": [f"v{v}" for v in range(NV)] + ["q", "k"], "spread": ["b0", "b1"],
                    "output": [f"out{o}" for o in range(NO)]}.get(op, [])

        class Step:

            def __init__(self, s, turn, first, off, lap=0, has=("max", "weights", "prep")):
                self.bm = s if "max" in has else None
                self.bw = s - 1 if "weights" in has else None
                self.bp = s + 1 if "prep" in has else None
                self.im, self.iw, self.ip = turn % NB, (turn - 1) % NB, (turn + 1) % NB
                self.um, self.up = turn // NB + 1 + lap, (turn + 1) // NB + 1 + lap
                self.early = has == ("max", "prep")
                self.work = [(op, n) for op, n in plan if roles[op] in has]
                if self.early:
                    self.work.sort(key=lambda o: roles[o[0]] != "prep")
                self.uses = [name for op, n in self.work for name in uses_of(op, n)]
                self.ring = ring_uses(self.uses, first, off)

        full = [name for op, n in plan for name in uses_of(op, n)]

        def walk(eng, do, chains=()):
            n = 0
            for s, has in ((-1, ("prep",)), (0, ("max", "prep"))):
                step = Step(s, s, n, 0, has=has)
                do(step)
                n += len(step.uses)
            per = NB * len(full)
            assert per % 2 == 0
            marks = [c.n for c in chains]
            rounds = (B - 2) // NB
            with eng.Fori(0, rounds) as i:
                for c in chains:
                    c.off = i * c.per
                for k in range(NB):
                    do(Step(i * NB + (1 + k), 1 + k, n + k * len(full), i * (per // 2), i))
            for c, m in zip(chains, marks):
                assert c.n - m == c.per, (tag, c.n - m)
                c.off, c.n = 0, m + rounds * c.per
            n += rounds * per
            for s, has in ((B - 1, ("max", "weights")), (B, ("weights",))):
                step = Step(s, s, n, 0, has=has)
                do(step)
                n += len(step.uses)

        def first_of(b, n):
            return isinstance(b, int) and b < n

        def tiles(b, tt=0, n=TT):
            return slice(2 * b + tt, 2 * b + tt + n) if isinstance(b, int) else bass.ds(b * 2 + tt, n)

        with nc.Block() as block:

            @block.sync
            def _(sp):
                for dst, src in first_loads:
                    sp.dma_start(dst[:], src).then_inc(proj_in, 16)
                if not own:
                    for i in range(2):
                        sp.dma_start(ctxT[:, i, :], w["ctxT"][i]).then_inc(ctx_in[i], 16)
                for dst, src in loads:
                    sp.dma_start(dst[:], src).then_inc(w_in, 16)
                sp.wait_ge(cleared, 2 * NB)
                for i in range(NB):
                    sp.dma_start(kst[i][STACK:STACK + 1], w["ones_row"]).then_inc(const_in, 16)

                def do(st):
                    if st.bp is not None:
                        if not own and not first_of(st.bp, 2):
                            sp.wait_ge(parts_done, st.bp - (NB - 2))
                            settle(sp, spare)
                            sp.dma_start(ctxT[:, st.ip, :], w["ctxT"][st.bp]).then_inc(ctx_in[st.ip], 16)
                        sp.wait_ge(parts_done, st.bp + 2)
                        for t in range(2):
                            sp.dma_start(scratch[st.ip][t].rearrange("c p n -> p c n"),
                                         parts[:, t]).then_inc(scr_done, 16)
                        sp.wait_ge(scr_done, 32 * (st.bp + 1))
                        settle(sp, spare)
                        if not first_of(st.bp, NB):
                            sp.wait_ge(scores, UNITS * (st.bp - 2) + 1)
                        for a in range(PARTS):
                            rows = slice(a * PARTS * HD, (a + 1) * PARTS * HD)
                            src = scratch[st.ip][0, a].rearrange("(d h) n -> d (h n)", d=HD)
                            sp.dma_start(qst[st.ip][rows].rearrange("p h n -> p (h n)"),
                                         src.unsqueeze(0).broadcast_to([PARTS, HD, H * S])).then_inc(stack_in[st.ip], 16)
                            src = scratch[st.ip][1].rearrange("c (d h) n -> (c d) (h n)", d=HD)
                            sp.dma_start(kst[st.ip][rows].rearrange("p h n -> p (h n)"), src).then_inc(stack_in[st.ip], 16)
                        sp.dma_start(qst[st.ip][STACK:STACK + 1], w["zeros_row"]).then_inc(stack_in[st.ip], 16)
                    if st.bm is not None:
                        bank, k = st.ring["mT"]
                        sp.wait_ge(a_free[bank], k + 1)
                        sp.dma_start(qst[st.im][STACK:STACK + 1], nmT[:, :]).then_inc(mrow, 16)

                walk(sp, do)

            @block.gpsimd
            def _(pool):
                for s, n in ((a_free[0], 1), (a_free[1], 1), (exp_done, 2), (pv_done, 2), (o_done, OS),
                             (parts_done, 1), (scores, 1)):
                    pool.sem_inc(s, n)
                for t in kst:
                    pool.memset(t[:].bitcast(F32), 0.0).then_inc(cleared, 1)
                for t in V:
                    pool.memset(t[:], 0.0).then_inc(consts, 1)
                pool.memset(nt.half[:, :], -0.5).then_inc(consts, 1)
                pool.wait_ge(consts, NB + 1)
                if not wide:
                    for t in V:
                        pool.memset(t[:, :, :, HD:HD + 1], 1.0).then_inc(consts, 1)
                ch = Chain(pool, pchain)
                ch.per = NB * 3

                def do(st):
                    if st.early:
                        pool.wait_ge(w_in, 16 * len(loads))
                    if st.bp is not None:
                        if not first_of(st.bp, 2):
                            pool.tensor_copy(xb[:, :, :], x_all[:, tiles(st.bp), :]).then_inc(xb_done, 1)
                        if own:
                            pool.wait_ge(leaky_done, st.bp + 1)
                        else:
                            for name in ("q", "k"):
                                bank, k = st.ring[name]
                                pool.wait_ge(a_free[bank], k + 1)
                        pool.wait_ge(scr_done, 32 * st.bp)
                        settle(pool, spare)
                        ch.link(pool.tensor_copy(parts[:, :, 0, :], zl[:]))
                        ch.link(pool.tensor_tensor(zu[:], zl[:], parts[:, :, 0, :], ALU.subtract))
                        settle(pool, spare)
                        ch.link(pool.tensor_copy(parts[:, :, 1, :], zu[:]))
                        pool.tensor_tensor(parts[:, :, 2, :], zu[:], parts[:, :, 1, :],
                                           ALU.subtract).then_inc(parts_done, 1)
                    if st.bw is not None:
                        other = x_all[:, tiles(st.bw), :] if own else bo[:, :].unsqueeze(1).broadcast_to([P, TT, D])
                        pool.tensor_tensor(xres[:, :, :], x_all[:, tiles(st.bw), :], other,
                                           ALU.add).then_inc(xres_done, 1)
                        pool.wait_ge(ve_done, st.bw + 1)
                        pool.tensor_tensor(nt.rstd[:, :], nt.ve[:, :], nt.half[:, :], ALU.pow).then_inc(rstd_done, 1)

                walk(pool, do, [ch])

            @block.scalar
            def _(act):
                if has_bias:
                    act.wait_ge(proj_in, 16 * len(first_loads))

                def take(st, name):
                    bank, k = st.ring[name]
                    act.wait_ge(a_full[bank], k)
                    return A[:, bank, :], a_free[bank]

                def exps(st, g):
                    for kt in range(TT):
                        act.wait_ge(scores, UNITS * st.bw + 2 * g + kt + 2)
                        act.wait_ge(pv_done, NG * st.bw + g + 1)
                        slot = (2 * g + kt) % 4
                        if causal and kt == 1:
                            src = Sc[:, kt, 0:GJ * P].rearrange("p (j q) -> p j q", j=GJ)
                            dst = E[:, slot, :, P:S]
                        else:
                            src = Sc[:, kt, :].rearrange("p (j q) -> p j q", j=GJ)
                            dst = E[:, slot, :, :]
                        act.activation(dst, src, ACT.Exp, scale=SCALE).then_inc(exp_done, 1)

                def keep(st, g):
                    act.wait_ge(pv_done, NG * st.bw + g + 3)
                    act.activation(Os[:, g], O[:, g % OS, :, 0:S], ACT.Copy).then_inc(o_done, 1)

                def do(st):
                    for op, n in st.work:
                        if op == "key":
                            exps(st, n)
                        elif op == "values":
                            keep(st, n)
                        elif op == "x_turn":
                            src, done = take(st, "xT")
                            act.activation(xT[:, :], src[:, 0:S], ACT.Copy).then_inc(done, 1)
                        elif op == "project":
                            for t, (name, bias) in enumerate((("q", bq), ("k", bk))):
                                src, done = take(st, name)
                                if t == 0:
                                    act.wait_ge(parts_done, st.bp + 1)
                                act.activation(z[:, t, :], src[:, 0:S], ACT.Identity,
                                               bias=bias[:, 0:1] if has_bias else 0.0).then_inc(done, 1)
                        elif op == "max_row":
                            src, done = take(st, "mT")
                            act.wait_ge(mrow, 16 * st.bm)
                            act.activation(nmT[:, :], src[0:H, 0:S], ACT.Copy, scale=-1.0).then_inc(done, 1)

                walk(act, do)

            @block.vector
            def _(dve):
                for t in qst:
                    dve.memset(t[64:P].bitcast(F32), 0.0).then_inc(cleared, 1)
                if has_bias:
                    dve.wait_ge(proj_in, 16 * len(first_loads))
                if masked or own:
                    dve.wait_ge(w_in, 16 * len(loads))
                dve.wait_ge(consts, NB + 1 if wide else 2 * NB + 1)
                ch = Chain(dve, chain)
                ch.per = NB * (4 if own else 2)
                if masked:
                    for n, m in enumerate((maskq, maskk)):
                        for c in range(2):
                            dve.tensor_scalar(m[:, :, c, :], mask32[:, n], 0, -BIG, ALU.is_equal,
                                              ALU.mult).then_inc(consts, 1)

                def take(st, name):
                    bank, k = st.ring[name]
                    dve.wait_ge(a_full[bank], k)
                    return A[:, bank, :], a_free[bank]

                def maxima(st, n):
                    for qt in range(TT):
                        src, done = take(st, f"m{n}{qt}")
                        keys = P if causal and qt == 0 else S
                        dve.tensor_reduce(mx[:, qt, 2 * n:2 * n + 2],
                                          src[:, 0:2 * keys].rearrange("p (h k) -> p h k", h=2),
                                          AX.X, ALU.max).then_inc(done, 1)

                def project(st):
                    if wide:
                        vals = V[st.ip][:].rearrange("p t h v -> p t (h v)")
                        for n in range(NV):
                            src, done = take(st, f"v{n}")
                            cols = slice(512 * (n % 2), 512 * (n % 2) + 512)
                            dve.tensor_tensor(zv[:, n // 2, cols], src, bv[:, cols], ALU.add).then_inc(done, 1)
                            dve.wait_ge(done, st.ring[f"v{n}"][1] + 1)
                            dve.scalar_tensor_tensor(vals[:, n // 2, cols], zv[:, n // 2, cols], 0.01,
                                                     zv[:, n // 2, cols], ALU.mult, ALU.max).then_inc(v_done, 1)
                    else:
                        src, done = take(st, "v0")
                        src = src[:, 0:S].rearrange("p (t h d) -> p t h d", t=TT, h=H)
                        for tt in range(TT):
                            dst = V[st.ip][:, tt, :, 0:HD]
                            if has_bias:
                                ins = dve.tensor_tensor(dst, src[:, tt], bv[:, :].rearrange("p (h d) -> p h d", h=H),
                                                        ALU.add)
                            else:
                                ins = dve.tensor_copy(dst, src[:, tt])
                        ins.then_inc(done, 1)
                    if own:
                        for name in ("q", "k"):
                            bank, k = st.ring[name]
                            dve.wait_ge(a_free[bank], k + 1)
                        dve.scalar_tensor_tensor(zl[:], z[:], 0.01, z[:], ALU.mult, ALU.max).then_inc(leaky_done, 1)

                def divide(st):
                    for n in range(2):
                        src, done = take(st, f"b{n}")
                        gs = slice(2 * n, 2 * n + 2)
                        src = src.rearrange("p (g q) -> p g q", g=2)
                        if C == 1:
                            dve.tensor_tensor(ON[:, gs, 0], Os[:, gs, 0], src, ALU.mult).then_inc(done, 1)
                        else:
                            dve.tensor_tensor(ON[:, gs], Os[:, gs], src.unsqueeze(2).broadcast_to([P, 2, C, S]),
                                              ALU.mult).then_inc(done, 1)

                def finish(st):
                    dve.wait_ge(xres_done, st.bw + 1)
                    for n in range(NO):
                        src, done = take(st, f"out{n}")
                        tts = slice(n * TT // NO, (n + 1) * TT // NO)
                        src = src[:, 0:TT // NO * D].rearrange("p (t d) -> p t d", d=D)
                        if own:
                            boc = bo[:, :].unsqueeze(1).broadcast_to([P, TT // NO, D])
                            dve.tensor_tensor(res[:, tts], src, boc, ALU.add).then_inc(done, 1)
                        else:
                            dve.tensor_tensor(nt.r[:, tts], src, xres[:, tts], ALU.add).then_inc(done, 1)
                    for n in range(NO):
                        bank, k = st.ring[f"out{n}"]
                        dve.wait_ge(a_free[bank], k + 1)
                    if own:
                        ch.link(dve.scalar_tensor_tensor(nt.r[:], res[:], 0.01, res[:], ALU.mult, ALU.max))
                        ch.link(dve.tensor_tensor(nt.r[:], nt.r[:], xres[:], ALU.add))
                    norm_stats(dve, ch.link, nt, ve_done, spare)
                    dve.wait_ge(rstd_done, st.bw + 1)
                    for tt in range(TT):
                        norm_apply(dve, nt, x_all[:, tiles(st.bw, tt, 1), :].squeeze(1), tt).then_inc(x_done, 1)

                def do(st):
                    for op, n in st.work:
                        if op == "max":
                            maxima(st, n)
                        elif op == "project":
                            project(st)
                        elif op == "sums":
                            dve.wait_ge(zc_full, st.bw + 1)
                            dve.reciprocal(Rz[:, :], Zc[:, 0:S]).then_inc(rz_done, 1)
                        elif op == "spread":
                            divide(st)
                        elif op == "output":
                            finish(st)

                walk(dve, do, [ch])

            @block.tensor
            def _(pe):
                pe.wait_ge(proj_in, 16 * len(first_loads))

                def use(st, name):
                    bank, k = st.ring[name]
                    pe.wait_ge(a_free[bank], k)
                    return A[:, bank, :], a_full[bank]

                def maxima(st, n):
                    q, k = qst[st.im], kst[st.im]
                    if n == 0:
                        pe.wait_ge(stack_in[st.im], 16 * LOADS * st.um)
                    for qt in range(TT):
                        dst, done = use(st, f"m{n}{qt}")
                        keys = P if causal and qt == 0 else S
                        for c in range(2):
                            mm = pe.matmul(dst[:, c * keys:(c + 1) * keys], q[:, 2 * n + c, qt * P:(qt + 1) * P],
                                           k[:, 2 * n + c, 0:keys], start=c == 0,
                                           stop=not (masked or causal) and c == 1, skip_group_check=True)
                        if masked:
                            mm = pe.matmul(dst[:, 0:2 * S], identb[:, :],
                                           maskq[:, qt].rearrange("p c k -> p (c k)"), start=False, stop=True,
                                           skip_group_check=True)
                        if causal:
                            mm = pe.matmul(dst[:, 0:2 * keys].rearrange("p (c k) -> p c k", c=2)[:, :, keys - P:keys],
                                           identb[:, :], maskq[:, qt], start=False, stop=True,
                                           skip_group_check=True)
                        mm.then_inc(done, 1)

                def by_key(st, g):
                    q, k = qst[st.iw], kst[st.iw]
                    if g == 0:
                        pe.wait_ge(mrow, 16 * (st.bw + 1))
                    for kt in range(TT):
                        pe.wait_ge(exp_done, UNITS * st.bw + 2 * g + kt + 1)
                        short = causal and kt == 1
                        nq = P if short else S
                        for bank in range(1 if short else 2):
                            heads = range(GJ) if short else range(2 * bank, 2 * bank + 2)
                            dst = Sc[:, kt, 512 * bank:512 * bank + 512]
                            for n, j in enumerate(heads):
                                mm = pe.matmul(dst[:, n * nq:(n + 1) * nq],
                                               k[:, GJ * g + j, kt * P:(kt + 1) * P],
                                               q[:, GJ * g + j, S - nq:S], start=n == 0,
                                               stop=not (masked or causal) and j == heads[-1], skip_group_check=True)
                            if masked:
                                mm = pe.matmul(dst, identb[:, :], maskk[:, kt].rearrange("p c q -> p (c q)"),
                                               start=False, stop=True, skip_group_check=True)
                            if causal:
                                d3 = dst.rearrange("p (n q) -> p n q", n=len(heads))
                                for n in range(0, len(heads), 2):
                                    mm = pe.matmul(d3[:, n:n + 2, 0:P], identb[:, :], maskk[:, kt],
                                                   start=False, stop=n + 2 == len(heads), skip_group_check=True)
                        mm.then_inc(scores, 1)

                def outputs(st, g):
                    if g == 0 and wide:
                        pe.wait_ge(v_done, NV * (st.bw + 1))
                    pe.wait_ge(o_done, NG * st.bw + g + 1)
                    for kt in range(TT):
                        pe.wait_ge(exp_done, UNITS * st.bw + 2 * g + kt + 3)
                        slot = (2 * g + kt) % 4
                        q0 = P if causal and kt == 1 else 0
                        for c in range(C):
                            for j in range(GJ):
                                mm = pe.matmul(O[32 * j:32 * j + 32, g % OS, c, q0:S],
                                               V[st.iw][:, kt, GJ * g + j, 32 * c:32 * c + 32],
                                               E[:, slot, j, q0:S], start=kt == 0 and c == 0, stop=kt == 1,
                                               skip_group_check=True)
                        if wide:
                            for j in range(GJ):
                                mm = pe.matmul(Zc[32 * j:32 * j + 32, 0:S], collect[:, g, :], E[:, slot, j, :],
                                               start=g == 0 and kt == 0, stop=g == NG - 1 and kt == 1,
                                               skip_group_check=True)
                    mm.then_inc(pv_done, 1)

                def denominators(st):
                    pe.wait_ge(o_done, NG * (st.bw + 1) + OS)
                    if wide:
                        pe.sem_inc(zc_full, 1)
                        return
                    for g in range(NG):
                        mm = pe.matmul(Zc[:, 0:S], collect[:, g, :], Os[:, g, 0, :], start=g == 0, stop=g == NG - 1)
                    mm.then_inc(zc_full, 1)

                def reciprocals(st):
                    pe.wait_ge(rz_done, st.bw + 1)
                    for n in range(2):
                        dst, done = use(st, f"b{n}")
                        for k in range(2):
                            mm = pe.matmul(dst[:, k * S:(k + 1) * S], spread[:, 2 * n + k, :], Rz[:, :], start=True,
                                           stop=True)
                        mm.then_inc(done, 1)

                def turn(st):
                    bank, k = st.ring[f"m{H // 2 - 1}{TT - 1}"]
                    pe.wait_ge(a_free[bank], k + 1)
                    dst, done = use(st, "mT")
                    for qt in range(TT):
                        mm = pe.transpose(dst[0:H, qt * P:(qt + 1) * P], mx[:, qt, :], ident[:, :])
                    mm.then_inc(done, 1)

                def turn_x(st):
                    src = xb
                    if first_of(st.bp, 2):
                        src = x_all[:, tiles(st.bp), :]
                    else:
                        pe.wait_ge(xb_done, st.bp - 1)
                    dst, done = use(st, "xT")
                    for tt in range(TT):
                        mm = pe.transpose(dst[:, tt * P:(tt + 1) * P], src[:, tt, :], ident[:, :])
                    mm.then_inc(done, 1)

                def project(st):
                    bank, k = st.ring["xT"]
                    pe.wait_ge(a_free[bank], k + 1)
                    kv = xT[:, :] if own else ctxT[:, st.ip, :]
                    if not own:
                        pe.wait_ge(ctx_in[st.ip], 16 * st.up)
                    if wide:
                        for n in range(NV):
                            dst, done = use(st, f"v{n}")
                            pe.matmul(dst, kv[:, (n // 2) * P:(n // 2 + 1) * P],
                                      wv[:, 512 * (n % 2):512 * (n % 2) + 512], start=True,
                                      stop=True).then_inc(done, 1)
                    else:
                        dst, done = use(st, "v0")
                        for tt in range(TT):
                            mm = pe.matmul(dst[:, tt * D:(tt + 1) * D], kv[:, tt * P:(tt + 1) * P], wv[:, :],
                                           start=True, stop=True)
                        mm.then_inc(done, 1)
                    for name, wt, src in (("q", wq, xT[:, :]), ("k", wk, kv)):
                        dst, done = use(st, name)
                        pe.matmul(dst[:, 0:S], wt[:, :], src, start=True, stop=True).then_inc(done, 1)

                def output(st):
                    bank, k = st.ring["b1"]
                    pe.wait_ge(a_free[bank], k + 1)
                    for tt in range(TT):
                        if tt % (TT // NO) == 0:
                            dst, done = use(st, f"out{tt // (TT // NO)}")
                        at = tt % (TT // NO)
                        for n in range(NG * C):
                            mm = pe.matmul(dst[:, at * D:(at + 1) * D], ON[:, n // C, n % C, tt * P:(tt + 1) * P],
                                           wo[:, n, :], start=n == 0, stop=n == NG * C - 1, skip_group_check=True)
                        if tt % (TT // NO) == TT // NO - 1:
                            mm.then_inc(done, 1)

                work = {"max": maxima, "key": by_key, "values": outputs}
                single = {"x_turn": turn_x, "project": project, "sums": denominators, "spread": reciprocals,
                          "max_row": turn, "output": output}

                def do(st):
                    for op, n in st.work:
                        if st.early and (op, n) == ("max", 0):
                            pe.wait_ge(const_in, 16 * NB)
                            pe.wait_ge(w_in, 16 * len(loads))
                            pe.wait_ge(consts, (NB + 1 if wide else 2 * NB + 1) + (4 if masked else 0))
                        if op in work:
                            work[op](st, n)
                        else:
                            single[op](st)

                walk(pe, do)


def moe(nc, x_all, w):
    NE, NP_ = 64, 32
    SL = NE * NP_
    CH = SL // P
    EC = P // NP_
    QT = 4
    NQ = CH // QT
    with ExitStack() as outer:
        so = Scope(nc, outer, "c")
        phi = so.sb("phi", [P, SL])
        xT = so.sb("xT", [P, B, S])
        yall = so.sb("yall", [P, CH, B, D + 1])
        top = so.sb("top", [P, B, S])
        top_dram = nc.dram_tensor("c_top_dram", (B, TT, P), F32).ap()
        ident = so.sb("ident", [P, P])

        with ExitStack() as ctx:
            sc = Scope(nc, ctx, "c1")
            We = [sc.sb(f"We{i}", [P, EC, D]) for i in range(2)]
            eb = sc.sb("eb", [P, CH, D])
            E = sc.sb("E", [P, 2, TT, B, P])
            M = sc.sb("M", [P, TT, P])
            Zs = sc.sb("Zs", [P, TT, P])
            half_sum = sc.sb("half_sum", [P, TT, B // 2, P])
            Rz = sc.sb("Rz", [P, TT, P])
            slots = sc.sb("slots", [P, B, P])
            pm = sc.sb("pm", [P, TT, B, CH])
            R = sc.sb("R", [P, TT, B])
            RT = sc.sb("RT", [TT * B, P])
            L = sc.ps("L", [P, TT, B, P])
            ST = sc.ps("ST", [P, B, P])
            Y = sc.ps("Y", [P, B, P])
            w_in = [sc.sem(f"w_in{i}") for i in range(2)]
            e_in = [sc.sem(f"e_in{i}") for i in range(2)]
            ident_in = sc.sem("ident_in")
            xt_full, xt_done = sc.sem("xt_full"), sc.sem("xt_done")
            consts = sc.sem("consts")
            l_full = sc.sem("l_full")
            shifted, l_free = sc.sem("shifted"), sc.sem("l_free")
            exp_done = sc.sem("exp_done")
            zs_done, pchain = sc.sem("zs_done"), sc.sem("pchain")
            rz_done = sc.sem("rz_done")
            weights_done = sc.sem("weights_done")
            st_full, st_done = sc.sem("st_full"), sc.sem("st_done")
            y_full, y_done = sc.sem("y_full"), sc.sem("y_done")
            chain = sc.sem("chain")
            r_done, rt_full, rt_done, row_in = (sc.sem(n) for n in ("r_done", "rt_full", "rt_done", "row_in"))
            spare = sc.sem("spare")

            with nc.Block() as block:

                def loop(eng, do, chain=None):
                    do(0, 0, 2, False)
                    do(1, 1, 2, True)
                    n = chain.n if chain else 0
                    with eng.Fori(0, (CH - 4) // 2) as i:
                        if chain:
                            chain.off = i * chain.per
                        do(i * 2 + 2, 0, 2, True)
                        do(i * 2 + 3, 1, 2, True)
                    if chain:
                        assert chain.n - n == chain.per, chain.n - n
                        chain.off, chain.n = 0, n + chain.per * (CH - 4) // 2
                    do(CH - 2, 0, 1, True)
                    do(CH - 1, 1, 0, True)

                @block.sync
                def _(sp):
                    sp.dma_start(ident[:, :], w["ident"]).then_inc(ident_in, 16)
                    for n in range(2):
                        sp.dma_start(phi[:, n * SL // 2:(n + 1) * SL // 2],
                                     w["c_phi"][:, n * SL // 2:(n + 1) * SL // 2]).then_inc(w_in[0], 16)
                    sp.dma_start(eb[:], w["c_b"]).then_inc(w_in[1], 16)

                    def do(c, par, more, before):
                        experts = slice(0, EC) if isinstance(c, int) and c == 0 else \
                            slice(EC * c, EC * c + EC) if isinstance(c, int) else bass.ds(c * EC, EC)
                        if before:
                            sp.wait_ge(y_full, c)
                            settle(sp, spare)
                        sp.dma_start(We[par][:], w["c_W"][:, experts, :]).then_inc(e_in[par], 16)
                    loop(sp, do)
                    sp.wait_ge(rt_done, 1)
                    for tt in range(TT):
                        sp.dma_start(top_dram[:, tt, :], RT[tt * B:(tt + 1) * B, :]).then_inc(row_in, 16)
                    sp.wait_ge(row_in, 32)
                    sp.dma_start(top[:].rearrange("p b n -> p (b n)"),
                                 top_dram.rearrange("b t n -> (b t n)").partition_broadcast(P)).then_inc(row_in, 16)
                    sp.wait_ge(row_in, 48)

                @block.gpsimd
                def _(pool):
                    pool.sem_inc(y_full, 1)
                    pool.memset(yall[:, :, :, D:D + 1], 1.0).then_inc(consts, 1)

                    ch = Chain(pool, pchain)
                    ch.per = 2 * 4

                    def do(c, par, more, before):
                        for tt in range(TT):
                            pool.wait_ge(exp_done, c * 2 + (tt + 1))
                            e = E[:, par, tt]
                            ch.link(pool.tensor_tensor(half_sum[:, tt], e[:, 0:4], e[:, 4:8], ALU.add))
                            ch.link(pool.tensor_tensor(half_sum[:, tt, 0:2], half_sum[:, tt, 0:2], half_sum[:, tt, 2:4], ALU.add))
                            pool.tensor_tensor(Zs[:, tt, :], half_sum[:, tt, 0], half_sum[:, tt, 1],
                                               ALU.add).then_inc(zs_done, 1)
                        for tt in range(TT):
                            pool.wait_ge(rz_done, c * 2 + (tt + 1))
                            pool.tensor_tensor(E[:, par, tt], E[:, par, tt],
                                               Rz[:, tt, :].unsqueeze(1).broadcast_to([P, B, P]),
                                               ALU.mult).then_inc(weights_done, 1)
                    loop(pool, do, ch)

                @block.scalar
                def _(act):
                    for n in range(4):
                        act.wait_ge(xt_full, n + 1)
                        act.activation(xT[:, 2 * n:2 * n + 2, :],
                                       L[:].rearrange("p t b n -> p (t b n)")[:, 512 * n:512 * n + 512]
                                       .rearrange("p (b m) -> p b m", b=2), ACT.Copy).then_inc(xt_done, 1)

                    def exps(c, par):
                        for tt in range(TT):
                            act.wait_ge(shifted, c * 2 + (tt + 1))
                            act.activation(E[:, par, tt], E[:, par, tt], ACT.Exp).then_inc(exp_done, 1)

                    exps(0, 0)

                    def do(c, par, more, before):
                        if more:
                            exps(c + 1, 1 - par)
                        act.wait_ge(st_full, c + 1)
                        if before:
                            act.wait_ge(y_full, c + 1)
                        act.activation(slots[:], ST[:], ACT.Copy).then_inc(st_done, 1)
                    loop(act, do)
                    act.wait_ge(rt_full, 1)
                    act.activation(RT[:, :], L[0:TT * B, 0, 0, :], ACT.Copy).then_inc(rt_done, 1)

                @block.vector
                def _(dve):
                    ch = Chain(dve, chain)
                    ch.per = 2 * 2

                    def shift(c, par):
                        for tt in range(TT):
                            dve.wait_ge(l_full, c * 2 + (tt + 1))
                            src = L[:, tt]
                            ch.link(dve.tensor_reduce(M[:, tt, :], src.rearrange("p b n -> p n b"), AX.X, ALU.max))
                            dve.tensor_tensor(E[:, par, tt], src, M[:, tt, :].unsqueeze(1).broadcast_to([P, B, P]),
                                              ALU.subtract).then_inc(shifted, 1)
                            dve.tensor_reduce(pm[:, tt, :, c] if isinstance(c, int)
                                              else pm[:, tt, :, bass.ds(c, 1)].squeeze(2),
                                              src, AX.X, ALU.max).then_inc(l_free, 1)

                    shift(0, 0)
                    dve.wait_ge(w_in[1], 16)

                    def evacuate(c):
                        dve.wait_ge(y_full, c + 2)
                        if isinstance(c, int):
                            dst, bias = yall[:, c, :, 0:D], eb[:, c, :]
                        else:
                            dst, bias = yall[:, bass.ds(c, 1), :, 0:D].squeeze(1), eb[:, bass.ds(c, 1), :].squeeze(1)
                        dve.tensor_tensor(dst, Y[:], bias.unsqueeze(1).broadcast_to([P, B, D]),
                                          ALU.add).then_inc(y_done, 1)

                    def do(c, par, more, before):
                        for tt in range(TT):
                            dve.wait_ge(zs_done, c * 2 + (tt + 1))
                            if before:
                                dve.wait_ge(weights_done, c * 2 + (tt - 1))
                                settle(dve, spare)
                            dve.reciprocal(Rz[:, tt, :], Zs[:, tt, :]).then_inc(rz_done, 1)
                        if more:
                            if before:
                                dve.wait_ge(st_full, c)
                            shift(c + 1, 1 - par)
                        if before:
                            evacuate(c - 1)
                    loop(dve, do, ch)
                    evacuate(CH - 1)
                    dve.tensor_reduce(R[:], pm[:], AX.X, ALU.max).then_inc(r_done, 1)

                @block.tensor
                def _(pe):
                    pe.wait_ge(ident_in, 16)
                    flat = L[:].rearrange("p t b n -> p (t b n)")
                    for n in range(4):
                        for k in range(4):
                            mm = pe.transpose(flat[:, 512 * n + P * k:512 * n + P * k + P],
                                              x_all[:, 4 * n + k, :], ident[:, :])
                        mm.then_inc(xt_full, 1)
                    pe.wait_ge(xt_done, 4)
                    pe.wait_ge(w_in[0], 32)

                    def logits(c, before):
                        cols = slice(c * P, c * P + P) if isinstance(c, int) else bass.ds(c * P, P)
                        for tt in range(TT):
                            if before:
                                pe.wait_ge(l_free, c * 2 + (tt - 1))
                            for b in range(B):
                                mm = pe.matmul(L[:, tt, b, :], xT[:, b, tt * P:(tt + 1) * P], phi[:, cols],
                                               start=True, stop=True)
                            mm.then_inc(l_full, 1)

                    logits(0, False)
                    logits(1, True)

                    def do(c, par, more, before):
                        pe.wait_ge(weights_done, c * 2 + 2)
                        if before:
                            pe.wait_ge(st_done, c)
                        for b in range(B):
                            for tt in range(TT):
                                mm = pe.matmul(ST[:, b, :], x_all[:, 2 * b + tt, :], E[:, par, tt, b, :],
                                               start=tt == 0, stop=tt == TT - 1)
                        mm.then_inc(st_full, 1)
                        if more == 2:
                            logits(c + 2, True)
                        pe.wait_ge(st_done, c + 1)
                        if before:
                            pe.wait_ge(y_done, c)
                        pe.wait_ge(e_in[par], 16 * (c // 2 + 1) if isinstance(c, int) else c * 8 + (16 - 8 * par))
                        for b in range(B):
                            for n in range(EC):
                                mm = pe.matmul(Y[NP_ * n:NP_ * n + NP_, b, :], slots[:, b, NP_ * n:NP_ * n + NP_],
                                               We[par][:, n, :], start=True, stop=True, skip_group_check=True)
                        mm.then_inc(y_full, 1)
                    loop(pe, do)
                    pe.wait_ge(r_done, 1)
                    pe.transpose(L[0:TT * B, 0, 0, :], R[:].rearrange("p t b -> p (t b)"),
                                 ident[:, :]).then_inc(rt_full, 1)

        with ExitStack() as ctx:
            sc = Scope(nc, ctx, "c2")
            CE = sc.sb("CE", [P, NQ, QT, S])
            rz = sc.sb("rz", [P, TT])
            nt = NormTiles(sc)
            LT = sc.ps("LT", [P, 2, QT, S])
            O = sc.ps("O", [P, TT, D + 1])
            consts = sc.sem("consts")
            l_full, shifted, exp_done, used = (sc.sem(n) for n in ("l_full", "shifted", "exp_done", "used"))
            o_done = sc.sem("o_done")
            rz_done, ve_done, rstd_done, x_done = (sc.sem(n) for n in ("rz_done", "ve_done", "rstd_done", "x_done"))
            chain, spare = sc.sem("chain"), sc.sem("spare")
            with nc.Block() as block:

                @block.gpsimd
                def _(pool):
                    pool.memset(nt.half[:, :], -0.5).then_inc(consts, 1)
                    pool.wait_ge(consts, 1)
                    pool.sem_inc(shifted, 2)
                    pool.sem_inc(used, NQ)
                    pool.sem_inc(o_done, 2)
                    with pool.Fori(0, B) as b:
                        pool.wait_ge(ve_done, b + 1)
                        pool.tensor_tensor(nt.rstd[:, :], nt.ve[:, :], nt.half[:, :], ALU.pow).then_inc(rstd_done, 1)

                @block.scalar
                def _(act):
                    with act.Fori(0, B) as b:
                        for q in range(NQ):
                            act.wait_ge(shifted, b * NQ + (q + 3))
                            act.activation(CE[:, q], CE[:, q], ACT.Exp).then_inc(exp_done, 1)

                def loop(eng, start, do, chain=None):
                    start()
                    with eng.Fori(0, B - 1) as b:
                        if chain:
                            chain.off = b * chain.per
                        do(b, True)
                    if chain:
                        assert chain.n == chain.per, chain.n
                        chain.off, chain.n = (B - 1) * chain.per, 0
                    do(B - 1, False)

                def of_batch(t, b):
                    return t[:, b] if isinstance(b, int) else t[:, bass.ds(b, 1)].squeeze(1)

                def tile(b, tt):
                    return x_all[:, 2 * b + tt, :] if isinstance(b, int) else x_all[:, bass.ds(b * 2 + tt, 1), :].squeeze(1)

                @block.vector
                def _(dve):
                    ch = Chain(dve, chain)
                    ch.per = 3

                    def shift(b, q):
                        dve.wait_ge(l_full, b * NQ + (q + 1))
                        dve.wait_ge(used, b * NQ + (q + 1))
                        dve.tensor_tensor(CE[:, q], LT[:, q % 2], of_batch(top, b).unsqueeze(1).broadcast_to([P, QT, S]),
                                          ALU.subtract).then_inc(shifted, 1)

                    def start():
                        dve.wait_ge(consts, 1)
                        shift(0, 0)
                        shift(0, 1)

                    def do(b, more):
                        shift(b, 2)
                        shift(b, 3)
                        if more:
                            shift(b + 1, 0)
                        dve.wait_ge(used, b * NQ + 2 * NQ)
                        ch.link(dve.reciprocal(rz[:, :], O[:, :, D]))
                        for tt in range(TT):
                            dve.scalar_tensor_tensor(nt.r[:, tt, :], O[:, tt, 0:D], rz[:, tt:tt + 1], tile(b, tt),
                                                     ALU.mult, ALU.add).then_inc(o_done, 1)
                        if more:
                            shift(b + 1, 1)
                        dve.wait_ge(o_done, b * 2 + 4)
                        settle(dve, spare)
                        norm_stats(dve, ch.link, nt, ve_done, spare)
                        dve.wait_ge(rstd_done, b + 1)
                        for tt in range(TT):
                            norm_apply(dve, nt, tile(b, tt), tt).then_inc(x_done, 1)
                    loop(dve, start, do, ch)

                @block.tensor
                def _(pe):
                    def logits(b, q):
                        pe.wait_ge(shifted, b * NQ + (q + 1))
                        for n in range(QT):
                            t = QT * q + n
                            mm = pe.matmul(LT[:, q % 2, n, :], phi[:, t * P:(t + 1) * P], of_batch(xT, b),
                                           start=True, stop=True)
                        mm.then_inc(l_full, 1)

                    def outputs(b, q):
                        pe.wait_ge(exp_done, b * NQ + (q + 1))
                        if q == 0:
                            pe.wait_ge(o_done, b * 2 + 2)
                        for n in range(QT):
                            t = QT * q + n
                            for tt in range(TT):
                                mm = pe.matmul(O[:, tt, :], CE[:, q, n, tt * P:(tt + 1) * P], of_batch(yall[:, t], b),
                                               start=t == 0 and tt == 0, stop=t == CH - 1, skip_group_check=True)
                        mm.then_inc(used, 1)

                    def start():
                        logits(0, 0)
                        logits(0, 1)

                    def do(b, more):
                        outputs(b, 0)
                        logits(b, 2)
                        outputs(b, 1)
                        logits(b, 3)
                        outputs(b, 2)
                        if more:
                            logits(b + 1, 0)
                        outputs(b, 3)
                        if more:
                            logits(b + 1, 1)
                    loop(pe, start, do)


def mlstm(nc, x_all, w):
    NH, DQ, DV = 8, 8, 16
    BH = B * NH
    CAP = 15.0
    EPS_H = 1e-6
    NGA = NH // GJ
    VC = 32
    with ExitStack() as outer:
        so = Scope(nc, outer, "a")
        bT = so.sb("bT", [P, TT, BH])
        emT = so.sb("emT", [P, TT, BH])
        ident = so.sb("ident", [P, P])
        g_dram = nc.dram_tensor("a_g", (BH, S), F32).ap()

        with ExitStack() as ctx:
            sc = Scope(nc, ctx, "a1")
            xT = sc.sb("xT", [P, B, S])
            wg = sc.sb("wg", [P, 2, B, BH])
            gb = sc.sb("gb", [BH, 2])
            pre = sc.sb("pre", [BH, 2, S])
            gate = sc.sb("gate", [BH, 2, S])
            zero = sc.sb("zero", [BH, S])
            F = sc.sb("F", [BH, S])
            bg = sc.sb("bg", [BH, S])
            g = sc.sb("g", [BH, S])
            m = sc.sb("m", [BH, S])
            em = sc.sb("em", [BH, S])
            G = sc.ps("G", [BH, 2, 512])
            T = sc.ps("T", [P, 2, TT, BH])
            w_in, x_in, g_full, pre_done, tanh_done, chain, g_done, m_done, em_done, t_full, t_done, g_out, consts = (
                sc.sem(n) for n in ("w_in", "x_in", "g_full", "pre_done", "tanh_done", "chain", "g_done", "m_done",
                                    "em_done", "t_full", "t_done", "g_out", "consts"))
            with nc.Block() as block:

                @block.sync
                def _(sp):
                    sp.dma_start(wg[:], w["a_wg"]).then_inc(w_in, 16)
                    sp.dma_start(gb[:, :], w["a_gb"]).then_inc(w_in, 16)
                    sp.dma_start(ident[:, :], w["ident"]).then_inc(w_in, 16)
                    sp.dma_start(xT[:], w["xT"].rearrange("b d n -> d b n")).then_inc(w_in, 16)
                    sp.dma_start(x_all[:], w["x"]).then_inc(x_in, 16)
                    sp.wait_ge(g_done, 1)
                    sp.dma_start(g_dram, g[:, :]).then_inc(g_out, 16)
                    sp.wait_ge(g_out, 16)
                    sp.wait_ge(x_in, 16)

                @block.tensor
                def _(pe):
                    pe.wait_ge(w_in, 64)
                    for k in range(2):
                        for b in range(B):
                            mm = pe.matmul(G[:, k, 0:S], wg[:, k, b, :], xT[:, b, :], start=b == 0, stop=b == B - 1)
                    mm.then_inc(g_full, 1)
                    pe.wait_ge(g_done, 1)
                    for tt in range(TT):
                        mm = pe.transpose(T[:, 0, tt, :], bg[:, tt * P:(tt + 1) * P], ident[0:BH, 0:BH])
                    pe.wait_ge(em_done, 1)
                    for tt in range(TT):
                        mm = pe.transpose(T[:, 1, tt, :], em[:, tt * P:(tt + 1) * P], ident[0:BH, 0:BH])
                    mm.then_inc(t_full, 1)

                @block.vector
                def _(dve):
                    ch = Chain(dve, chain)
                    ch.link(dve.memset(zero[:, :], 0.0))
                    dve.wait_ge(w_in, 64)
                    dve.wait_ge(g_full, 1)
                    for k in range(2):
                        dve.tensor_scalar(pre[:, k, :], G[:, k, 0:S], gb[:, k:k + 1], 1.0 / CAP, ALU.add,
                                          ALU.mult).then_inc(pre_done, 1)
                    dve.wait_ge(tanh_done, 1)
                    ch.link(dve.tensor_scalar(gate[:], gate[:], CAP, None, ALU.mult))
                    ch.link(dve.tensor_tensor_scan(F[:, :], gate[:, 1, :], zero[:, :], 0.0, ALU.add, ALU.add))
                    ch.link(dve.tensor_tensor(bg[:, :], gate[:, 0, :], F[:, :], ALU.subtract))
                    dve.tensor_tensor_scan(g[:, :], bg[:, :], bg[:, :], 0.0, ALU.max, ALU.max).then_inc(g_done, 1)
                    dve.wait_ge(g_done, 1)
                    dve.tensor_tensor(m[:, :], g[:, :], F[:, :], ALU.add).then_inc(m_done, 1)
                    dve.wait_ge(t_full, 1)
                    dve.tensor_copy(bT[:], T[:, 0]).then_inc(t_done, 1)
                    dve.tensor_copy(emT[:], T[:, 1]).then_inc(t_done, 1)

                @block.scalar
                def _(act):
                    act.wait_ge(pre_done, 2)
                    act.activation(gate[:], pre[:], ACT.Tanh).then_inc(tanh_done, 1)
                    act.wait_ge(m_done, 1)
                    act.activation(em[:, :], m[:, :], ACT.Exp, scale=-1.0).then_inc(em_done, 1)

        with ExitStack() as ctx:
            sc = Scope(nc, ctx, "a2")
            wq, wk = sc.sb("wq", [P, NGA, P]), sc.sb("wk", [P, NGA, P])
            wvo = sc.sb("wvo", [P, 2 * D])
            wout = sc.sb("wout", [P, D])
            lnw, lnb = sc.sb("lnw", [P, D]), sc.sb("lnb", [P, D])
            mask = sc.sb("mask", [P, S])
            xT = sc.sb("xT", [P, S])
            g = sc.sb("g", [P, NH, S])
            bs = sc.sb("bs", [P, TT, NH])
            q, kx = sc.sb("q", [P, NGA, S]), sc.sb("kx", [P, NGA, GJ, S])
            V = sc.sb("V", [P, TT, NH, VC])
            og = sc.sb("og", [P, TT, D])
            sg = sc.sb("sg", [P, TT, D])
            W = sc.sb("W", [P, NH, S + P])
            Os = sc.sb("Os", [P, NGA, S])
            den = sc.sb("den", [P, TT, NH])
            rden = sc.sb("rden", [P, TT, NH])
            hn = sc.sb("hn", [P, TT, D])
            hT = sc.sb("hT", [P, S])
            ht = NormTiles(sc)
            nt = NormTiles(Scope(nc, ctx, "a3"))
            X = sc.ps("X", [P, 512])
            O = sc.ps("O", [P, NGA, S])
            S0 = sc.ps("S0", [P, NH, S])
            S1 = sc.ps("S1", [P, NH, P])
            QK = S1[:].rearrange("p h n -> p (h n)").rearrange("p (t g n) -> p t g n", t=2, g=NGA)
            (w_in, x_in, consts, gt_in, x_full, x_free, qk_full, qk_done, bs_done, s_full, arg_done, w_done, p_done,
             pv_full, pv_free, chain, xg_done, h_ve, h_rstd, h_done, ve_done, rstd_done, x_done, spare, og_done,
             hT_done) = (sc.sem(n) for n in (
                 "w_in", "x_in", "consts", "gt_in", "x_full", "x_free", "qk_full", "qk_done", "bs_done", "s_full",
                 "arg_done", "w_done", "p_done", "pv_full", "pv_free", "chain", "xg_done", "h_ve", "h_rstd",
                 "h_done", "ve_done", "rstd_done", "x_done", "spare", "og_done", "hT_done"))
            loads = [(wq, w["a_wq"]), (wk, w["a_wk"]), (wvo, w["a_wvo"]), (wout, w["a_wout"]),
                     (lnw, w["a_lnw"].partition_broadcast(P)), (lnb, w["a_lnb"].partition_broadcast(P)),
                     (mask, w["a_mask"])]

            def uses(b, last):
                return (None, b * 4 + 2, b * 4 + 3, b * 4 + 4) if last else \
                    (b * 4 + 2, b * 4 + 3, b * 4 + 4, b * 4 + 5)

            def loop(eng, early, late, chain=None):
                early(0, 1)
                n = chain.n if chain else 0
                with eng.Fori(0, B - 1) as b:
                    if chain:
                        chain.off = b * chain.per
                    u = uses(b, False)
                    late(b, None, 0)
                    early(b + 1, u[0])
                    late(b, u, 1)
                if chain:
                    assert chain.n - n == chain.per, chain.n - n
                    chain.off, chain.n = 0, n + (B - 1) * chain.per
                late(B - 1, None, 0)
                late(B - 1, uses(B - 1, True), 1)

            def tiles(b, tt=0, n=1):
                return slice(2 * b + tt, 2 * b + tt + n) if isinstance(b, int) else bass.ds(b * 2 + tt, n)

            with nc.Block() as block:

                @block.sync
                def _(sp):
                    for dst, src in loads:
                        sp.dma_start(dst[:], src).then_inc(w_in, 16)

                    def early(b, _):
                        if not isinstance(b, int):
                            sp.wait_ge(s_full, b)
                            settle(sp, spare)
                            sp.wait_ge(arg_done, b * 2)
                            settle(sp, spare)
                        sp.dma_start(xT[:, :], w["xT"][b]).then_inc(x_in, 16)
                        rows = slice(0, NH) if isinstance(b, int) else bass.ds(b * NH, NH)
                        sp.dma_start(g[:], g_dram[rows, :].unsqueeze(0).broadcast_to([P, NH, S])).then_inc(gt_in, 16)
                    loop(sp, early, lambda *a: None)

                @block.gpsimd
                def _(pool):
                    pool.sem_inc(h_done, 1)
                    pool.sem_inc(pv_free, 1)
                    pool.memset(kx[:], 0.0).then_inc(consts, 1)
                    pool.memset(V[:], 0.0).then_inc(consts, 1)
                    pool.wait_ge(consts, 2)
                    pool.memset(V[:, :, :, DV:DV + 1], 1.0).then_inc(consts, 1)
                    pool.memset(ht.half[:, :], -0.5).then_inc(consts, 1)
                    pool.memset(nt.half[:, :], -0.5).then_inc(consts, 1)
                    pool.wait_ge(consts, 5)

                    def late(b, u, part):
                        if part == 1:
                            pool.wait_ge(h_ve, b + 1)
                            pool.tensor_tensor(ht.rstd[:, :], ht.ve[:, :], ht.half[:, :], ALU.pow).then_inc(h_rstd, 1)
                            pool.wait_ge(ve_done, b + 1)
                            pool.tensor_tensor(nt.rstd[:, :], nt.ve[:, :], nt.half[:, :], ALU.pow)\
                                .then_inc(rstd_done, 1)
                    loop(pool, lambda *a: None, late)

                @block.scalar
                def _(act):
                    act.wait_ge(consts, 5)

                    def early(b, use):
                        for t in range(2):
                            act.wait_ge(qk_full, b * 2 + t + 1)
                            if t == 0 and not isinstance(b, int):
                                act.wait_ge(s_full, b)
                            if t == 0:
                                act.activation(q[:], QK[:, t], ACT.Copy).then_inc(qk_done, 1)
                            else:
                                for j in range(GJ):
                                    rows = slice(32 * j, 32 * j + 32)
                                    act.activation(kx[rows, :, j, :], QK[rows, t], ACT.Copy).then_inc(qk_done, 1)
                        for kt in range(TT):
                            act.wait_ge(arg_done, b * 2 + kt + 1)
                            cols = slice(0, S) if kt == 0 else slice(S, S + P)
                            act.activation(W[:, :, cols], W[:, :, cols], ACT.Exp, scale=-1.0).then_inc(w_done, 1)

                    def late(b, u, part):
                        if part == 0:
                            act.wait_ge(p_done, b * 2 + 1)
                            act.wait_ge(h_done, b + 1)
                            act.activation(sg[:], og[:], ACT.Tanh, scale=0.5).then_inc(og_done, 1)
                            return
                        act.wait_ge(pv_full, b + 1)
                        act.activation(Os[:], O[:], ACT.Copy).then_inc(pv_free, 1)
                        act.wait_ge(x_full, u[2])
                        act.activation(hT[:, :], X[:, 0:S], ACT.Copy, scale=0.5).then_inc(x_free, 1)
                    loop(act, early, late)

                @block.vector
                def _(dve):
                    dve.wait_ge(w_in, 16 * len(loads))
                    dve.wait_ge(consts, 5)
                    ch = Chain(dve, chain)
                    ch.per = CHAIN_A

                    def early(b, use):
                        rows = slice(NH * b, NH * b + NH) if isinstance(b, int) else bass.ds(b * NH, NH)
                        ch.link(dve.tensor_copy(bs[:], bT[:, :, rows]))
                        dve.wait_ge(gt_in, (b + 1) * 16)
                        if not isinstance(b, int):
                            dve.wait_ge(pv_full, b)
                        for kt in range(TT):
                            for h in range(NH):
                                cols = slice(0, S) if kt == 0 else slice(S, S + P)
                                gs = g[:, h, 0:S] if kt == 0 else g[:, h, P:S]
                                ins = dve.scalar_tensor_tensor(W[:, h, cols], gs, bs[:, kt, h:h + 1],
                                                               mask[:, 0:S] if kt == 0 else mask[:, 0:P],
                                                               ALU.subtract, ALU.add)
                            ins.then_inc(arg_done, 1)
                        dve.wait_ge(x_full, use)
                        if not isinstance(b, int):
                            dve.wait_ge(og_done, b)
                        vo = X[:, :].rearrange("p (t n) -> p t n", t=TT)
                        for tt in range(TT):
                            dve.tensor_copy(V[:, tt, :, 0:DV], vo[:, tt, 0:D].rearrange("p (h d) -> p h d", h=NH))
                        dve.tensor_copy(og[:], vo[:, :, D:2 * D]).then_inc(x_free, 1)
                        dve.wait_ge(s_full, b + 1)
                        for kt in range(TT):
                            dve.wait_ge(w_done, b * 2 + kt + 1)
                            cols = slice(0, S) if kt == 0 else slice(S, S + P)
                            dve.scalar_tensor_tensor(W[:, :, cols], S0[:] if kt == 0 else S1[:],
                                                     float(DQ) ** -0.5, W[:, :, cols], ALU.mult,
                                                     ALU.mult).then_inc(p_done, 1)

                    def late(b, u, part):
                        if part == 0:
                            return
                        rows = slice(NH * b, NH * b + NH) if isinstance(b, int) else bass.ds(b * NH, NH)
                        dve.wait_ge(x_full, u[1])
                        o = X[:, :].rearrange("p (t h v) -> p t h v", t=TT, h=NH)
                        ch.link(dve.tensor_tensor(den[:], o[:, :, :, DV], emT[:, :, rows], ALU.max))
                        ch.link(dve.scalar_tensor_tensor(den[:], o[:, :, :, DV], -1.0, den[:], ALU.mult, ALU.max))
                        ch.link(dve.tensor_scalar(den[:], den[:], 1e-6, None, ALU.add))
                        ch.link(dve.reciprocal(rden[:], den[:]))
                        for tt in range(TT):
                            ins = dve.tensor_tensor(ht.r[:, tt, :].rearrange("p (h v) -> p h v", h=NH),
                                                    o[:, tt, :, 0:DV],
                                                    rden[:, tt, :].unsqueeze(2).broadcast_to([P, NH, DV]), ALU.mult)
                        ins.then_inc(x_free, 1)
                        dve.wait_ge(x_free, u[1])
                        settle(dve, spare)
                        norm_stats(dve, ch.link, ht, h_ve, spare, EPS_H)
                        dve.wait_ge(h_rstd, b + 1)
                        for tt in range(TT):
                            ins = norm_apply(dve, ht, hn[:, tt, :], tt)
                        ch.link(ins)
                        ch.link(dve.tensor_tensor(hn[:], hn[:], lnw[:, :].unsqueeze(1).broadcast_to([P, TT, D]),
                                                  ALU.mult))
                        ch.link(dve.tensor_tensor(hn[:], hn[:], lnb[:, :].unsqueeze(1).broadcast_to([P, TT, D]),
                                                  ALU.add))
                        dve.wait_ge(og_done, b + 1)
                        dve.scalar_tensor_tensor(hn[:], sg[:], 1.0, hn[:], ALU.add, ALU.mult).then_inc(h_done, 1)
                        dve.wait_ge(x_full, u[3])
                        y = X[:, 0:TT * D].rearrange("p (t d) -> p t d", t=TT)
                        dve.tensor_tensor(nt.r[:], y, x_all[:, tiles(b, 0, 2), :], ALU.add).then_inc(x_free, 1)
                        dve.wait_ge(x_free, u[3])
                        settle(dve, spare)
                        norm_stats(dve, ch.link, nt, ve_done, spare)
                        dve.wait_ge(rstd_done, b + 1)
                        for tt in range(TT):
                            norm_apply(dve, nt, x_all[:, tiles(b, tt), :].squeeze(1), tt).then_inc(x_done, 1)
                    loop(dve, early, late, ch)

                @block.tensor
                def _(pe):
                    pe.wait_ge(w_in, 16 * len(loads))
                    pe.wait_ge(consts, 5)

                    def early(b, use):
                        pe.wait_ge(x_in, (b + 1) * 16)
                        pe.wait_ge(x_free, use - 1)
                        for tt in range(TT):
                            mm = pe.matmul(X[:, tt * 2 * D:(tt + 1) * 2 * D], xT[:, tt * P:(tt + 1) * P], wvo[:, :],
                                           start=True, stop=True)
                        mm.then_inc(x_full, 1)
                        if not isinstance(b, int):
                            pe.wait_ge(p_done, b * 2)
                        for t, wt in enumerate((wq, wk)):
                            for gg in range(NGA):
                                mm = pe.matmul(QK[:, t, gg, :], wt[:, gg, :], xT[:, :], start=True, stop=True)
                            mm.then_inc(qk_full, 1)
                        pe.wait_ge(qk_done, b * 5 + 5)
                        for h in range(NH):
                            gg, j = h // GJ, h % GJ
                            pe.matmul(S0[:, h, :], kx[:, gg, j, 0:P], q[:, gg, :], start=True, stop=True)
                            mm = pe.matmul(S1[:, h, :], kx[:, gg, j, P:S], q[:, gg, P:S], start=True, stop=True)
                        mm.then_inc(s_full, 1)

                    def late(b, u, part):
                        if part == 0:
                            pe.wait_ge(p_done, b * 2 + 2)
                            pe.wait_ge(pv_free, b + 1)
                            for gg in range(NGA):
                                for kt in range(TT):
                                    for j in range(GJ):
                                        h = GJ * gg + j
                                        src = W[:, h, 0:S] if kt == 0 else W[:, h, S:S + P]
                                        mm = pe.matmul(O[32 * j:32 * j + 32, gg, kt * P:S], V[:, kt, h, :], src,
                                                       start=kt == 0, stop=kt == 1, skip_group_check=True)
                            mm.then_inc(pv_full, 1)
                            return
                        pe.wait_ge(pv_free, b + 2)
                        pe.wait_ge(x_free, u[1] - 1)
                        for tt in range(TT):
                            for gg in range(NGA):
                                mm = pe.transpose(X[:, (tt * NGA + gg) * P:(tt * NGA + gg + 1) * P],
                                                  Os[:, gg, tt * P:(tt + 1) * P], ident[:, :])
                        mm.then_inc(x_full, 1)
                        pe.wait_ge(h_done, b + 2)
                        for tt in range(TT):
                            mm = pe.transpose(X[:, tt * P:(tt + 1) * P], hn[:, tt, :], ident[:, :])
                        mm.then_inc(x_full, 1)
                        pe.wait_ge(x_free, u[2])
                        for tt in range(TT):
                            mm = pe.matmul(X[:, tt * D:(tt + 1) * D], hT[:, tt * P:(tt + 1) * P], wout[:, :],
                                           start=True, stop=True)
                        mm.then_inc(x_full, 1)
                    loop(pe, early, late)


CHAIN_A = 12


def ffn(nc, x_all, w, out):
    HID, RANK = 512, 16
    HC = HID // P
    with ExitStack() as ctx:
        sc = Scope(nc, ctx, "f")
        wf = sc.sb("wf", [P, HC, D])
        wp = sc.sb("wp", [P, HID])
        bf_, v = sc.sb("fast_bT", [RANK, RANK]), sc.sb("v", [RANK, D])
        uT = sc.sb("uT", [RANK, HID])
        gate = sc.sb("gate", [P, 1])
        ident = sc.sb("ident", [P, P])
        tmp = sc.sb("tmp", [P, HC, D])
        tern = sc.sb("tern", [P, HC, D])
        scf, scp = sc.sb("scf", [P, HC]), sc.sb("scp", [P, 1])
        half, nhalf = sc.sb("edge", [P, HC]), sc.sb("nedge", [P, HC])
        bv = sc.sb("bv", [RANK, D])
        A1 = sc.sb("A1", [P, HC, D])
        A2 = sc.sb("A2", [P, HC, D])
        A1T = sc.sb("A1T", [P, HC, P])
        A2T = sc.sb("A2T", [P, HC, D])
        xb = sc.sb("xb", [P, TT, D])
        xT = sc.sb("xT", [P, S])
        rl = sc.sb("rl", [P, HC, S])
        r2 = sc.sb("r2", [P, HC, S])
        y = sc.sb("y", [P, TT, D])
        nt = NormTiles(sc)
        XT = sc.ps("XT", [P, 512])
        HT = sc.ps("HT", [P, HC, S])
        Y = sc.ps("Y", [P, 512])
        WT = sc.ps("WT", [P, 2, HC, P])
        (w_in, chain, consts, bv_full, bv_done, um_full, a1_done, a2_done, wt_full, wt_done, xb_done, xt_full, xt_done,
         h_full, rl_done, r2_done, y_full, y_free, ve_done, rstd_done, n_done, out_done, spare) = (
            sc.sem(n) for n in ("w_in", "chain", "consts", "bv_full", "bv_done", "um_full", "a1_done", "a2_done",
                                "wt_full", "wt_done", "xb_done", "xt_full", "xt_done", "h_full", "rl_done",
                                "r2_done", "y_full", "y_free", "ve_done", "rstd_done", "n_done", "out_done", "spare"))
        loads = [(wf, w["f_wfc"]), (wp, w["f_wproj"]), (bf_, w["f_fast_bT"]), (v, w["f_v"]), (uT, w["f_uT"]),
                 (gate, w["f_gate"].partition_broadcast(P)), (ident, w["ident"])]

        def tiles(b, tt=0, n=1):
            return slice(2 * b + tt, 2 * b + tt + n) if isinstance(b, int) else bass.ds(b * 2 + tt, n)

        def loop(eng, early, late, chain=None):
            early(0)
            n = chain.n if chain else 0
            with eng.Fori(0, B - 1) as b:
                if chain:
                    chain.off = b * chain.per
                early(b + 1)
                late(b)
            if chain:
                assert chain.n - n == chain.per, chain.n - n
                chain.off, chain.n = 0, n + (B - 1) * chain.per
            late(B - 1)

        with nc.Block() as block:

            @block.sync
            def _(sp):
                for dst, src in loads:
                    sp.dma_start(dst[:], src).then_inc(w_in, 16)

                def late(b):
                    sp.wait_ge(n_done, b * 2 + 4)
                    settle(sp, spare)
                    sp.dma_start(out[b].rearrange("(t p) d -> p t d", p=P), y[:]).then_inc(out_done, 16)
                loop(sp, lambda b: None, late)
                sp.wait_ge(out_done, 16 * B + 16)

            @block.gpsimd
            def _(pool):
                for s, n in ((n_done, 2), (out_done, 16), (y_free, 1)):
                    pool.sem_inc(s, n)
                pool.memset(nt.half[:, :], -0.5).then_inc(consts, 1)
                pool.wait_ge(consts, 1)

                def early(b):
                    if not isinstance(b, int):
                        pool.wait_ge(xt_full, b)
                        settle(pool, spare)
                    pool.tensor_copy(xb[:], x_all[:, tiles(b, 0, 2), :]).then_inc(xb_done, 1)

                def late(b):
                    pool.wait_ge(ve_done, b + 1)
                    pool.tensor_tensor(nt.rstd[:, :], nt.ve[:, :], nt.half[:, :], ALU.pow).then_inc(rstd_done, 1)
                loop(pool, early, late)

            @block.scalar
            def _(act):
                act.wait_ge(bv_full, 1)
                act.activation(bv[:, :], XT[0:RANK, 0:D], ACT.Copy).then_inc(bv_done, 1)
                for n, (dst, width) in enumerate(((A1T, P), (A2T, D))):
                    act.wait_ge(wt_full, n + 1)
                    act.activation(dst[:], WT[:, n], ACT.Copy).then_inc(wt_done, 1)

                def early(b):
                    act.wait_ge(xt_full, b + 1)
                    if not isinstance(b, int):
                        act.wait_ge(h_full, b)
                    act.activation(xT[:, :], XT[:, 0:S], ACT.Copy).then_inc(xt_done, 1)
                    act.wait_ge(h_full, b + 1)
                    if not isinstance(b, int):
                        act.wait_ge(r2_done, b)
                    act.activation(rl[:], HT[:], ACT.Relu).then_inc(rl_done, 1)
                loop(act, early, lambda b: None)

            @block.vector
            def _(dve):
                ch = Chain(dve, chain)
                ch.per = 2
                dve.wait_ge(w_in, 16 * len(loads))
                wpt = wp[:, :].rearrange("p (c d) -> p c d", c=HC)

                def ternary(wt, scale, dst, tiles_):
                    ch.link(dve.scalar_tensor_tensor(tmp[:], wt, -1.0, wt, ALU.mult, ALU.max))
                    src = tmp[:] if tiles_ == HC else tmp[:].rearrange("p c d -> p (c d)").unsqueeze(1)
                    ch.link(dve.tensor_reduce(scale[:, :], src, AX.X, ALU.add))
                    ch.link(dve.tensor_scalar(scale[:, :], scale[:, :], tiles_ / float(HID), 1e-5, ALU.mult, ALU.max))
                    wide = scale[:, :].unsqueeze(2).broadcast_to([P, HC, D]) if tiles_ == HC else \
                        scale[:, :].unsqueeze(2).broadcast_to([P, HC, D])
                    ch.link(dve.tensor_scalar(half[:, 0:tiles_], scale[:, :], 0.5, None, ALU.mult))
                    ch.link(dve.tensor_scalar(nhalf[:, 0:tiles_], scale[:, :], -0.5, None, ALU.mult))
                    edge = half[:, 0:tiles_].unsqueeze(2).broadcast_to([P, HC, D])
                    ch.link(dve.tensor_tensor(tern[:], wt, edge, ALU.is_gt))
                    ch.link(dve.tensor_tensor(tmp[:], wt, nhalf[:, 0:tiles_].unsqueeze(2).broadcast_to([P, HC, D]), ALU.is_lt))
                    ch.link(dve.tensor_tensor(tern[:], tern[:], tmp[:], ALU.subtract))
                    ch.link(dve.tensor_tensor(tern[:], tern[:], wt, ALU.subtract))
                    ch.link(dve.tensor_tensor(tern[:], tern[:], wt, ALU.add))
                    return dve.tensor_tensor(dst[:], tern[:], wide, ALU.mult)

                ternary(wpt, scp, A2, 1).then_inc(a2_done, 1)
                dve.wait_ge(a2_done, 1)
                ch.link(ternary(wf[:], scf, A1, HC))
                dve.wait_ge(um_full, 1)
                um = HT[:, 0:2, :].rearrange("p a n -> p (a n)").rearrange("p (c d) -> p c d", c=HC)
                dve.scalar_tensor_tensor(A1[:], um, gate[:, 0:1], A1[:], ALU.mult, ALU.add).then_inc(a1_done, 1)

                def early(b):
                    dve.wait_ge(rl_done, b + 1)
                    if not isinstance(b, int):
                        dve.wait_ge(y_full, b)
                    dve.scalar_tensor_tensor(r2[:], HT[:], 0.0, rl[:], ALU.max, ALU.mult).then_inc(r2_done, 1)

                def late(b):
                    dve.wait_ge(y_full, b + 1)
                    dve.wait_ge(n_done, b * 2 + 2)
                    dve.tensor_tensor(nt.r[:], Y[:, 0:TT * D].rearrange("p (t d) -> p t d", t=TT),
                                      x_all[:, tiles(b, 0, 2), :], ALU.add).then_inc(y_free, 1)
                    dve.wait_ge(y_free, b + 2)
                    settle(dve, spare)
                    norm_stats(dve, ch.link, nt, ve_done, spare)
                    dve.wait_ge(rstd_done, b + 1)
                    dve.wait_ge(out_done, b * 16 + 16)
                    for tt in range(TT):
                        norm_apply(dve, nt, y[:, tt, :], tt).then_inc(n_done, 1)
                loop(dve, early, late, ch)

            @block.tensor
            def _(pe):
                pe.wait_ge(w_in, 16 * len(loads))
                pe.matmul(XT[0:RANK, 0:D], bf_[:, :], v[:, :], start=True, stop=True).then_inc(bv_full, 1)
                pe.wait_ge(bv_done, 1)
                um = HT[:, 0:2, :].rearrange("p a n -> p (a n)")
                for c in range(HC):
                    mm = pe.matmul(um[:, c * D:(c + 1) * D], uT[:, c * P:(c + 1) * P], bv[:, :], start=True, stop=True)
                mm.then_inc(um_full, 1)
                for n, (src, ready) in enumerate(((A1, a1_done), (A2, a2_done))):
                    pe.wait_ge(ready, 1)
                    for c in range(HC):
                        mm = pe.transpose(WT[:, n, c, :], src[:, c, :], ident[:, :])
                    mm.then_inc(wt_full, 1)
                pe.wait_ge(wt_done, 2)

                def early(b):
                    pe.wait_ge(xb_done, b + 1)
                    for tt in range(TT):
                        mm = pe.transpose(XT[:, tt * P:(tt + 1) * P], xb[:, tt, :], ident[:, :])
                    mm.then_inc(xt_full, 1)
                    pe.wait_ge(xt_done, b + 1)
                    if not isinstance(b, int):
                        pe.wait_ge(r2_done, b)
                    for c in range(HC):
                        mm = pe.matmul(HT[:, c, :], A1T[:, c, :], xT[:, :], start=True, stop=True)
                    mm.then_inc(h_full, 1)

                def late(b):
                    pe.wait_ge(r2_done, b + 1)
                    pe.wait_ge(y_free, b + 1)
                    for tt in range(TT):
                        for c in range(HC):
                            mm = pe.matmul(Y[:, tt * D:(tt + 1) * D], r2[:, c, tt * P:(tt + 1) * P], A2T[:, c, :],
                                           start=c == 0, stop=c == HC - 1)
                    mm.then_inc(y_full, 1)
                loop(pe, early, late)


def decoder(nc, w, out):
    with nc.sbuf_tensor("x_all", [P, B * TT, D], F32) as x_all:
        mlstm(nc, x_all, w)
        attention(nc, x_all, w, "b", masked=True)
        moe(nc, x_all, w)
        attention(nc, x_all, w, "d", own=True, wide=True)
        attention(nc, x_all, w, "e", causal=True)
        ffn(nc, x_all, w, out)



def lay(i):

    import numpy as np

    bf=np.dtype("bfloat16")
    f=lambda a: np.ascontiguousarray(a)
    B,S,D=8,256,128
    perm=lambda w: f(w.T.reshape(128,16,8).transpose(0,2,1).reshape(128,128))
    pcol=lambda b: f(b.reshape(16,8).T.reshape(128,1))
    def wo_n(w):
        t=w.T.reshape(4,4,8,128).transpose(1,2,0,3)
        o=np.zeros((4,32,4,128),w.dtype); o[:,:8]=t
        return o.reshape(128,4,128)
    eye=np.eye(128)
    c=np.where(np.arange(128)[None,:]>np.arange(128)[:,None],-1e30,0.0).astype(bf)
    o={
     "ctxT": f(i["ctx_1024"].transpose(0,2,1)),
     "ident": eye.astype(np.float32), "identb": eye.astype(bf),
     "ones_row": np.ones((1,16,256),bf), "zeros_row": np.zeros((1,16,256),bf),
     "causal_q": f(np.broadcast_to(c[:,None,None,:],(128,2,2,128))),
     "causal_k": f(np.broadcast_to(c.T[:,None,None,:],(128,2,2,128))),
     "b_wq": perm(i["L0_xattn_wq"]), "b_wk": perm(i["L0_xattn_wk"]), "b_wv": f(i["L0_xattn_wv"].T),
     "b_wo": wo_n(i["L0_xattn_wo"]), "b_bo": i["L0_xattn_bo"],
     "e_wq": perm(i["L1_xattn_Wq"]), "e_wk": perm(i["L1_xattn_Wk"]), "e_wv": f(i["L1_xattn_Wv"].T),
     "e_wo": wo_n(i["L1_xattn_Wo"]), "e_bo": i["L1_xattn_bo"],
     "e_bq": pcol(i["L1_xattn_bq"]), "e_bk": pcol(i["L1_xattn_bk"]), "e_bv": i["L1_xattn_bv"],
    }
    m=i["mask_1x1xSxS2_ik0"][0,0]
    o["mask"]=f(np.stack([m.reshape(2,128,256).transpose(1,0,2), m.T.reshape(2,128,256).transpose(1,0,2)],1))
    Wc=i["L1_attn_Wc"]; bc=i["L1_attn_bc"]
    o["d_wq"]=perm(Wc[:128]); o["d_wk"]=perm(Wc[128:256]); o["d_wv"]=f(Wc[256:].T)
    o["d_bq"]=pcol(bc[:128]); o["d_bk"]=pcol(bc[128:256]); o["d_bv"]=bc[256:]
    o["d_wo"]=f(i["L1_attn_Wo"].T.reshape(4,4,2,32,128).transpose(1,3,0,2,4).reshape(128,8,128))
    o["d_bo"]=i["L1_attn_bo"]
    r=np.arange(128)
    col=np.stack([((r[:,None]//32==r[None,:]//32)&(r[:,None]%32==8)&(r[None,:]%4==g)) for g in range(4)],1)
    o["collect"]=f(col.astype(np.float32))
    o["collect_wide"]=f(np.broadcast_to(np.stack([r[:32]%4==g for g in range(4)]),(128,4,32)).astype(np.float32))
    o["spread"]=f(np.stack([((r[:,None]//32==r[None,:]//32)&(r[:,None]%32==g)) for g in range(4)],1).astype(np.float32))
    x=i["x"]
    o["x"]=f(x.reshape(16,128,128).transpose(1,0,2)); o["xT"]=f(x.transpose(0,2,1))
    wg=np.zeros((128,2,8,8,8),np.float32)
    for b in range(8):
        wg[:,0,b,b]=i["L0_attn_Wi"].T; wg[:,1,b,b]=i["L0_attn_Wf"].T
    o["a_wg"]=wg.reshape(128,2,8,64)
    o["a_gb"]=f(np.stack([np.tile(i["L0_attn_bi"],8),np.tile(i["L0_attn_bf"],8)],1))
    def pad(w_):
        t=np.zeros((128,2,4,32),w_.dtype); t[...,:8]=w_.T.reshape(128,2,4,8); return t.reshape(128,2,128)
    o["a_wq"]=pad(i["L0_attn_Wq"]); o["a_wk"]=pad(i["L0_attn_Wk"])
    o["a_wvo"]=f(np.concatenate([i["L0_attn_Wv"].T,i["L0_attn_Wog"].T],1))
    o["a_wout"]=f(i["L0_attn_Wout"].T); o["a_lnw"]=i["L0_attn_ln_w"]; o["a_lnb"]=i["L0_attn_ln_b"]
    o["a_mask"]=f(np.where(np.arange(256)[None,:]<np.arange(128)[:,None],1e30,0.0).astype(np.float32))
    o["f_wfc"]=f(i["L1_ffn_w_fc"].reshape(4,128,128).transpose(1,0,2)); o["f_wproj"]=i["L1_ffn_w_proj"]
    o["f_fast_bT"]=f(i["L1_ffn_fast_b"].T); o["f_v"]=i["L1_ffn_v"]; o["f_uT"]=f(i["L1_ffn_u"].T)
    o["f_gate"]=i["L1_ffn_gate"].reshape(1)
    o["c_phi"]=f(i["L0_ffn_phi"].reshape(128,2048))
    o["c_W"]=f(i["L0_ffn_W"].transpose(1,0,2))
    o["c_b"]=f(np.broadcast_to(i["L0_ffn_b"].reshape(16,4,1,128),(16,4,32,128)).reshape(16,128,128).transpose(1,0,2))
    return o


def kernel(**inputs):
    import numpy as np
    import concourse.bacc as bacc
    from concourse.bass_utils import run_bass_kernel_spmd

    nc = bacc.Bacc("TRN2", target_bir_lowering=False, num_devices=1)
    arrays = {f"in_{k}": np.ascontiguousarray(v) for k, v in lay({k: np.asarray(v) for k, v in inputs.items()}).items()}
    w = {k[3:]: nc.dram_tensor(k, v.shape, mybir.dt.from_np(v.dtype), kind="ExternalInput").ap()
         for k, v in arrays.items()}
    out = nc.dram_tensor("out", (B, S, D), F32, kind="ExternalOutput").ap()
    decoder(nc, w, out)
    return run_bass_kernel_spmd(nc, [arrays], core_ids=[0]).results[0]["out"]
```

```python
from contextlib import ExitStack

import concourse.bass as bass
from concourse import mybir

F32 = mybir.dt.float32
BF16 = mybir.dt.bfloat16
I32 = mybir.dt.int32
ALU = mybir.AluOpType
ACT = mybir.ActivationFunctionType
AX = mybir.AxisListType

B, S, D = 8, 256, 128
P = 128
TT = S // P
EPS = 1e-5
BIG = 1e30
H, HD = 16, 8
NG, GJ = 4, 4
PARTS = 3
STACK = PARTS * PARTS * HD
SCALE = float(HD) ** -0.5


class Scope:

    def __init__(self, nc, ctx, tag):
        self.nc, self.ctx, self.tag, self.sems = nc, ctx, tag, []
        ctx.callback(self.clear)

    def sb(self, name, shape, dt=F32):
        return self.ctx.enter_context(self.nc.sbuf_tensor(f"{self.tag}_{name}", shape, dt))

    def ps(self, name, shape, dt=F32):
        return self.ctx.enter_context(self.nc.psum_tensor(f"{self.tag}_{name}", shape, dt))

    def sem(self, name):
        self.sems.append(self.nc.alloc_semaphore(f"{self.tag}_{name}"))
        return self.sems[-1]

    def clear(self):
        if self.sems:
            self.nc.all_engine_barrier()
            self.nc.clear_and_free_semaphores(self.sems)
            self.nc.all_engine_barrier()


class Chain:

    def __init__(self, eng, sem):
        self.eng, self.sem, self.n, self.off = eng, sem, 0, 0

    def link(self, ins):
        self.n += 1
        ins.then_inc(self.sem, 1)
        self.eng.wait_ge(self.sem, self.off + self.n)


class Held:

    def __init__(self, nc, ctx, w):
        self.sc, self.w, self.tiles, self.loads = Scope(nc, ctx, "held"), w, {}, {}
        self.add("shared", "ident", [P, P])
        self.add("shared", "identb", [P, P], BF16)
        self.add("shared", "collect", [P, NG, P])
        self.add("shared", "spread", [P, NG, P])
        for tag in ("b", "c", "d", "e", "f"):
            wide = tag == "d"
            if tag == "b":
                self.add(tag, "mask", [P, 2, TT, S], I32)
            if tag in ("b", "d", "e"):
                for n in ("wq", "wk"):
                    self.add(tag, f"{tag}_{n}", [P, P])
                self.add(tag, f"{tag}_wv", [P, 1024 if wide else P])
                self.add(tag, f"{tag}_wo", [P, NG * (2 if wide else 1), D])
                self.add(tag, f"{tag}_bo", [P, D], spread=True)
            if tag in ("d", "e"):
                self.add(tag, f"{tag}_bq", [P, 1])
                self.add(tag, f"{tag}_bk", [P, 1])
                self.add(tag, f"{tag}_bv", [P, 1024 if wide else P], spread=True)
            if tag == "c":
                self.add(tag, "c_phi", [P, 2048])
                self.add(tag, "c_b", [P, 16, D])
            if tag == "d":
                self.add(tag, "collect_wide", [P, NG, 32])
            if tag == "e":
                self.add(tag, "causal_q", [P, TT, 2, P], BF16)
                self.add(tag, "causal_k", [P, TT, 2, P], BF16)
            if tag == "f":
                self.add(tag, "f_wfc", [P, 4, D])
                self.add(tag, "f_wproj", [P, 512])
                self.add(tag, "f_fast_bT", [16, 16])
                self.add(tag, "f_v", [16, D])
                self.add(tag, "f_uT", [16, 512])
                self.add(tag, "f_gate", [P, 1], spread=True)
        self.full = {tag: self.sc.sem(f"{tag}_in") for tag in self.loads}

    def add(self, tag, name, shape, dt=F32, spread=False):
        self.tiles[name] = self.sc.sb(name, shape, dt)
        src = self.w[name].partition_broadcast(P) if spread else self.w[name]
        self.loads.setdefault(tag, []).append((self.tiles[name], src))

    def __getitem__(self, name):
        return self.tiles[name]

    def load(self, eng, *tags):
        for tag in tags:
            for dst, src in self.loads[tag]:
                eng.dma_start(dst[:], src).then_inc(self.full[tag], 16)

    def wait(self, eng, tag):
        eng.wait_ge(self.full[tag], 16 * len(self.loads[tag]))


def settle(eng, spare):
    eng.sem_inc(spare, 1)


def ring_uses(names, first, off, banks=2):
    return {name: ((first + i) % banks, (first + i) // banks + 1 + off) for i, name in enumerate(names)}



def norm_stats(dve, link, t, ve_done, spare, eps=EPS):
    for tt in range(t.n):
        ins = dve.bn_stats(t.stats[:, tt, :], t.r[:, tt, :])
    link(ins)
    settle(dve, spare)
    for tt in range(t.n):
        ins = dve.bn_aggr(t.mv[:, tt, :], t.stats[:, tt, :])
    link(ins)
    dve.tensor_scalar(t.ve[:, :], t.mv[:, :, 1], eps, None, ALU.add).then_inc(ve_done, 1)


def norm_apply(dve, t, out, tt):
    return dve.tensor_scalar(out, t.r[:, tt, :], t.mv[:, tt, 0:1], t.rstd[:, tt:tt + 1], ALU.subtract, ALU.mult)


class NormTiles:

    def __init__(self, sc, n=TT):
        self.n = n
        self.r = sc.sb("r", [P, n, D])
        self.stats = sc.sb("stats", [P, n, 6])
        self.mv = sc.sb("mv", [P, n, 2])
        self.ve = sc.sb("ve", [P, n])
        self.rstd = sc.sb("rstd", [P, n])
        self.half = sc.sb("half", [P, n])


def plan_of(text):
    return [(word.rstrip("0123456789"), int(word[len(word.rstrip("0123456789")):] or 0)) for word in text.split()]


PLANS = {
    "a": plan_of("""
        k outputs q result by_token apply values head_norm scores turn decay"""),
    "b": plan_of("""
        key0 x_turn max0 values0 max1 k key1 max2 q key2 values1 max3 key3 max4 value0 values2 max5 values3
        max6 max7 sums max_row spread output"""),
    "d": plan_of("""
        key0 max0 values0 max1 key1 max2 x_turn values1 q k key2 value0 max3 values2 max4 key3 max5 value1
        value2 values3 max6 max7 max_row sums value3 spread output"""),
    "e": plan_of("""
        x_turn max0 key0 k key1 q max1 values0 key2 values1 max2 key3 max3 values2 max4 value0 values3 max5
        max6 sums max7 spread max_row output"""),
}



def attention(nc, x_all, w, held, tag, causal=False, masked=False, own=False, wide=False):
    C = 2 if wide else 1
    VH = 64 if wide else 32
    NV = 4 if wide else 1
    NO = 2 if wide else 1
    RING = 2 if wide else 3
    LOADS = 2 * PARTS + 1
    UNITS = 2 * NG
    NB = 3
    EARLY = 0 if wide else 1
    with ExitStack() as ctx:
        sc = Scope(nc, ctx, tag)
        A = sc.ps("A", [P, RING, 512])
        Sc = sc.ps("Sc", [P, 2, 1024])
        O = sc.ps("O", [P, C, 512 // C])
        Zc = sc.ps("Zc", [P, 512]) if wide else O[:, 0, :]

        has_bias = f"{tag}_bq" in w
        wq, wk, wv, wo, bo = (held[f"{tag}_{n}"] for n in ("wq", "wk", "wv", "wo", "bo"))
        bq, bk, bv = (held[f"{tag}_{n}"] for n in ("bq", "bk", "bv")) if has_bias else (None, None, None)
        ident, identb = held["ident"], held["identb"]
        collect, spread = held["collect_wide" if wide else "collect"], held["spread"]
        mask32 = held["mask"] if masked else None
        if masked:
            maskq = sc.sb("maskq", [P, TT, 2, S], BF16)
            maskk = sc.sb("maskk", [P, TT, 2, S], BF16)
        elif causal:
            maskq, maskk = held["causal_q"], held["causal_k"]

        xb = sc.sb("xb", [P, TT, D])
        xT = sc.sb("xT", [P, S])
        ctxT = sc.sb("ctxT", [P, NB, S])
        z = sc.sb("z", [P, 2, S])
        zu = sc.sb("zu", [P, 2, S])
        zl = sc.sb("zl", [P, 2, S]) if own else z
        parts = sc.sb("parts", [P, 2, PARTS, S], BF16)
        qst = [sc.sb(f"qst{i}", [P, H, S], BF16) for i in range(NB)]
        kst = [sc.sb(f"kst{i}", [P, H, S], BF16) for i in range(NB)]
        V = [sc.sb(f"V{i}", [P, TT, H, VH]) for i in range(NB)]
        zv = sc.sb("zv", [P, TT, 1024]) if wide else None
        mx = sc.sb("mx", [P, TT, H])
        nmT = sc.sb("nmT", [H, S], BF16)
        E = sc.sb("E", [P, 4, GJ, S])
        Os = sc.sb("Os", [P, NG, C, S])
        Rz = sc.sb("Rz", [P, S])
        ON = sc.sb("ON", [P, NG, C, S])
        xres = sc.sb("xres", [P, TT, D])
        res = sc.sb("res", [P, TT, D])
        nt = NormTiles(sc)
        scratch = [nc.dram_tensor(f"{tag}_scratch{i}", (2, PARTS, P, S), BF16).ap() for i in range(NB)]

        stack_in = [sc.sem(f"stack_in{i}") for i in range(NB)]
        ctx_in = [sc.sem(f"ctx_in{i}") for i in range(NB)]
        a_full = [sc.sem(f"a_full{i}") for i in range(RING)]
        a_free = [sc.sem(f"a_free{i}") for i in range(RING)]
        cleared = [sc.sem(f"cleared{i}") for i in range(NB)]
        (v_clear, consts, scores, exp_done, pv_done, o_done, zc_full, rz_done, chain, pchain, mrow,
         xb_done, parts_done, scr_done, v_done, leaky_done, xres_done, ve_done, rstd_done, x_done,
         spare) = (sc.sem(n) for n in (
             "v_clear", "consts", "scores", "exp_done", "pv_done", "o_done", "zc_full", "rz_done",
             "chain", "pchain", "mrow", "xb_done", "parts_done", "scr_done", "v_done",
             "leaky_done", "xres_done", "ve_done", "rstd_done", "x_done", "spare"))

        plan = PLANS[tag]
        qk_last = [op for op, _ in plan if op in ("q", "k")][-1]
        roles = {"max": "max", "max_row": "max", "x_turn": "prep", "value": "prep", "q": "prep", "k": "prep",
                 "key": "weights", "values": "weights", "sums": "weights", "spread": "weights", "output": "weights"}

        def uses_of(op, n):
            return {"max": [f"m{n}{qt}" for qt in range(TT)], "x_turn": ["xT"], "max_row": ["mT"],
                    "value": [f"v{n}"], "q": ["q"], "k": ["k"], "spread": ["b0", "b1"],
                    "output": [f"out{o}" for o in range(NO)]}.get(op, [])

        class Step:

            def __init__(self, s, turn, first, off, lap=0, has=("max", "weights", "prep")):
                self.bm = s if "max" in has else None
                self.bw = s - 1 if "weights" in has else None
                self.bp = s + 1 if "prep" in has else None
                self.im, self.iw, self.ip = turn % NB, (turn - 1) % NB, (turn + 1) % NB
                self.um, self.up = turn // NB + 1 + lap, (turn + 1) // NB + 1 + lap
                self.early = has == ("max", "prep")
                self.work = [(op, n) for op, n in plan if roles[op] in has]
                if self.early:
                    self.work.sort(key=lambda o: roles[o[0]] != "prep")
                self.uses = [name for op, n in self.work for name in uses_of(op, n)]
                self.ring = ring_uses(self.uses, first, off, RING)

        full = [name for op, n in plan for name in uses_of(op, n)]

        def walk(eng, do, chains=()):
            n = 0
            for s, has in ((-1, ("prep",)), (0, ("max", "prep"))):
                step = Step(s, s, n, 0, has=has)
                do(step)
                n += len(step.uses)
            per = NB * len(full)
            assert per % RING == 0
            marks = [c.n for c in chains]
            rounds = (B - 2) // NB
            with eng.Fori(0, rounds) as i:
                for c in chains:
                    c.off = i * c.per
                for k in range(NB):
                    do(Step(i * NB + (1 + k), 1 + k, n + k * len(full), i * (per // RING), i))
            for c, m in zip(chains, marks):
                assert c.n - m == c.per, (tag, c.n - m)
                c.off, c.n = 0, m + rounds * c.per
            n += rounds * per
            for s, has in ((B - 1, ("max", "weights")), (B, ("weights",))):
                step = Step(s, s, n, 0, has=has)
                do(step)
                n += len(step.uses)

        def first_of(b, n):
            return isinstance(b, int) and b < n

        def start_next(st, start):
            if first_of(st.bp, 2):
                start(st.bp + 1)

        def split(eng, ch):
            ch.link(eng.tensor_copy(parts[:, :, 0, :], zl[:]))
            ch.link(eng.tensor_tensor(zu[:], zl[:], parts[:, :, 0, :], ALU.subtract))
            settle(eng, spare)
            ch.link(eng.tensor_copy(parts[:, :, 1, :], zu[:]))
            eng.tensor_tensor(parts[:, :, 2, :], zu[:], parts[:, :, 1, :], ALU.subtract).then_inc(parts_done, 1)

        def tiles(b, tt=0, n=TT):
            return slice(2 * b + tt, 2 * b + tt + n) if isinstance(b, int) else bass.ds(b * 2 + tt, n)

        with nc.Block() as block:

            @block.sync
            def _(sp):
                if not own:
                    for i in range(2):
                        sp.dma_start(ctxT[:, i, :], w["ctxT"][i]).then_inc(ctx_in[i], 16)

                def start(i):
                    sp.wait_ge(cleared[i], 2)
                    sp.dma_start(kst[i][STACK:STACK + 1], w["ones_row"]).then_inc(stack_in[i], 16)

                start(0)

                def do(st):
                    if st.bp is not None:
                        if not own and not first_of(st.bp, 2):
                            sp.wait_ge(parts_done, st.bp - (NB - 2))
                            settle(sp, spare)
                            sp.dma_start(ctxT[:, st.ip, :], w["ctxT"][st.bp]).then_inc(ctx_in[st.ip], 16)
                        sp.wait_ge(parts_done, st.bp + 2)
                        for t in range(2):
                            sp.dma_start(scratch[st.ip][t].rearrange("c p n -> p c n"),
                                         parts[:, t]).then_inc(scr_done, 16)
                        sp.wait_ge(scr_done, 32 * (st.bp + 1))
                        settle(sp, spare)
                        if not first_of(st.bp, NB):
                            sp.wait_ge(scores, UNITS * (st.bp - 2) + 1)
                        for a in range(PARTS):
                            rows = slice(a * PARTS * HD, (a + 1) * PARTS * HD)
                            src = scratch[st.ip][0, a].rearrange("(d h) n -> d (h n)", d=HD)
                            sp.dma_start(qst[st.ip][rows].rearrange("p h n -> p (h n)"),
                                         src.unsqueeze(0).broadcast_to([PARTS, HD, H * S]))\
                                .then_inc(stack_in[st.ip], 16)
                            src = scratch[st.ip][1].rearrange("c (d h) n -> (c d) (h n)", d=HD)
                            sp.dma_start(kst[st.ip][rows].rearrange("p h n -> p (h n)"), src)\
                                .then_inc(stack_in[st.ip], 16)
                        sp.dma_start(qst[st.ip][STACK:STACK + 1], w["zeros_row"]).then_inc(stack_in[st.ip], 16)
                    if st.bm is not None:
                        bank, k = st.ring["mT"]
                        sp.wait_ge(a_free[bank], k + 1)
                        sp.dma_start(qst[st.im][STACK:STACK + 1], nmT[:, :]).then_inc(mrow, 16)
                    start_next(st, start)

                walk(sp, do)

            @block.gpsimd
            def _(pool):
                for s, n in (*((free, 1) for free in a_free), (exp_done, 2), (pv_done, 2), (o_done, 1),
                             (parts_done, 1), (scores, 1)):
                    pool.sem_inc(s, n)
                pool.memset(nt.half[:, :], -0.5).then_inc(consts, 1)

                def start(i):
                    pool.memset(kst[i][:].bitcast(F32), 0.0).then_inc(cleared[i], 1)
                    pool.memset(V[i][:], 0.0).then_inc(v_clear, 1)
                    if not wide:
                        pool.wait_ge(v_clear, 2 * i + 1)
                        pool.memset(V[i][:, :, :, HD:HD + 1], 1.0).then_inc(v_clear, 1)

                start(0)
                ch = Chain(pool, pchain)
                ch.per = NB * 3

                def do(st):
                    if st.early:
                        held.wait(pool, tag)
                    if st.bp is not None and not first_of(st.bp, EARLY):
                        if own:
                            pool.wait_ge(leaky_done, st.bp + 1)
                        else:
                            for name in ("q", "k"):
                                bank, k = st.ring[name]
                                pool.wait_ge(a_free[bank], k + 1)
                        pool.wait_ge(scr_done, 32 * st.bp)
                        settle(pool, spare)
                        split(pool, ch)
                    if st.bw is not None:
                        other = x_all[:, tiles(st.bw), :] if own else bo[:, :].unsqueeze(1).broadcast_to([P, TT, D])
                        pool.tensor_tensor(xres[:, :, :], x_all[:, tiles(st.bw), :], other,
                                           ALU.add).then_inc(xres_done, 1)
                        pool.wait_ge(ve_done, st.bw + 1)
                        pool.tensor_tensor(nt.rstd[:, :], nt.ve[:, :], nt.half[:, :], ALU.pow).then_inc(rstd_done, 1)
                    start_next(st, start)

                walk(pool, do, [ch])

            @block.scalar
            def _(act):
                held.wait(act, tag)

                def take(st, name):
                    bank, k = st.ring[name]
                    act.wait_ge(a_full[bank], k)
                    return A[:, bank, :], a_free[bank]

                def exps(st, g):
                    for kt in range(TT):
                        act.wait_ge(scores, UNITS * st.bw + 2 * g + kt + 2)
                        act.wait_ge(pv_done, NG * st.bw + g + 1)
                        slot = (2 * g + kt) % 4
                        if causal and kt == 1:
                            src = Sc[:, kt, 0:GJ * P].rearrange("p (j q) -> p j q", j=GJ)
                            dst = E[:, slot, :, P:S]
                        else:
                            src = Sc[:, kt, :].rearrange("p (j q) -> p j q", j=GJ)
                            dst = E[:, slot, :, :]
                        act.activation(dst, src, ACT.Exp, scale=SCALE).then_inc(exp_done, 1)

                def keep(st, g):
                    act.wait_ge(pv_done, NG * st.bw + g + 3)
                    act.activation(Os[:, g], O[:, :, 0:S], ACT.Copy).then_inc(o_done, 1)

                def do(st):
                    if st.bp is not None and not first_of(st.bp, 2):
                        act.activation(xb[:, :, :], x_all[:, tiles(st.bp), :], ACT.Copy).then_inc(xb_done, 1)
                    for op, n in st.work:
                        if op == "key":
                            exps(st, n)
                        elif op == "values":
                            keep(st, n)
                        elif op == "x_turn":
                            src, done = take(st, "xT")
                            act.activation(xT[:, :], src[:, 0:S], ACT.Copy).then_inc(done, 1)
                        elif op in ("q", "k"):
                            t, bias = (0, bq) if op == "q" else (1, bk)
                            src, done = take(st, op)
                            act.wait_ge(parts_done, st.bp + 1)
                            act.activation(z[:, t, :], src[:, 0:S], ACT.Identity,
                                           bias=bias[:, 0:1] if has_bias else 0.0).then_inc(done, 1)
                        elif op == "max_row":
                            src, done = take(st, "mT")
                            act.wait_ge(mrow, 16 * st.bm)
                            act.activation(nmT[:, :], src[0:H, 0:S], ACT.Copy, scale=-1.0).then_inc(done, 1)
                    if st.early and tag == "b":
                        held.load(act, "c")

                walk(act, do)

            @block.vector
            def _(dve):
                def start(i):
                    dve.memset(qst[i][64:P].bitcast(F32), 0.0).then_inc(cleared[i], 1)
                    if i == NB - 1:
                        dve.wait_ge(v_clear, NB * (1 if wide else 2))

                start(0)
                held.wait(dve, tag)
                dve.wait_ge(consts, 1)
                ch = Chain(dve, chain)
                ch.per = NB * (4 if own else 2)
                if masked:
                    for n, m in enumerate((maskq, maskk)):
                        for c in range(2):
                            dve.tensor_scalar(m[:, :, c, :], mask32[:, n], 0, -BIG, ALU.is_equal,
                                              ALU.mult).then_inc(consts, 1)

                def take(st, name):
                    bank, k = st.ring[name]
                    dve.wait_ge(a_full[bank], k)
                    return A[:, bank, :], a_free[bank]

                def maxima(st, n):
                    for qt in range(TT):
                        src, done = take(st, f"m{n}{qt}")
                        keys = P if causal and qt == 0 else S
                        dve.tensor_reduce(mx[:, qt, 2 * n:2 * n + 2],
                                          src[:, 0:2 * keys].rearrange("p (h k) -> p h k", h=2),
                                          AX.X, ALU.max).then_inc(done, 1)

                def values(st, n):
                    if n == 0 and first_of(st.bp, 2):
                        dve.wait_ge(v_clear, (st.bp + 1) * (1 if wide else 2))
                    if wide:
                        vals = V[st.ip][:].rearrange("p t h v -> p t (h v)")
                        src, done = take(st, f"v{n}")
                        cols = slice(512 * (n % 2), 512 * (n % 2) + 512)
                        dve.tensor_tensor(zv[:, n // 2, cols], src, bv[:, cols], ALU.add).then_inc(done, 1)
                        dve.wait_ge(done, st.ring[f"v{n}"][1] + 1)
                        dve.scalar_tensor_tensor(vals[:, n // 2, cols], zv[:, n // 2, cols], 0.01,
                                                 zv[:, n // 2, cols], ALU.mult, ALU.max).then_inc(v_done, 1)
                    else:
                        src, done = take(st, "v0")
                        src = src[:, 0:S].rearrange("p (t h d) -> p t h d", t=TT, h=H)
                        for tt in range(TT):
                            dst = V[st.ip][:, tt, :, 0:HD]
                            if has_bias:
                                ins = dve.tensor_tensor(dst, src[:, tt], bv[:, :].rearrange("p (h d) -> p h d", h=H),
                                                        ALU.add)
                            else:
                                ins = dve.tensor_copy(dst, src[:, tt])
                        ins.then_inc(done, 1)

                def q_and_k(st):
                    if own or first_of(st.bp, EARLY):
                        for name in ("q", "k"):
                            bank, k = st.ring[name]
                            dve.wait_ge(a_free[bank], k + 1)
                    if own:
                        dve.scalar_tensor_tensor(zl[:], z[:], 0.01, z[:], ALU.mult, ALU.max).then_inc(leaky_done, 1)
                    if first_of(st.bp, EARLY):
                        if own:
                            dve.wait_ge(leaky_done, st.bp + 1)
                        if st.bp:
                            dve.wait_ge(scr_done, 32 * st.bp)
                        settle(dve, spare)
                        split(dve, ch)

                def divide(st):
                    for tt in range(TT):
                        src, done = take(st, f"b{tt}")
                        qs = slice(tt * P, (tt + 1) * P)
                        src = src.rearrange("p (g q) -> p g q", g=NG)
                        if C == 1:
                            dve.tensor_tensor(ON[:, :, 0, qs], Os[:, :, 0, qs], src, ALU.mult).then_inc(done, 1)
                        else:
                            dve.tensor_tensor(ON[:, :, :, qs], Os[:, :, :, qs],
                                              src.unsqueeze(2).broadcast_to([P, NG, C, P]), ALU.mult).then_inc(done, 1)

                def finish(st):
                    dve.wait_ge(xres_done, st.bw + 1)
                    for n in range(NO):
                        src, done = take(st, f"out{n}")
                        tts = slice(n * TT // NO, (n + 1) * TT // NO)
                        src = src[:, 0:TT // NO * D].rearrange("p (t d) -> p t d", d=D)
                        if own:
                            boc = bo[:, :].unsqueeze(1).broadcast_to([P, TT // NO, D])
                            dve.tensor_tensor(res[:, tts], src, boc, ALU.add).then_inc(done, 1)
                        else:
                            dve.tensor_tensor(nt.r[:, tts], src, xres[:, tts], ALU.add).then_inc(done, 1)
                    for n in range(NO):
                        bank, k = st.ring[f"out{n}"]
                        dve.wait_ge(a_free[bank], k + 1)
                    if own:
                        ch.link(dve.scalar_tensor_tensor(nt.r[:], res[:], 0.01, res[:], ALU.mult, ALU.max))
                        ch.link(dve.tensor_tensor(nt.r[:], nt.r[:], xres[:], ALU.add))
                    norm_stats(dve, ch.link, nt, ve_done, spare)
                    dve.wait_ge(rstd_done, st.bw + 1)
                    for tt in range(TT):
                        norm_apply(dve, nt, x_all[:, tiles(st.bw, tt, 1), :].squeeze(1), tt).then_inc(x_done, 1)

                def do(st):
                    for op, n in st.work:
                        if op == "max":
                            maxima(st, n)
                        elif op == "value":
                            values(st, n)
                        elif op == qk_last:
                            q_and_k(st)
                        elif op == "sums":
                            dve.wait_ge(zc_full, st.bw + 1)
                            for tt in range(TT):
                                qs = slice(tt * P, (tt + 1) * P)
                                dve.reciprocal(Rz[:, qs], Zc[:, qs]).then_inc(rz_done, 1)
                        elif op == "spread":
                            divide(st)
                        elif op == "output":
                            finish(st)
                    start_next(st, start)

                walk(dve, do, [ch])

            @block.tensor
            def _(pe):
                held.wait(pe, "shared")
                held.wait(pe, tag)

                def use(st, name):
                    bank, k = st.ring[name]
                    pe.wait_ge(a_free[bank], k)
                    return A[:, bank, :], a_full[bank]

                def maxima(st, n):
                    q, k = qst[st.im], kst[st.im]
                    if n == 0:
                        pe.wait_ge(stack_in[st.im], 16 * LOADS * st.um + 16)
                    for qt in range(TT):
                        dst, done = use(st, f"m{n}{qt}")
                        keys = P if causal and qt == 0 else S
                        for c in range(2):
                            mm = pe.matmul(dst[:, c * keys:(c + 1) * keys], q[:, 2 * n + c, qt * P:(qt + 1) * P],
                                           k[:, 2 * n + c, 0:keys], start=c == 0,
                                           stop=not (masked or causal) and c == 1, skip_group_check=True)
                        if masked:
                            mm = pe.matmul(dst[:, 0:2 * S], identb[:, :],
                                           maskq[:, qt].rearrange("p c k -> p (c k)"), start=False, stop=True,
                                           skip_group_check=True)
                        if causal:
                            mm = pe.matmul(dst[:, 0:2 * keys].rearrange("p (c k) -> p c k", c=2)[:, :, keys - P:keys],
                                           identb[:, :], maskq[:, qt], start=False, stop=True,
                                           skip_group_check=True)
                        mm.then_inc(done, 1)

                def by_key(st, g):
                    q, k = qst[st.iw], kst[st.iw]
                    if g == 0:
                        pe.wait_ge(mrow, 16 * (st.bw + 1))
                    for kt in range(TT):
                        pe.wait_ge(exp_done, UNITS * st.bw + 2 * g + kt + 1)
                        short = causal and kt == 1
                        nq = P if short else S
                        for bank in range(1 if short else 2):
                            heads = range(GJ) if short else range(2 * bank, 2 * bank + 2)
                            dst = Sc[:, kt, 512 * bank:512 * bank + 512]
                            for n, j in enumerate(heads):
                                mm = pe.matmul(dst[:, n * nq:(n + 1) * nq],
                                               k[:, GJ * g + j, kt * P:(kt + 1) * P],
                                               q[:, GJ * g + j, S - nq:S], start=n == 0,
                                               stop=not (masked or causal) and j == heads[-1], skip_group_check=True)
                            if masked:
                                mm = pe.matmul(dst, identb[:, :], maskk[:, kt].rearrange("p c q -> p (c q)"),
                                               start=False, stop=True, skip_group_check=True)
                            if causal:
                                d3 = dst.rearrange("p (n q) -> p n q", n=len(heads))
                                for n in range(0, len(heads), 2):
                                    mm = pe.matmul(d3[:, n:n + 2, 0:P], identb[:, :], maskk[:, kt],
                                                   start=False, stop=n + 2 == len(heads), skip_group_check=True)
                        mm.then_inc(scores, 1)

                def outputs(st, g):
                    if g == 0 and wide:
                        pe.wait_ge(v_done, NV * (st.bw + 1))
                    pe.wait_ge(o_done, NG * st.bw + g + 1)
                    for kt in range(TT):
                        pe.wait_ge(exp_done, UNITS * st.bw + 2 * g + kt + 3)
                        slot = (2 * g + kt) % 4
                        q0 = P if causal and kt == 1 else 0
                        for c in range(C):
                            for j in range(GJ):
                                mm = pe.matmul(O[32 * j:32 * j + 32, c, q0:S],
                                               V[st.iw][:, kt, GJ * g + j, 32 * c:32 * c + 32],
                                               E[:, slot, j, q0:S], start=kt == 0 and c == 0, stop=kt == 1,
                                               skip_group_check=True)
                        if wide:
                            for j in range(GJ):
                                mm = pe.matmul(Zc[32 * j:32 * j + 32, 0:S], collect[:, g, :], E[:, slot, j, :],
                                               start=g == 0 and kt == 0, stop=g == NG - 1 and kt == 1,
                                               skip_group_check=True)
                    mm.then_inc(pv_done, 1)

                def denominators(st):
                    pe.wait_ge(o_done, NG * (st.bw + 1) + 1)
                    if wide:
                        pe.sem_inc(zc_full, 1)
                        return
                    for g in range(NG):
                        mm = pe.matmul(Zc[:, 0:S], collect[:, g, :], Os[:, g, 0, :], start=g == 0, stop=g == NG - 1)
                    mm.then_inc(zc_full, 1)

                def reciprocals(st):
                    for tt in range(TT):
                        pe.wait_ge(rz_done, st.bw * 2 + (tt + 1))
                        dst, done = use(st, f"b{tt}")
                        for g in range(NG):
                            mm = pe.matmul(dst[:, g * P:(g + 1) * P], spread[:, g, :], Rz[:, tt * P:(tt + 1) * P],
                                           start=True, stop=True)
                        mm.then_inc(done, 1)

                def turn(st):
                    bank, k = st.ring[f"m{H // 2 - 1}{TT - 1}"]
                    pe.wait_ge(a_free[bank], k + 1)
                    dst, done = use(st, "mT")
                    for qt in range(TT):
                        mm = pe.transpose(dst[0:H, qt * P:(qt + 1) * P], mx[:, qt, :], ident[:, :])
                    mm.then_inc(done, 1)

                def turn_x(st):
                    src = xb
                    if first_of(st.bp, 2):
                        src = x_all[:, tiles(st.bp), :]
                    else:
                        pe.wait_ge(xb_done, st.bp - 1)
                    dst, done = use(st, "xT")
                    for tt in range(TT):
                        mm = pe.transpose(dst[:, tt * P:(tt + 1) * P], src[:, tt, :], ident[:, :])
                    mm.then_inc(done, 1)

                def source(st):
                    bank, k = st.ring["xT"]
                    pe.wait_ge(a_free[bank], k + 1)
                    if own:
                        return xT[:, :]
                    pe.wait_ge(ctx_in[st.ip], 16 * st.up)
                    return ctxT[:, st.ip, :]

                def project_values(st, n):
                    kv = source(st)
                    dst, done = use(st, f"v{n}")
                    if wide:
                        mm = pe.matmul(dst, kv[:, (n // 2) * P:(n // 2 + 1) * P],
                                       wv[:, 512 * (n % 2):512 * (n % 2) + 512], start=True, stop=True)
                    else:
                        for tt in range(TT):
                            mm = pe.matmul(dst[:, tt * D:(tt + 1) * D], kv[:, tt * P:(tt + 1) * P], wv[:, :],
                                           start=True, stop=True)
                    mm.then_inc(done, 1)

                def project_q(st):
                    bank, k = st.ring["xT"]
                    pe.wait_ge(a_free[bank], k + 1)
                    dst, done = use(st, "q")
                    pe.matmul(dst[:, 0:S], wq[:, :], xT[:, :], start=True, stop=True).then_inc(done, 1)

                def project_k(st):
                    kv = source(st)
                    dst, done = use(st, "k")
                    pe.matmul(dst[:, 0:S], wk[:, :], kv, start=True, stop=True).then_inc(done, 1)

                def output(st):
                    for tt in range(TT):
                        bank, k = st.ring[f"b{tt}"]
                        pe.wait_ge(a_free[bank], k + 1)
                        if tt % (TT // NO) == 0:
                            dst, done = use(st, f"out{tt // (TT // NO)}")
                        at = tt % (TT // NO)
                        for n in range(NG * C):
                            mm = pe.matmul(dst[:, at * D:(at + 1) * D], ON[:, n // C, n % C, tt * P:(tt + 1) * P],
                                           wo[:, n, :], start=n == 0, stop=n == NG * C - 1, skip_group_check=True)
                        if tt % (TT // NO) == TT // NO - 1:
                            mm.then_inc(done, 1)

                work = {"max": maxima, "key": by_key, "values": outputs, "value": project_values}
                single = {"x_turn": turn_x, "q": project_q, "k": project_k, "sums": denominators, "spread": reciprocals,
                          "max_row": turn, "output": output}

                def do(st):
                    for op, n in st.work:
                        if st.early and (op, n) == ("max", 0):
                            pe.wait_ge(consts, 1 + (4 if masked else 0))
                        if op in work:
                            work[op](st, n)
                        else:
                            single[op](st)

                walk(pe, do)


def moe(nc, x_all, w, held):
    NE, NP_ = 64, 32
    SL = NE * NP_
    CH = SL // P
    EC = P // NP_
    QT = 4
    NQ = CH // QT
    with ExitStack() as outer:
        so = Scope(nc, outer, "c")
        phi, eb, ident = held["c_phi"], held["c_b"], held["ident"]
        xT = so.sb("xT", [P, B, S])
        yall = so.sb("yall", [P, CH, B, D + 1])
        top = so.sb("top", [P, B, S])
        top_dram = nc.dram_tensor("c_top_dram", (B, TT, P), F32).ap()

        with ExitStack() as ctx:
            sc = Scope(nc, ctx, "c1")
            We = [sc.sb(f"We{i}", [P, EC, D]) for i in range(2)]
            E = sc.sb("E", [P, 2, TT, B, P])
            M = sc.sb("M", [P, TT, P])
            Zs = sc.sb("Zs", [P, TT, P])
            half_sum = sc.sb("half_sum", [P, TT, B // 2, P])
            Rz = sc.sb("Rz", [P, TT, P])
            slots = sc.sb("slots", [P, B, P])
            pm = sc.sb("pm", [P, TT, B, CH])
            R = sc.sb("R", [P, TT, B])
            RT = sc.sb("RT", [TT * B, P])
            L = sc.ps("L", [P, TT, B, P])
            ST = sc.ps("ST", [P, B, P])
            Y = sc.ps("Y", [P, B, P])
            e_in = [sc.sem(f"e_in{i}") for i in range(2)]
            xt_full, xt_done = sc.sem("xt_full"), sc.sem("xt_done")
            consts = sc.sem("consts")
            l_full = sc.sem("l_full")
            shifted, l_free = sc.sem("shifted"), sc.sem("l_free")
            exp_done = sc.sem("exp_done")
            zs_done, pchain = sc.sem("zs_done"), sc.sem("pchain")
            rz_done = sc.sem("rz_done")
            weights_done = sc.sem("weights_done")
            st_full, st_done = sc.sem("st_full"), sc.sem("st_done")
            y_full, y_done = sc.sem("y_full"), sc.sem("y_done")
            chain = sc.sem("chain")
            r_done, rt_full, rt_done, row_in = (sc.sem(n) for n in ("r_done", "rt_full", "rt_done", "row_in"))
            spare = sc.sem("spare")

            with nc.Block() as block:

                def loop(eng, do, chain=None):
                    do(0, 0, 2, False)
                    do(1, 1, 2, True)
                    n = chain.n if chain else 0
                    with eng.Fori(0, (CH - 4) // 2) as i:
                        if chain:
                            chain.off = i * chain.per
                        do(i * 2 + 2, 0, 2, True)
                        do(i * 2 + 3, 1, 2, True)
                    if chain:
                        assert chain.n - n == chain.per, chain.n - n
                        chain.off, chain.n = 0, n + chain.per * (CH - 4) // 2
                    do(CH - 2, 0, 1, True)
                    do(CH - 1, 1, 0, True)

                @block.sync
                def _(sp):
                    def do(c, par, more, before):
                        experts = slice(0, EC) if isinstance(c, int) and c == 0 else \
                            slice(EC * c, EC * c + EC) if isinstance(c, int) else bass.ds(c * EC, EC)
                        if before:
                            sp.wait_ge(y_full, c)
                            settle(sp, spare)
                        sp.dma_start(We[par][:], w["c_W"][:, experts, :]).then_inc(e_in[par], 16)
                    loop(sp, do)
                    sp.wait_ge(rt_done, 1)
                    for tt in range(TT):
                        sp.dma_start(top_dram[:, tt, :], RT[tt * B:(tt + 1) * B, :]).then_inc(row_in, 16)
                    sp.wait_ge(row_in, 32)
                    sp.dma_start(top[:].rearrange("p b n -> p (b n)"),
                                 top_dram.rearrange("b t n -> (b t n)").partition_broadcast(P)).then_inc(row_in, 16)
                    sp.wait_ge(row_in, 48)

                @block.gpsimd
                def _(pool):
                    pool.sem_inc(y_full, 1)
                    pool.memset(yall[:, :, :, D:D + 1], 1.0).then_inc(consts, 1)

                    ch = Chain(pool, pchain)
                    ch.per = 2 * 4

                    def do(c, par, more, before):
                        for tt in range(TT):
                            pool.wait_ge(exp_done, c * 2 + (tt + 1))
                            e = E[:, par, tt]
                            ch.link(pool.tensor_tensor(half_sum[:, tt], e[:, 0:4], e[:, 4:8], ALU.add))
                            ch.link(pool.tensor_tensor(half_sum[:, tt, 0:2], half_sum[:, tt, 0:2],
                                                       half_sum[:, tt, 2:4], ALU.add))
                            pool.tensor_tensor(Zs[:, tt, :], half_sum[:, tt, 0], half_sum[:, tt, 1],
                                               ALU.add).then_inc(zs_done, 1)
                        for tt in range(TT):
                            pool.wait_ge(rz_done, c * 2 + (tt + 1))
                            pool.tensor_tensor(E[:, par, tt], E[:, par, tt],
                                               Rz[:, tt, :].unsqueeze(1).broadcast_to([P, B, P]),
                                               ALU.mult).then_inc(weights_done, 1)
                    loop(pool, do, ch)

                @block.scalar
                def _(act):
                    LATER = {1: "d", CH - 2: "e", CH - 1: "f"}
                    for n in range(4):
                        act.wait_ge(xt_full, n + 1)
                        act.activation(xT[:, 2 * n:2 * n + 2, :],
                                       L[:].rearrange("p t b n -> p (t b n)")[:, 512 * n:512 * n + 512]
                                       .rearrange("p (b m) -> p b m", b=2), ACT.Copy).then_inc(xt_done, 1)

                    def exps(c, par):
                        for tt in range(TT):
                            act.wait_ge(shifted, c * 2 + (tt + 1))
                            act.activation(E[:, par, tt], E[:, par, tt], ACT.Exp).then_inc(exp_done, 1)

                    exps(0, 0)

                    def do(c, par, more, before):
                        if more:
                            exps(c + 1, 1 - par)
                        if more == 0:
                            act.wait_ge(rt_full, 1)
                            act.activation(RT[:, :], L[0:TT * B, 0, 0, :], ACT.Copy).then_inc(rt_done, 1)
                        act.wait_ge(st_full, c + 1)
                        if before:
                            act.wait_ge(y_full, c + 1)
                        act.activation(slots[:], ST[:], ACT.Copy).then_inc(st_done, 1)
                        if isinstance(c, int) and c in LATER:
                            held.load(act, LATER[c])
                    loop(act, do)

                @block.vector
                def _(dve):
                    ch = Chain(dve, chain)
                    ch.per = 2 * 2

                    def shift(c, par):
                        for tt in range(TT):
                            dve.wait_ge(l_full, c * 2 + (tt + 1))
                            src = L[:, tt]
                            ch.link(dve.tensor_reduce(M[:, tt, :], src.rearrange("p b n -> p n b"), AX.X, ALU.max))
                            dve.tensor_tensor(E[:, par, tt], src, M[:, tt, :].unsqueeze(1).broadcast_to([P, B, P]),
                                              ALU.subtract).then_inc(shifted, 1)
                            dve.tensor_reduce(pm[:, tt, :, c] if isinstance(c, int)
                                              else pm[:, tt, :, bass.ds(c, 1)].squeeze(2),
                                              src, AX.X, ALU.max).then_inc(l_free, 1)

                    shift(0, 0)
                    held.wait(dve, "c")

                    def evacuate(c):
                        dve.wait_ge(y_full, c + 2)
                        if isinstance(c, int):
                            dst, bias = yall[:, c, :, 0:D], eb[:, c, :]
                        else:
                            dst, bias = yall[:, bass.ds(c, 1), :, 0:D].squeeze(1), eb[:, bass.ds(c, 1), :].squeeze(1)
                        dve.tensor_tensor(dst, Y[:], bias.unsqueeze(1).broadcast_to([P, B, D]),
                                          ALU.add).then_inc(y_done, 1)

                    def do(c, par, more, before):
                        for tt in range(TT):
                            dve.wait_ge(zs_done, c * 2 + (tt + 1))
                            if before:
                                dve.wait_ge(weights_done, c * 2 + (tt - 1))
                                settle(dve, spare)
                            dve.reciprocal(Rz[:, tt, :], Zs[:, tt, :]).then_inc(rz_done, 1)
                        if more:
                            if before:
                                dve.wait_ge(st_full, c)
                            shift(c + 1, 1 - par)
                        if more == 1:
                            dve.wait_ge(l_free, 2 * CH)
                            dve.tensor_reduce(R[:], pm[:], AX.X, ALU.max).then_inc(r_done, 1)
                        if before:
                            evacuate(c - 1)
                    loop(dve, do, ch)
                    evacuate(CH - 1)

                @block.tensor
                def _(pe):
                    held.wait(pe, "shared")
                    held.wait(pe, "c")
                    flat = L[:].rearrange("p t b n -> p (t b n)")
                    for n in range(4):
                        for k in range(4):
                            mm = pe.transpose(flat[:, 512 * n + P * k:512 * n + P * k + P],
                                              x_all[:, 4 * n + k, :], ident[:, :])
                        mm.then_inc(xt_full, 1)
                    pe.wait_ge(xt_done, 4)

                    def logits(c, before):
                        cols = slice(c * P, c * P + P) if isinstance(c, int) else bass.ds(c * P, P)
                        for tt in range(TT):
                            if before:
                                pe.wait_ge(l_free, c * 2 + (tt - 1))
                            for b in range(B):
                                mm = pe.matmul(L[:, tt, b, :], xT[:, b, tt * P:(tt + 1) * P], phi[:, cols],
                                               start=True, stop=True)
                            mm.then_inc(l_full, 1)

                    logits(0, False)
                    logits(1, True)

                    def do(c, par, more, before):
                        if more == 0:
                            pe.wait_ge(r_done, 1)
                            pe.transpose(L[0:TT * B, 0, 0, :], R[:].rearrange("p t b -> p (t b)"),
                                         ident[:, :]).then_inc(rt_full, 1)
                        pe.wait_ge(weights_done, c * 2 + 2)
                        if before:
                            pe.wait_ge(st_done, c)
                        for b in range(B):
                            for tt in range(TT):
                                mm = pe.matmul(ST[:, b, :], x_all[:, 2 * b + tt, :], E[:, par, tt, b, :],
                                               start=tt == 0, stop=tt == TT - 1)
                        mm.then_inc(st_full, 1)
                        if more == 2:
                            logits(c + 2, True)
                        pe.wait_ge(st_done, c + 1)
                        if before:
                            pe.wait_ge(y_done, c)
                        pe.wait_ge(e_in[par], 16 * (c // 2 + 1) if isinstance(c, int) else c * 8 + (16 - 8 * par))
                        for b in range(B):
                            for n in range(EC):
                                mm = pe.matmul(Y[NP_ * n:NP_ * n + NP_, b, :], slots[:, b, NP_ * n:NP_ * n + NP_],
                                               We[par][:, n, :], start=True, stop=True, skip_group_check=True)
                        mm.then_inc(y_full, 1)
                    loop(pe, do)

        with ExitStack() as ctx:
            sc = Scope(nc, ctx, "c2")
            CE = sc.sb("CE", [P, NQ, QT, S])
            rz = sc.sb("rz", [P, TT])
            nt = NormTiles(sc)
            LT = sc.ps("LT", [P, 2, QT, S])
            O = sc.ps("O", [P, TT, D + 1])
            consts = sc.sem("consts")
            l_full, shifted, exp_done, used = (sc.sem(n) for n in ("l_full", "shifted", "exp_done", "used"))
            o_done = sc.sem("o_done")
            rz_done, ve_done, rstd_done, x_done = (sc.sem(n) for n in ("rz_done", "ve_done", "rstd_done", "x_done"))
            chain, spare = sc.sem("chain"), sc.sem("spare")
            with nc.Block() as block:

                @block.gpsimd
                def _(pool):
                    pool.memset(nt.half[:, :], -0.5).then_inc(consts, 1)
                    pool.wait_ge(consts, 1)
                    pool.sem_inc(shifted, 2)
                    pool.sem_inc(used, NQ)
                    pool.sem_inc(o_done, 2)
                    with pool.Fori(0, B) as b:
                        pool.wait_ge(ve_done, b + 1)
                        pool.tensor_tensor(nt.rstd[:, :], nt.ve[:, :], nt.half[:, :], ALU.pow).then_inc(rstd_done, 1)

                @block.scalar
                def _(act):
                    with act.Fori(0, B) as b:
                        for q in range(NQ):
                            act.wait_ge(shifted, b * NQ + (q + 3))
                            act.activation(CE[:, q], CE[:, q], ACT.Exp).then_inc(exp_done, 1)

                def loop(eng, start, do, chain=None):
                    start()
                    with eng.Fori(0, B - 1) as b:
                        if chain:
                            chain.off = b * chain.per
                        do(b, True)
                    if chain:
                        assert chain.n == chain.per, chain.n
                        chain.off, chain.n = (B - 1) * chain.per, 0
                    do(B - 1, False)

                def of_batch(t, b):
                    return t[:, b] if isinstance(b, int) else t[:, bass.ds(b, 1)].squeeze(1)

                def tile(b, tt):
                    if isinstance(b, int):
                        return x_all[:, 2 * b + tt, :]
                    return x_all[:, bass.ds(b * 2 + tt, 1), :].squeeze(1)

                @block.vector
                def _(dve):
                    ch = Chain(dve, chain)
                    ch.per = 3

                    def shift(b, q):
                        dve.wait_ge(l_full, b * NQ + (q + 1))
                        dve.wait_ge(used, b * NQ + (q + 1))
                        dve.tensor_tensor(CE[:, q], LT[:, q % 2],
                                          of_batch(top, b).unsqueeze(1).broadcast_to([P, QT, S]),
                                          ALU.subtract).then_inc(shifted, 1)

                    def start():
                        dve.wait_ge(consts, 1)
                        shift(0, 0)
                        shift(0, 1)

                    def do(b, more):
                        shift(b, 2)
                        shift(b, 3)
                        if more:
                            shift(b + 1, 0)
                        dve.wait_ge(used, b * NQ + 2 * NQ)
                        ch.link(dve.reciprocal(rz[:, :], O[:, :, D]))
                        for tt in range(TT):
                            dve.scalar_tensor_tensor(nt.r[:, tt, :], O[:, tt, 0:D], rz[:, tt:tt + 1], tile(b, tt),
                                                     ALU.mult, ALU.add).then_inc(o_done, 1)
                        if more:
                            shift(b + 1, 1)
                        dve.wait_ge(o_done, b * 2 + 4)
                        settle(dve, spare)
                        norm_stats(dve, ch.link, nt, ve_done, spare)
                        dve.wait_ge(rstd_done, b + 1)
                        for tt in range(TT):
                            norm_apply(dve, nt, tile(b, tt), tt).then_inc(x_done, 1)
                    loop(dve, start, do, ch)

                @block.tensor
                def _(pe):
                    def logits(b, q):
                        pe.wait_ge(shifted, b * NQ + (q + 1))
                        for n in range(QT):
                            t = QT * q + n
                            mm = pe.matmul(LT[:, q % 2, n, :], phi[:, t * P:(t + 1) * P], of_batch(xT, b),
                                           start=True, stop=True)
                        mm.then_inc(l_full, 1)

                    def outputs(b, q):
                        pe.wait_ge(exp_done, b * NQ + (q + 1))
                        if q == 0:
                            pe.wait_ge(o_done, b * 2 + 2)
                        for n in range(QT):
                            t = QT * q + n
                            for tt in range(TT):
                                mm = pe.matmul(O[:, tt, :], CE[:, q, n, tt * P:(tt + 1) * P], of_batch(yall[:, t], b),
                                               start=t == 0 and tt == 0, stop=t == CH - 1, skip_group_check=True)
                        mm.then_inc(used, 1)

                    def start():
                        logits(0, 0)
                        logits(0, 1)

                    def do(b, more):
                        outputs(b, 0)
                        logits(b, 2)
                        outputs(b, 1)
                        logits(b, 3)
                        outputs(b, 2)
                        if more:
                            logits(b + 1, 0)
                        outputs(b, 3)
                        if more:
                            logits(b + 1, 1)
                    loop(pe, start, do)


def mlstm(nc, x_all, w, held):
    NH, DQ, DV = 8, 8, 16
    BH = B * NH
    CAP = 15.0
    EPS_H = 1e-6
    NGA = NH // GJ
    VC = 32
    with ExitStack() as outer:
        so = Scope(nc, outer, "a")
        bT = so.sb("bT", [P, TT, BH])
        emT = so.sb("emT", [P, TT, BH])
        ident = so.sb("ident", [P, P])
        g_dram = nc.dram_tensor("a_g", (BH, S), F32).ap()
        wq, wk = so.sb("wq", [P, NGA, P]), so.sb("wk", [P, NGA, P])
        wvo = so.sb("wvo", [P, 2 * D])
        wout = so.sb("wout", [P, D])
        lnw, lnb = so.sb("lnw", [P, D]), so.sb("lnb", [P, D])
        mask = so.sb("mask", [P, P])
        loads = [(wvo, w["a_wvo"]), (wq, w["a_wq"]), (wk, w["a_wk"]), (mask, w["a_mask"]),
                 (wout, w["a_wout"]), (lnw, w["a_lnw"].partition_broadcast(P)),
                 (lnb, w["a_lnb"].partition_broadcast(P))]
        later_in = so.sem("later_in")

        with ExitStack() as ctx:
            sc = Scope(nc, ctx, "a1")
            xT = sc.sb("xT", [P, B, S])
            wg = sc.sb("wg", [P, 2, B, BH])
            gb = sc.sb("gb", [BH, 2])
            pre = sc.sb("pre", [BH, 2, S])
            gate = sc.sb("gate", [BH, 2, S])
            zero = sc.sb("zero", [BH, S])
            F = sc.sb("F", [BH, S])
            bg = sc.sb("bg", [BH, S])
            g = sc.sb("g", [BH, S])
            m = sc.sb("m", [BH, S])
            em = sc.sb("em", [BH, S])
            G = sc.ps("G", [BH, 2, 512])
            T = sc.ps("T", [P, 2, TT, BH])
            w_in, x_in, g_full, pre_done, tanh_done, chain, g_done, m_done, em_done, t_full, t_done, g_out, consts = (
                sc.sem(n) for n in ("w_in", "x_in", "g_full", "pre_done", "tanh_done", "chain", "g_done", "m_done",
                                    "em_done", "t_full", "t_done", "g_out", "consts"))
            xT_in = [sc.sem(f"xT_in{n}") for n in range(4)]
            gb_in = sc.sem("gb_in")
            with nc.Block() as block:

                @block.sync
                def _(sp):
                    sp.dma_start(wg[:], w["a_wg"]).then_inc(w_in, 16)
                    for n in range(4):
                        pair = slice(2 * n, 2 * n + 2)
                        sp.dma_start(xT[:, pair, :], w["xT"][pair].rearrange("b d n -> d b n")).then_inc(xT_in[n], 16)
                    sp.dma_start(gb[:, :], w["a_gb"]).then_inc(gb_in, 16)
                    sp.dma_start(ident[:, :], w["ident"]).then_inc(gb_in, 16)
                    for dst, src in loads:
                        sp.dma_start(dst[:], src).then_inc(later_in, 16)
                    sp.dma_start(x_all[:], w["x"]).then_inc(x_in, 16)
                    sp.wait_ge(g_done, 1)
                    sp.dma_start(g_dram, g[:, :]).then_inc(g_out, 16)
                    sp.wait_ge(g_out, 16)
                    sp.wait_ge(x_in, 16)

                @block.tensor
                def _(pe):
                    pe.wait_ge(w_in, 16)
                    for b in range(B):
                        if b % 2 == 0:
                            pe.wait_ge(xT_in[b // 2], 16)
                        for k in range(2):
                            mm = pe.matmul(G[:, k, 0:S], wg[:, k, b, :], xT[:, b, :], start=b == 0, stop=b == B - 1)
                    mm.then_inc(g_full, 1)
                    pe.wait_ge(gb_in, 32)
                    pe.wait_ge(g_done, 1)
                    for tt in range(TT):
                        mm = pe.transpose(T[:, 0, tt, :], bg[:, tt * P:(tt + 1) * P], ident[0:BH, 0:BH])
                    pe.wait_ge(em_done, 1)
                    for tt in range(TT):
                        mm = pe.transpose(T[:, 1, tt, :], em[:, tt * P:(tt + 1) * P], ident[0:BH, 0:BH])
                    mm.then_inc(t_full, 1)

                @block.vector
                def _(dve):
                    ch = Chain(dve, chain)
                    ch.link(dve.memset(zero[:, :], 0.0))
                    dve.wait_ge(gb_in, 32)
                    dve.wait_ge(g_full, 1)
                    for k in range(2):
                        dve.tensor_scalar(pre[:, k, :], G[:, k, 0:S], gb[:, k:k + 1], 1.0 / CAP, ALU.add,
                                          ALU.mult).then_inc(pre_done, 1)
                    dve.wait_ge(tanh_done, 1)
                    ch.link(dve.tensor_scalar(gate[:], gate[:], CAP, None, ALU.mult))
                    ch.link(dve.tensor_tensor_scan(F[:, :], gate[:, 1, :], zero[:, :], 0.0, ALU.add, ALU.add))
                    ch.link(dve.tensor_tensor(bg[:, :], gate[:, 0, :], F[:, :], ALU.subtract))
                    dve.tensor_tensor_scan(g[:, :], bg[:, :], bg[:, :], 0.0, ALU.max, ALU.max).then_inc(g_done, 1)
                    dve.wait_ge(g_done, 1)
                    dve.tensor_tensor(m[:, :], g[:, :], F[:, :], ALU.add).then_inc(m_done, 1)
                    dve.wait_ge(t_full, 1)
                    dve.tensor_copy(bT[:], T[:, 0]).then_inc(t_done, 1)
                    dve.tensor_copy(emT[:], T[:, 1]).then_inc(t_done, 1)

                @block.scalar
                def _(act):
                    act.wait_ge(pre_done, 2)
                    act.activation(gate[:], pre[:], ACT.Tanh).then_inc(tanh_done, 1)
                    act.wait_ge(m_done, 1)
                    act.activation(em[:, :], m[:, :], ACT.Exp, scale=-1.0).then_inc(em_done, 1)

        with ExitStack() as ctx:
            sc = Scope(nc, ctx, "a2")
            q, kx = sc.sb("q", [P, NGA, S]), sc.sb("kx", [P, NGA, GJ, S])
            xT = sc.sb("xT", [P, 2, S])
            bs = sc.sb("bs", [P, 2, TT, NH])
            V = sc.sb("V", [P, 2, TT, NH, VC])
            sg = sc.sb("sg", [P, 2, TT, D])
            W = [sc.sb(f"W{i}", [P, NH, S + P]) for i in range(2)]
            Os = sc.sb("Os", [P, NGA, S])
            den = sc.sb("den", [P, TT, NH])
            rden = sc.sb("rden", [P, TT, NH])
            hn = sc.sb("hn", [P, TT, D])
            hT = sc.sb("hT", [P, S])
            ht = NormTiles(sc)
            nt = NormTiles(Scope(nc, ctx, "a3"))
            X = sc.ps("X", [P, 2, 512])
            S0 = sc.ps("S0", [P, NH, S])
            S1 = sc.ps("S1", [P, NH, P])
            x_full = [sc.sem(f"x_full{i}") for i in range(2)]
            x_free = [sc.sem(f"x_free{i}") for i in range(2)]
            x_in = [sc.sem(f"x_in{i}") for i in range(2)]
            g_in = [sc.sem(f"g_in{i}") for i in range(2)]
            (consts, cleared, kx_clear, bs_done, arg_done, w_done, s_full, p_done, chain, h_ve, h_rstd,
             h_done, kept, hT_done, ve_done, rstd_done, x_done, spare) = (sc.sem(n) for n in (
                 "consts", "cleared", "kx_clear", "bs_done", "arg_done", "w_done", "s_full",
                 "p_done", "chain", "h_ve", "h_rstd", "h_done", "kept", "hT_done", "ve_done", "rstd_done",
                 "x_done", "spare"))

            roles = {"decay": 0, "values": 1, "q": 1, "k": 1, "scores": 1, "outputs": 2, "by_token": 2, "head_norm": 2,
                     "turn": 2, "result": 3, "apply": 3}
            ring_of = {"values", "q", "k", "outputs", "by_token", "turn", "result"}

            class Step:
                def __init__(self, s, turn, first, off, stages=(0, 1, 2, 3)):
                    self.b = [s + 1, s, s - 1, s - 2]
                    self.par = [(turn + 1) % 2, turn % 2, (turn + 1) % 2, turn % 2]
                    self.work = [op for op, _ in PLANS["a"] if roles[op] in stages]
                    self.uses = [op for op in self.work if op in ring_of]
                    self.ring = ring_uses(self.uses, first, off)

            def walk(eng, do, chain=None):
                n = 0
                for s, stages in ((-1, (0,)), (0, (0, 1)), (1, (0, 1, 2)), (2, (0, 1, 2, 3))):
                    step = Step(s, s, n, 0, stages)
                    do(step)
                    n += len(step.uses)
                mark = chain.n if chain else 0
                rounds, per = (B - 4) // 2, 2 * len(ring_of)
                with eng.Fori(0, rounds) as i:
                    if chain:
                        chain.off = i * chain.per
                    for k in range(2):
                        do(Step(i * 2 + (3 + k), 3 + k, n + k * len(ring_of), i * (per // 2)))
                if chain:
                    assert chain.n - mark == chain.per, chain.n - mark
                    chain.off, chain.n = 0, mark + rounds * chain.per
                n += rounds * per
                for s, stages in ((B - 1, (1, 2, 3)), (B, (2, 3)), (B + 1, (3,))):
                    step = Step(s, s, n, 0, stages)
                    do(step)
                    n += len(step.uses)

            def need(eng, sem, count):
                if not (isinstance(count, int) and count <= 0):
                    eng.wait_ge(sem, count)

            def tiles(b, tt=0, n=TT):
                return slice(2 * b + tt, 2 * b + tt + n) if isinstance(b, int) else bass.ds(b * 2 + tt, n)

            def rows_of(b):
                return slice(NH * b, NH * b + NH) if isinstance(b, int) else bass.ds(b * NH, NH)

            def use_no(b, par):
                return 16 * (b // 2 + 1) if isinstance(b, int) else b * 8 + (16 - 8 * par)

            with nc.Block() as block:

                @block.sync
                def _(sp):
                    def do(st):
                        b, par = st.b[0], st.par[0]
                        if "decay" not in st.work:
                            return
                        need(sp, s_full, b - 1)
                        settle(sp, spare)
                        sp.dma_start(xT[:, par, :], w["xT"][b]).then_inc(x_in[par], 16)
                        need(sp, kept, b - 1)
                        settle(sp, spare)
                        g = g_dram[rows_of(b), :].unsqueeze(0)
                        sp.dma_start(W[par][:, :, 0:S], g.broadcast_to([P, NH, S])).then_inc(g_in[par], 16)
                        sp.dma_start(W[par][:, :, S:S + P],
                                     g[:, :, P:S].broadcast_to([P, NH, P])).then_inc(g_in[par], 16)
                    walk(sp, do)

                @block.gpsimd
                def _(pool):
                    for s in x_free:
                        pool.sem_inc(s, 1)
                    pool.memset(V[:], 0.0).then_inc(cleared, 1)
                    pool.memset(ht.half[:, :], -0.5).then_inc(consts, 1)
                    pool.memset(nt.half[:, :], -0.5).then_inc(consts, 1)
                    pool.wait_ge(cleared, 1)
                    pool.memset(V[:, :, :, :, DV:DV + 1], 1.0).then_inc(consts, 1)
                    pool.wait_ge(consts, 3)
                    pool.wait_ge(later_in, 16 * len(loads))

                    def do(st):
                        for op in st.work:
                            b, par = st.b[roles[op]], st.par[roles[op]]
                            if op == "decay":
                                need(pool, w_done, b * 2 - 2)
                                settle(pool, spare)
                                pool.tensor_copy(bs[:, par], bT[:, :, rows_of(b)]).then_inc(bs_done, 1)
                                pool.wait_ge(g_in[par], use_no(b, par) * 2)
                                for cols in (slice(0, P), slice(S, S + P)):
                                    pool.tensor_tensor(W[par][:, :, cols], W[par][:, :, cols],
                                                       mask[:, :].unsqueeze(1).broadcast_to([P, NH, P]),
                                                       ALU.add).then_inc(arg_done, 1)
                            elif op == "head_norm":
                                pool.wait_ge(h_ve, b + 1)
                                pool.tensor_tensor(ht.rstd[:, :], ht.ve[:, :], ht.half[:, :],
                                                   ALU.pow).then_inc(h_rstd, 1)
                            elif op == "apply":
                                pool.wait_ge(ve_done, b + 1)
                                pool.tensor_tensor(nt.rstd[:, :], nt.ve[:, :], nt.half[:, :],
                                                   ALU.pow).then_inc(rstd_done, 1)
                    walk(pool, do)

                @block.scalar
                def _(act):
                    act.wait_ge(consts, 3)
                    act.wait_ge(kx_clear, 1)

                    def take(st, name):
                        bank, k = st.ring[name]
                        act.wait_ge(x_full[bank], k)
                        return X[:, bank, :], x_free[bank], k

                    def decay(b, par):
                        act.wait_ge(bs_done, b + 1)
                        for kt in range(TT):
                            act.wait_ge(arg_done, b * 2 + kt + 1)
                            cols = slice(0, S) if kt == 0 else slice(S, S + P)
                            for h in range(NH):
                                ins = act.activation(W[par][:, h, cols], W[par][:, h, cols], ACT.Exp,
                                                     bias=bs[:, par, kt, h:h + 1], scale=-1.0)
                            ins.then_inc(w_done, 1)

                    def do(st):
                        filling = isinstance(st.b[1], int) and st.b[1] < 0
                        for op in st.work:
                            b, par = st.b[roles[op]], st.par[roles[op]]
                            if op == "decay" and not filling:
                                decay(b, par)
                            elif op == "values":
                                src, done, k = take(st, op)
                                need(act, h_done, b - 1)
                                vo = src.rearrange("p (t n) -> p t n", t=TT)
                                for tt in range(TT):
                                    act.activation(V[:, par, tt, :, 0:DV],
                                                   vo[:, tt, 0:D].rearrange("p (h v) -> p h v", h=NH), ACT.Copy)
                                act.activation(sg[:, par], vo[:, :, D:2 * D], ACT.Tanh, scale=0.5).then_inc(done, 1)
                            elif op == "q":
                                src, done, k = take(st, op)
                                need(act, s_full, b)
                                act.activation(q[:], src.rearrange("p (g n) -> p g n", g=NGA),
                                               ACT.Copy).then_inc(done, 1)
                                if isinstance(b, int) and b == 0:
                                    decay(0, 0)
                            elif op == "outputs":
                                src, done, k = take(st, op)
                                need(act, h_done, b)
                                act.activation(Os[:], src.rearrange("p (g n) -> p g n", g=NGA),
                                               ACT.Copy).then_inc(done, 1)
                                act.wait_ge(done, k + 1)
                                act.sem_inc(kept, 1)
                            elif op == "turn":
                                src, done, k = take(st, op)
                                need(act, ve_done, b)
                                act.activation(hT[:, :], src[:, 0:S], ACT.Copy, scale=0.5).then_inc(done, 1)
                                act.wait_ge(done, k + 1)
                                act.sem_inc(hT_done, 1)
                        if isinstance(st.b[1], int) and st.b[1] == 0:
                            held.load(act, "shared", "b")
                    walk(act, do)

                @block.vector
                def _(dve):
                    dve.memset(kx[:], 0.0).then_inc(kx_clear, 1)
                    dve.wait_ge(later_in, 16 * len(loads))
                    dve.wait_ge(consts, 3)
                    dve.wait_ge(kx_clear, 1)
                    ch = Chain(dve, chain)
                    ch.per = 2 * 11

                    def take(st, name):
                        bank, k = st.ring[name]
                        dve.wait_ge(x_full[bank], k)
                        return X[:, bank, :], x_free[bank], k

                    def do(st):
                        for op in st.work:
                            b, par = st.b[roles[op]], st.par[roles[op]]
                            if op == "k":
                                src, done, k = take(st, op)
                                src = src.rearrange("p (g n) -> p g n", g=NGA)
                                need(dve, s_full, b)
                                for j in range(GJ):
                                    rows = slice(32 * j, 32 * j + 32)
                                    ins = dve.tensor_copy(kx[rows, :, j, :], src[rows])
                                ins.then_inc(done, 1)
                            elif op == "scores":
                                dve.wait_ge(s_full, b + 1)
                                for kt in range(TT):
                                    dve.wait_ge(w_done, b * 2 + kt + 1)
                                    cols = slice(0, S) if kt == 0 else slice(S, S + P)
                                    dve.scalar_tensor_tensor(W[par][:, :, cols], S0[:] if kt == 0 else S1[:],
                                                             float(DQ) ** -0.5, W[par][:, :, cols], ALU.mult,
                                                             ALU.mult).then_inc(p_done, 1)
                            elif op == "by_token":
                                src, done, k = take(st, op)
                                o = src.rearrange("p (t h v) -> p t h v", t=TT, h=NH)
                                ch.link(dve.tensor_tensor(den[:], o[:, :, :, DV], emT[:, :, rows_of(b)], ALU.max))
                                ch.link(dve.scalar_tensor_tensor(den[:], o[:, :, :, DV], -1.0, den[:], ALU.mult,
                                                                 ALU.max))
                                ch.link(dve.tensor_scalar(den[:], den[:], 1e-6, None, ALU.add))
                                ch.link(dve.reciprocal(rden[:], den[:]))
                                for tt in range(TT):
                                    ins = dve.tensor_tensor(ht.r[:, tt, :].rearrange("p (h v) -> p h v", h=NH),
                                                            o[:, tt, :, 0:DV],
                                                            rden[:, tt, :].unsqueeze(2).broadcast_to([P, NH, DV]),
                                                            ALU.mult)
                                ins.then_inc(done, 1)
                                dve.wait_ge(done, k + 1)
                                settle(dve, spare)
                                norm_stats(dve, ch.link, ht, h_ve, spare, EPS_H)
                            elif op == "head_norm":
                                dve.wait_ge(h_rstd, b + 1)
                                for tt in range(TT):
                                    ins = norm_apply(dve, ht, hn[:, tt, :], tt)
                                ch.link(ins)
                                ch.link(dve.tensor_tensor(hn[:], hn[:], lnw[:, :].unsqueeze(1)
                                                          .broadcast_to([P, TT, D]), ALU.mult))
                                ch.link(dve.tensor_tensor(hn[:], hn[:], lnb[:, :].unsqueeze(1)
                                                          .broadcast_to([P, TT, D]), ALU.add))
                                dve.scalar_tensor_tensor(hn[:], sg[:, par], 1.0, hn[:], ALU.add,
                                                         ALU.mult).then_inc(h_done, 1)
                            elif op == "result":
                                need(dve, x_done, b * 2)
                                src, done, k = take(st, op)
                                y = src[:, 0:TT * D].rearrange("p (t d) -> p t d", t=TT)
                                dve.tensor_tensor(nt.r[:], y, x_all[:, tiles(b), :], ALU.add).then_inc(done, 1)
                                dve.wait_ge(done, k + 1)
                                settle(dve, spare)
                                norm_stats(dve, ch.link, nt, ve_done, spare)
                            elif op == "apply":
                                dve.wait_ge(rstd_done, b + 1)
                                for tt in range(TT):
                                    norm_apply(dve, nt, x_all[:, tiles(b, tt, 1), :].squeeze(1), tt)\
                                        .then_inc(x_done, 1)
                    walk(dve, do, ch)

                @block.tensor
                def _(pe):
                    pe.wait_ge(later_in, 16 * len(loads))
                    pe.wait_ge(consts, 3)
                    pe.wait_ge(kx_clear, 1)

                    def do(st):
                        for op in st.work:
                            b, par = st.b[roles[op]], st.par[roles[op]]
                            if op in st.ring:
                                bank, k = st.ring[op]
                                pe.wait_ge(x_free[bank], k)
                                dst, done = X[:, bank, :], x_full[bank]
                            if op == "values":
                                pe.wait_ge(x_in[par], use_no(b, par))
                                for tt in range(TT):
                                    mm = pe.matmul(dst[:, tt * 2 * D:(tt + 1) * 2 * D],
                                                   xT[:, par, tt * P:(tt + 1) * P], wvo[:, :], start=True, stop=True)
                                mm.then_inc(done, 1)
                            elif op in ("q", "k"):
                                pe.wait_ge(x_in[par], use_no(b, par))
                                wt = wq if op == "q" else wk
                                for gg in range(NGA):
                                    mm = pe.matmul(dst[:, gg * S:(gg + 1) * S], wt[:, gg, :], xT[:, par, :],
                                                   start=True, stop=True)
                                mm.then_inc(done, 1)
                            elif op == "scores":
                                for name in ("q", "k"):
                                    bank, k = st.ring[name]
                                    pe.wait_ge(x_free[bank], k + 1)
                                need(pe, p_done, b * 2)
                                for h in range(NH):
                                    gg, j = h // GJ, h % GJ
                                    pe.matmul(S0[:, h, :], kx[:, gg, j, 0:P], q[:, gg, :], start=True, stop=True)
                                    mm = pe.matmul(S1[:, h, :], kx[:, gg, j, P:S], q[:, gg, P:S], start=True,
                                                   stop=True)
                                mm.then_inc(s_full, 1)
                            elif op == "outputs":
                                pe.wait_ge(p_done, b * 2 + 2)
                                o = dst.rearrange("p (g n) -> p g n", g=NGA)
                                for gg in range(NGA):
                                    for kt in range(TT):
                                        for j in range(GJ):
                                            h = GJ * gg + j
                                            src = W[par][:, h, 0:S] if kt == 0 else W[par][:, h, S:S + P]
                                            mm = pe.matmul(o[32 * j:32 * j + 32, gg, kt * P:S],
                                                           V[:, par, kt, h, :], src, start=kt == 0, stop=kt == 1,
                                                           skip_group_check=True)
                                mm.then_inc(done, 1)
                            elif op == "by_token":
                                kept, k = st.ring["outputs"]
                                pe.wait_ge(x_free[kept], k + 1)
                                for tt in range(TT):
                                    for gg in range(NGA):
                                        mm = pe.transpose(dst[:, (tt * NGA + gg) * P:(tt * NGA + gg + 1) * P],
                                                          Os[:, gg, tt * P:(tt + 1) * P], ident[:, :])
                                mm.then_inc(done, 1)
                            elif op == "turn":
                                pe.wait_ge(h_done, b + 1)
                                for tt in range(TT):
                                    mm = pe.transpose(dst[:, tt * P:(tt + 1) * P], hn[:, tt, :], ident[:, :])
                                mm.then_inc(done, 1)
                            elif op == "result":
                                pe.wait_ge(hT_done, b + 1)
                                for tt in range(TT):
                                    mm = pe.matmul(dst[:, tt * D:(tt + 1) * D], hT[:, tt * P:(tt + 1) * P],
                                                   wout[:, :], start=True, stop=True)
                                mm.then_inc(done, 1)
                    walk(pe, do)


def ffn(nc, x_all, w, held, out):
    HID, RANK = 512, 16
    HC = HID // P
    BU = 2
    UN, UT = B // BU, BU * TT
    with ExitStack() as ctx:
        sc = Scope(nc, ctx, "f")
        wf, wp, bf_, v, uT, gate = (held[f"f_{n}"] for n in ("wfc", "wproj", "fast_bT", "v", "uT", "gate"))
        ident = held["ident"]
        tmp = sc.sb("tmp", [P, HC, D])
        tern = sc.sb("tern", [P, HC, D])
        scf, scp = sc.sb("scf", [P, HC]), sc.sb("scp", [P, 1])
        half, nhalf = sc.sb("edge", [P, HC]), sc.sb("nedge", [P, HC])
        bv = sc.sb("bv", [RANK, D])
        A1 = sc.sb("A1", [P, HC, D])
        A2 = sc.sb("A2", [P, HC, D])
        A1T = sc.sb("A1T", [P, HC, P])
        A2T = sc.sb("A2T", [P, HC, D])
        xT = sc.sb("xT", [P, UN, BU * S])
        rl = sc.sb("rl", [P, HC, BU * S])
        r2 = sc.sb("r2", [P, HC, BU * S])
        y = sc.sb("y", [P, UT, D])
        nt = NormTiles(sc, UT)
        XT = sc.ps("XT", [P, 512])
        HT = sc.ps("HT", [P, HC, BU * S])
        Y = sc.ps("Y", [P, UT, D])
        WT = sc.ps("WT", [P, 2, HC, P])
        (chain, consts, bv_full, bv_done, um_full, a1_done, a2_done, wt_full, wt_done, xt_full, xt_done,
         h_full, rl_done, r2_done, y_full, y_free, ve_done, rstd_done, n_done, out_done, spare) = (
            sc.sem(n) for n in ("chain", "consts", "bv_full", "bv_done", "um_full", "a1_done", "a2_done",
                                "wt_full", "wt_done", "xt_full", "xt_done", "h_full", "rl_done",
                                "r2_done", "y_full", "y_free", "ve_done", "rstd_done", "n_done", "out_done", "spare"))
        def tiles(u, first=0, n=UT):
            return slice(UT * u + first, UT * u + first + n) if isinstance(u, int) else bass.ds(u * UT + first, n)

        def loop(eng, early, late, chain=None):
            early(0)
            n = chain.n if chain else 0
            with eng.Fori(0, UN - 1) as u:
                if chain:
                    chain.off = u * chain.per
                early(u + 1)
                late(u)
            if chain:
                assert chain.n - n == chain.per, chain.n - n
                chain.off, chain.n = 0, n + (UN - 1) * chain.per
            late(UN - 1)

        with nc.Block() as block:

            @block.sync
            def _(sp):
                def late(u):
                    for b in range(BU):
                        sp.wait_ge(n_done, u * UT + (UT + TT * b + TT))
                        settle(sp, spare)
                        rows = out[BU * u + b] if isinstance(u, int) else out[bass.ds(u * BU + b, 1)].squeeze(0)
                        sp.dma_start(rows.rearrange("(t p) d -> p t d", p=P),
                                     y[:, TT * b:TT * b + TT]).then_inc(out_done, 16)
                loop(sp, lambda u: None, late)
                sp.wait_ge(out_done, 16 * B + 16 * BU)

            @block.gpsimd
            def _(pool):
                for s, n in ((n_done, UT), (out_done, 16 * BU), (y_free, 1)):
                    pool.sem_inc(s, n)
                pool.memset(nt.half[:, :], -0.5).then_inc(consts, 1)
                pool.wait_ge(consts, 1)

                def late(u):
                    pool.wait_ge(ve_done, u + 1)
                    pool.tensor_tensor(nt.rstd[:, :], nt.ve[:, :], nt.half[:, :], ALU.pow).then_inc(rstd_done, 1)
                loop(pool, lambda u: None, late)

            @block.scalar
            def _(act):
                act.wait_ge(bv_full, 1)
                act.activation(bv[:, :], XT[0:RANK, 0:D], ACT.Copy).then_inc(bv_done, 1)
                for u in range(UN):
                    act.wait_ge(xt_full, u + 1)
                    act.activation(xT[:, u, :], XT[:, :], ACT.Copy).then_inc(xt_done, 1)
                act.wait_ge(wt_full, 1)
                act.activation(A1T[:], WT[:, 0], ACT.Copy).then_inc(wt_done, 1)

                def early(u):
                    for n in range(2):
                        cs = slice(HC // 2 * n, HC // 2 * (n + 1))
                        act.wait_ge(h_full, u * 2 + (n + 1))
                        if not isinstance(u, int):
                            act.wait_ge(r2_done, u * 2 + (n - 1))
                        act.activation(rl[:, cs], HT[:, cs], ACT.Relu).then_inc(rl_done, 1)

                early(0)
                act.wait_ge(wt_full, 2)
                act.activation(A2T[:], WT[:, 1], ACT.Copy).then_inc(wt_done, 1)
                with act.Fori(0, UN - 1) as u:
                    early(u + 1)

            @block.vector
            def _(dve):
                ch = Chain(dve, chain)
                ch.per = 2
                held.wait(dve, "f")
                wpt = wp[:, :].rearrange("p (c d) -> p c d", c=HC)

                def ternary(wt, scale, dst, tiles_):
                    ch.link(dve.scalar_tensor_tensor(tmp[:], wt, -1.0, wt, ALU.mult, ALU.max))
                    src = tmp[:] if tiles_ == HC else tmp[:].rearrange("p c d -> p (c d)").unsqueeze(1)
                    ch.link(dve.tensor_reduce(scale[:, :], src, AX.X, ALU.add))
                    ch.link(dve.tensor_scalar(scale[:, :], scale[:, :], tiles_ / float(HID), 1e-5, ALU.mult, ALU.max))
                    wide = scale[:, :].unsqueeze(2).broadcast_to([P, HC, D])
                    ch.link(dve.tensor_scalar(half[:, 0:tiles_], scale[:, :], 0.5, None, ALU.mult))
                    ch.link(dve.tensor_scalar(nhalf[:, 0:tiles_], scale[:, :], -0.5, None, ALU.mult))
                    edge = half[:, 0:tiles_].unsqueeze(2).broadcast_to([P, HC, D])
                    ch.link(dve.tensor_tensor(tern[:], wt, edge, ALU.is_gt))
                    edge = nhalf[:, 0:tiles_].unsqueeze(2).broadcast_to([P, HC, D])
                    ch.link(dve.tensor_tensor(tmp[:], wt, edge, ALU.is_lt))
                    ch.link(dve.tensor_tensor(tern[:], tern[:], tmp[:], ALU.subtract))
                    ch.link(dve.tensor_tensor(tern[:], tern[:], wt, ALU.subtract))
                    ch.link(dve.tensor_tensor(tern[:], tern[:], wt, ALU.add))
                    return dve.tensor_tensor(dst[:], tern[:], wide, ALU.mult)

                ch.link(ternary(wf[:], scf, A1, HC))
                dve.wait_ge(um_full, 1)
                um = HT[:, 0, :].rearrange("p (c d) -> p c d", c=HC)
                dve.scalar_tensor_tensor(A1[:], um, gate[:, 0:1], A1[:], ALU.mult, ALU.add).then_inc(a1_done, 1)
                ternary(wpt, scp, A2, 1).then_inc(a2_done, 1)

                def early(u):
                    for n in range(2):
                        cs = slice(HC // 2 * n, HC // 2 * (n + 1))
                        dve.wait_ge(rl_done, u * 2 + (n + 1))
                        if not isinstance(u, int):
                            dve.wait_ge(y_full, u)
                        dve.scalar_tensor_tensor(r2[:, cs], HT[:, cs], 0.0, rl[:, cs], ALU.max,
                                                 ALU.mult).then_inc(r2_done, 1)

                def late(u):
                    dve.wait_ge(y_full, u + 1)
                    dve.wait_ge(n_done, u * UT + UT)
                    dve.tensor_tensor(nt.r[:], Y[:], x_all[:, tiles(u), :], ALU.add).then_inc(y_free, 1)
                    dve.wait_ge(y_free, u + 2)
                    settle(dve, spare)
                    norm_stats(dve, ch.link, nt, ve_done, spare)
                    dve.wait_ge(rstd_done, u + 1)
                    dve.wait_ge(out_done, u * (16 * BU) + 16 * BU)
                    for tt in range(UT):
                        norm_apply(dve, nt, y[:, tt, :], tt).then_inc(n_done, 1)
                loop(dve, early, late, ch)

            @block.tensor
            def _(pe):
                held.wait(pe, "shared")
                held.wait(pe, "f")
                pe.matmul(XT[0:RANK, 0:D], bf_[:, :], v[:, :], start=True, stop=True).then_inc(bv_full, 1)
                pe.wait_ge(bv_done, 1)
                for c in range(HC):
                    mm = pe.matmul(HT[:, 0, c * D:(c + 1) * D], uT[:, c * P:(c + 1) * P], bv[:, :], start=True,
                                   stop=True)
                mm.then_inc(um_full, 1)
                for u in range(UN):
                    if u:
                        pe.wait_ge(xt_done, u)
                    for n in range(UT):
                        mm = pe.transpose(XT[:, n * P:(n + 1) * P], x_all[:, UT * u + n, :], ident[:, :])
                    mm.then_inc(xt_full, 1)
                pe.wait_ge(xt_done, UN)

                def turn(n, src, ready):
                    pe.wait_ge(ready, 1)
                    for c in range(HC):
                        mm = pe.transpose(WT[:, n, c, :], src[:, c, :], ident[:, :])
                    mm.then_inc(wt_full, 1)
                    pe.wait_ge(wt_done, n + 1)

                def early(u):
                    xu = xT[:, u, :] if isinstance(u, int) else xT[:, bass.ds(u, 1), :].squeeze(1)
                    for c in range(HC):
                        if c % 2 == 0 and not isinstance(u, int):
                            pe.wait_ge(r2_done, u * 2 + (c // 2 - 1))
                        mm = pe.matmul(HT[:, c, :], A1T[:, c, :], xu, start=True, stop=True)
                        if c % 2 == 1:
                            mm.then_inc(h_full, 1)

                def late(u):
                    pe.wait_ge(r2_done, u * 2 + 2)
                    pe.wait_ge(y_free, u + 1)
                    for tt in range(UT):
                        for c in range(HC):
                            mm = pe.matmul(Y[:, tt, :], r2[:, c, tt * P:(tt + 1) * P], A2T[:, c, :],
                                           start=c == 0, stop=c == HC - 1)
                    mm.then_inc(y_full, 1)

                turn(0, A1, a1_done)
                early(0)
                turn(1, A2, a2_done)
                with pe.Fori(0, UN - 1) as u:
                    early(u + 1)
                    late(u)
                late(UN - 1)


def decoder(nc, w, out):
    with ExitStack() as ctx:
        x_all = ctx.enter_context(nc.sbuf_tensor("x_all", [P, B * TT, D], F32))
        held = Held(nc, ctx, w)
        mlstm(nc, x_all, w, held)
        attention(nc, x_all, w, held, "b", masked=True)
        moe(nc, x_all, w, held)
        attention(nc, x_all, w, held, "d", own=True, wide=True)
        attention(nc, x_all, w, held, "e", causal=True)
        ffn(nc, x_all, w, held, out)



def lay(i):
    import numpy as np

    bf16 = np.dtype("bfloat16")
    f32 = np.float32
    dense = np.ascontiguousarray

    def by_column(w):
        return dense(w.T.reshape(D, H, HD).transpose(0, 2, 1).reshape(D, D))

    def bias_by_column(b):
        return dense(b.reshape(H, HD).T.reshape(D, 1))

    def output_rows(w):
        rows = np.zeros((GJ, 32, NG, D), w.dtype)
        rows[:, :HD] = w.T.reshape(NG, GJ, HD, D).transpose(1, 2, 0, 3)
        return rows.reshape(P, NG, D)

    def head_rows(w):
        t = np.zeros((D, 2, GJ, 32), w.dtype)
        t[..., :HD] = w.T.reshape(D, 2, GJ, HD)
        return t.reshape(D, 2, P)

    def gate_columns(w):
        t = np.zeros((D, B, B, 8), w.dtype)
        for b in range(B):
            t[:, b, b] = w.T
        return t.reshape(D, B, B * 8)

    r = np.arange(P)
    same_head = r[:, None] // 32 == r[None, :] // 32
    eye = np.eye(P)
    future = np.where(r[None, :] > r[:, None], -BIG, 0.0).astype(bf16)
    mask = i["mask_1x1xSxS2_ik0"][0, 0]
    c_attn, c_bias = i["L1_attn_Wc"], i["L1_attn_bc"]
    x = i["x"]
    return {
        "ident": eye.astype(f32), "identb": eye.astype(bf16),
        "ones_row": np.ones((1, H, S), bf16), "zeros_row": np.zeros((1, H, S), bf16),
        "ctxT": dense(i["ctx_1024"].transpose(0, 2, 1)),
        "x": dense(x.reshape(B * TT, P, D).transpose(1, 0, 2)), "xT": dense(x.transpose(0, 2, 1)),
        "collect": dense(np.stack([same_head & (r[:, None] % 32 == HD) & (r[None, :] % 4 == g)
                                   for g in range(NG)], 1).astype(f32)),
        "collect_wide": dense(np.broadcast_to(np.stack([r[:32] % 4 == g for g in range(NG)]),
                                              (P, NG, 32)).astype(f32)),
        "spread": dense(np.stack([same_head & (r[:, None] % 32 == g) for g in range(NG)], 1).astype(f32)),
        "mask": dense(np.stack([mask.reshape(TT, P, S).transpose(1, 0, 2),
                                mask.T.reshape(TT, P, S).transpose(1, 0, 2)], 1)),
        "b_wq": by_column(i["L0_xattn_wq"]), "b_wk": by_column(i["L0_xattn_wk"]), "b_wv": dense(i["L0_xattn_wv"].T),
        "b_wo": output_rows(i["L0_xattn_wo"]), "b_bo": i["L0_xattn_bo"],
        "causal_q": dense(np.broadcast_to(future[:, None, None, :], (P, TT, 2, P))),
        "causal_k": dense(np.broadcast_to(future.T[:, None, None, :], (P, TT, 2, P))),
        "e_wq": by_column(i["L1_xattn_Wq"]), "e_wk": by_column(i["L1_xattn_Wk"]), "e_wv": dense(i["L1_xattn_Wv"].T),
        "e_wo": output_rows(i["L1_xattn_Wo"]), "e_bo": i["L1_xattn_bo"],
        "e_bq": bias_by_column(i["L1_xattn_bq"]), "e_bk": bias_by_column(i["L1_xattn_bk"]),
        "e_bv": i["L1_xattn_bv"],
        "d_wq": by_column(c_attn[:D]), "d_wk": by_column(c_attn[D:2 * D]), "d_wv": dense(c_attn[2 * D:].T),
        "d_bq": bias_by_column(c_bias[:D]), "d_bk": bias_by_column(c_bias[D:2 * D]), "d_bv": c_bias[2 * D:],
        "d_wo": dense(i["L1_attn_Wo"].T.reshape(NG, GJ, 2, 32, D).transpose(1, 3, 0, 2, 4).reshape(P, 2 * NG, D)),
        "d_bo": i["L1_attn_bo"],
        "a_wg": dense(np.stack([gate_columns(i["L0_attn_Wi"]), gate_columns(i["L0_attn_Wf"])], 1)),
        "a_gb": dense(np.stack([np.tile(i["L0_attn_bi"], B), np.tile(i["L0_attn_bf"], B)], 1)),
        "a_wq": head_rows(i["L0_attn_Wq"]), "a_wk": head_rows(i["L0_attn_Wk"]),
        "a_wvo": dense(np.concatenate([i["L0_attn_Wv"].T, i["L0_attn_Wog"].T], 1)),
        "a_wout": dense(i["L0_attn_Wout"].T), "a_lnw": i["L0_attn_ln_w"], "a_lnb": i["L0_attn_ln_b"],
        "a_mask": dense(np.where(r[None, :] < r[:, None], BIG, 0.0).astype(f32)),
        "c_phi": dense(i["L0_ffn_phi"].reshape(D, 2048)),
        "c_W": dense(i["L0_ffn_W"].transpose(1, 0, 2)),
        "c_b": dense(np.broadcast_to(i["L0_ffn_b"].reshape(16, 4, 1, D), (16, 4, 32, D))
                     .reshape(16, P, D).transpose(1, 0, 2)),
        "f_wfc": dense(i["L1_ffn_w_fc"].reshape(4, P, D).transpose(1, 0, 2)), "f_wproj": i["L1_ffn_w_proj"],
        "f_fast_bT": dense(i["L1_ffn_fast_b"].T), "f_v": i["L1_ffn_v"], "f_uT": dense(i["L1_ffn_u"].T),
        "f_gate": i["L1_ffn_gate"].reshape(1),
    }


def kernel(**inputs):
    import numpy as np
    import concourse.bacc as bacc
    from concourse.bass_utils import run_bass_kernel_spmd

    nc = bacc.Bacc("TRN2", target_bir_lowering=False, num_devices=1)
    arrays = {f"in_{k}": np.ascontiguousarray(v) for k, v in lay({k: np.asarray(v) for k, v in inputs.items()}).items()}
    w = {k[3:]: nc.dram_tensor(k, v.shape, mybir.dt.from_np(v.dtype), kind="ExternalInput").ap()
         for k, v in arrays.items()}
    out = nc.dram_tensor("out", (B, S, D), F32, kind="ExternalOutput").ap()
    decoder(nc, w, out)
    return run_bass_kernel_spmd(nc, [arrays], core_ids=[0]).results[0]["out"]
```
